# Optimizing a Trainium2 kernel written in Bass

```python
import numpy as np
import jax
import jax.numpy as jnp

def _softmax(x, axis=-1):
    return jax.nn.softmax(x, axis=axis)

def _gelu(x):
    return jax.nn.gelu(x, approximate=True)

def _silu(x):
    return jax.nn.silu(x)

def _sigmoid(x):
    return jax.nn.sigmoid(x)

def _layernorm(x, axis=-1, eps=1e-05):
    m = jnp.mean(x, axis=axis, keepdims=True)
    v = jnp.var(x, axis=axis, keepdims=True)
    return (x - m) / jnp.sqrt(v + eps)

def _scatter_add(tgt, idx, src, axis=0):
    return tgt.at[idx].add(src)

def _segment_sum(src, seg, n):
    return jax.ops.segment_sum(src, seg, n)
kernel_name = 'mk_seq_postln_d1_jaxref_r8_3d1f8f'

def setup_inputs(seed: int=0):
    np.random.seed(seed)
    _w = jnp.asarray

    def _L0_attn_setup():
        import jax, jax.numpy as jnp
        import numpy as np
        B, N, E = (4, 256, 128)
        H = 8
        D1 = 3 * E
        DH = D1 // H
        R = 64
        GAMMA = 0.99
        EPS = 1e-08

        def _srms(x):
            rms = jnp.linalg.norm(x, axis=-1, keepdims=True) * x.shape[-1] ** (-0.5)
            return x / (rms + EPS)
        key = jax.random.key(seed)
        ks = jax.random.split(key, 20)

        def lin(k, din, dout):
            kw, kb = jax.random.split(k)
            w = jax.random.normal(kw, (din, dout), jnp.float32) * din ** (-0.5)
            b = jax.random.normal(kb, (dout,), jnp.float32) * 0.02
            return (w, b)
        x = jax.random.normal(ks[0], (B, N, E), jnp.float32)
        u_w, u_b = lin(ks[1], E, D1)
        v_w, v_b = lin(ks[2], E, D1)
        o_w, o_b = lin(ks[3], D1, E)
        pos_w, pos_b = lin(ks[4], 1, R)
        lw0, lb0 = lin(ks[5], R, R)
        lw1, lb1 = lin(ks[6], R, R)
        lw2, lb2 = lin(ks[7], R, R)
        out_w, out_b = lin(ks[8], R, H * DH)
        return dict(x=x, u_w=u_w, u_b=u_b, v_w=v_w, v_b=v_b, o_w=o_w, o_b=o_b, pos_w=pos_w, pos_b=pos_b, lw0=lw0, lb0=lb0, lw1=lw1, lb1=lb1, lw2=lw2, lb2=lb2, out_w=out_w, out_b=out_b)
    _L0_attn_in = _L0_attn_setup()

    def _L0_ffn_setup():
        import jax, jax.numpy as jnp
        import numpy as np
        B, L, D = (4, 256, 128)
        H = 16
        E = 16
        NS = 16
        S = NS // E
        F = 512
        EPS = 1e-05

        def _layernorm(x, g, b):
            mu = jnp.mean(x, axis=-1, keepdims=True)
            var = jnp.mean(jnp.square(x - mu), axis=-1, keepdims=True)
            return (x - mu) * jax.lax.rsqrt(var + EPS) * g + b

        def _mha(q, k, v, Wq, bq, Wk, bk, Wv, bv, Wo, bo):
            Bq, Lq, Dm = q.shape
            dh = Dm // H
            qh = (q @ Wq + bq).reshape(Bq, Lq, H, dh)
            kh = (k @ Wk + bk).reshape(Bq, -1, H, dh)
            vh = (v @ Wv + bv).reshape(Bq, -1, H, dh)
            scores = jnp.einsum('bqhd,bkhd->bhqk', qh, kh) / jnp.asarray(np.sqrt(dh), q.dtype)
            attn = jax.nn.softmax(scores, axis=-1)
            out = jnp.einsum('bhqk,bkhd->bqhd', attn, vh).reshape(Bq, Lq, Dm)
            return out @ Wo + bo
        key = jax.random.key(seed)
        ks = jax.random.split(key, 32)
        s = 0.02
        d = {}
        d['x'] = jax.random.normal(ks[0], (B, L, D), jnp.float32)
        d['slot_query'] = jax.random.normal(ks[1], (1, NS, D), jnp.float32) * 0.01
        for i, nm in enumerate(['d_Wq', 'd_Wk', 'd_Wv', 'd_Wo']):
            d[nm] = jax.random.normal(ks[2 + i], (D, D), jnp.float32) * s
        for nm in ['d_bq', 'd_bk', 'd_bv', 'd_bo']:
            d[nm] = jnp.zeros((D,), jnp.float32)
        for i, nm in enumerate(['c_Wq', 'c_Wk', 'c_Wv', 'c_Wo']):
            d[nm] = jax.random.normal(ks[6 + i], (D, D), jnp.float32) * s
        for nm in ['c_bq', 'c_bk', 'c_bv', 'c_bo']:
            d[nm] = jnp.zeros((D,), jnp.float32)
        d['e_ln_g'] = jnp.ones((E, D), jnp.float32)
        d['e_ln_b'] = jnp.zeros((E, D), jnp.float32)
        d['e_W1'] = jax.random.normal(ks[10], (E, D, F), jnp.float32) * s
        d['e_b1'] = jnp.zeros((E, F), jnp.float32)
        d['e_Wg'] = jax.random.normal(ks[11], (E, D, F), jnp.float32) * s
        d['e_bg'] = jnp.zeros((E, F), jnp.float32)
        d['e_W2'] = jax.random.normal(ks[12], (E, F, D), jnp.float32) * s
        d['e_b2'] = jnp.zeros((E, D), jnp.float32)
        return d
    _L0_ffn_in = _L0_ffn_setup()
    _d = {'L0_attn_x': _L0_attn_in['x'], 'L0_attn_u_w': _L0_attn_in['u_w'], 'L0_attn_u_b': _L0_attn_in['u_b'], 'L0_attn_v_w': _L0_attn_in['v_w'], 'L0_attn_v_b': _L0_attn_in['v_b'], 'L0_attn_o_w': _L0_attn_in['o_w'], 'L0_attn_o_b': _L0_attn_in['o_b'], 'L0_attn_pos_w': _L0_attn_in['pos_w'], 'L0_attn_pos_b': _L0_attn_in['pos_b'], 'L0_attn_lw0': _L0_attn_in['lw0'], 'L0_attn_lb0': _L0_attn_in['lb0'], 'L0_attn_lw1': _L0_attn_in['lw1'], 'L0_attn_lb1': _L0_attn_in['lb1'], 'L0_attn_lw2': _L0_attn_in['lw2'], 'L0_attn_lb2': _L0_attn_in['lb2'], 'L0_attn_out_w': _L0_attn_in['out_w'], 'L0_attn_out_b': _L0_attn_in['out_b'], 'L0_ffn_slot_query': _L0_ffn_in['slot_query'], 'L0_ffn_d_Wq': _L0_ffn_in['d_Wq'], 'L0_ffn_d_Wk': _L0_ffn_in['d_Wk'], 'L0_ffn_d_Wv': _L0_ffn_in['d_Wv'], 'L0_ffn_d_Wo': _L0_ffn_in['d_Wo'], 'L0_ffn_d_bq': _L0_ffn_in['d_bq'], 'L0_ffn_d_bk': _L0_ffn_in['d_bk'], 'L0_ffn_d_bv': _L0_ffn_in['d_bv'], 'L0_ffn_d_bo': _L0_ffn_in['d_bo'], 'L0_ffn_c_Wq': _L0_ffn_in['c_Wq'], 'L0_ffn_c_Wk': _L0_ffn_in['c_Wk'], 'L0_ffn_c_Wv': _L0_ffn_in['c_Wv'], 'L0_ffn_c_Wo': _L0_ffn_in['c_Wo'], 'L0_ffn_c_bq': _L0_ffn_in['c_bq'], 'L0_ffn_c_bk': _L0_ffn_in['c_bk'], 'L0_ffn_c_bv': _L0_ffn_in['c_bv'], 'L0_ffn_c_bo': _L0_ffn_in['c_bo'], 'L0_ffn_e_ln_g': _L0_ffn_in['e_ln_g'], 'L0_ffn_e_ln_b': _L0_ffn_in['e_ln_b'], 'L0_ffn_e_W1': _L0_ffn_in['e_W1'], 'L0_ffn_e_b1': _L0_ffn_in['e_b1'], 'L0_ffn_e_Wg': _L0_ffn_in['e_Wg'], 'L0_ffn_e_bg': _L0_ffn_in['e_bg'], 'L0_ffn_e_W2': _L0_ffn_in['e_W2'], 'L0_ffn_e_b2': _L0_ffn_in['e_b2']}
    _x0 = _d['L0_attn_x']
    _d['L0_attn_x'] = jax.random.normal(jax.random.fold_in(jax.random.key(seed), 1), (16, 256, 128), dtype=_x0.dtype)
    del _x0
    return _d

def reference(L0_attn_x, L0_attn_u_w, L0_attn_u_b, L0_attn_v_w, L0_attn_v_b, L0_attn_o_w, L0_attn_o_b, L0_attn_pos_w, L0_attn_pos_b, L0_attn_lw0, L0_attn_lb0, L0_attn_lw1, L0_attn_lb1, L0_attn_lw2, L0_attn_lb2, L0_attn_out_w, L0_attn_out_b, L0_ffn_slot_query, L0_ffn_d_Wq, L0_ffn_d_Wk, L0_ffn_d_Wv, L0_ffn_d_Wo, L0_ffn_d_bq, L0_ffn_d_bk, L0_ffn_d_bv, L0_ffn_d_bo, L0_ffn_c_Wq, L0_ffn_c_Wk, L0_ffn_c_Wv, L0_ffn_c_Wo, L0_ffn_c_bq, L0_ffn_c_bk, L0_ffn_c_bv, L0_ffn_c_bo, L0_ffn_e_ln_g, L0_ffn_e_ln_b, L0_ffn_e_W1, L0_ffn_e_b1, L0_ffn_e_Wg, L0_ffn_e_bg, L0_ffn_e_W2, L0_ffn_e_b2):

    def _L0_attn_ref(x, u_w, u_b, v_w, v_b, o_w, o_b, pos_w, pos_b, lw0, lb0, lw1, lb1, lw2, lb2, out_w, out_b):
        import jax, jax.numpy as jnp
        import numpy as np
        B, N, E = (4, 256, 128)
        H = 8
        D1 = 3 * E
        DH = D1 // H
        R = 64
        GAMMA = 0.99
        EPS = 1e-08

        def _srms(x):
            rms = jnp.linalg.norm(x, axis=-1, keepdims=True) * x.shape[-1] ** (-0.5)
            return x / (rms + EPS)
        b, n, _ = x.shape
        u = jax.nn.silu(x @ u_w + u_b)
        v = jax.nn.silu(x @ v_w + v_b)
        v = v.reshape(b, n, H, DH).transpose(0, 2, 1, 3)
        pos_idx = jnp.arange(n, dtype=x.dtype)[:, None]
        h_ = pos_idx @ pos_w + pos_b
        for w, bb in ((lw0, lb0), (lw1, lb1), (lw2, lb2)):
            h_ = jax.nn.relu(_srms(h_)) @ w + bb
        coefs = jax.nn.relu(_srms(h_)) @ out_w + out_b
        coefs = coefs.reshape(n, H, DH).transpose(1, 0, 2)
        zero = coefs[:, :1]
        pos = coefs[:, 1:]
        decay = GAMMA ** jnp.arange(1, n, dtype=x.dtype)[None, :, None]
        pos = pos * decay
        a = jnp.concatenate([zero, pos, zero], axis=1)
        m = 2 * n
        av = jnp.fft.rfft(a, m, axis=1)
        xv = jnp.fft.rfft(v, m, axis=2)
        tv = jnp.fft.irfft(av[None] * xv, m, axis=2)[:, :, :n, :]
        out = tv.transpose(0, 2, 1, 3).reshape(b, n, H * DH)
        out = u * out
        return out @ o_w + o_b

    def _L0_ffn_ref(x, slot_query, d_Wq, d_Wk, d_Wv, d_Wo, d_bq, d_bk, d_bv, d_bo, c_Wq, c_Wk, c_Wv, c_Wo, c_bq, c_bk, c_bv, c_bo, e_ln_g, e_ln_b, e_W1, e_b1, e_Wg, e_bg, e_W2, e_b2):
        import jax, jax.numpy as jnp
        import numpy as np
        B, L, D = (4, 256, 128)
        H = 16
        E = 16
        NS = 16
        S = NS // E
        F = 512
        EPS = 1e-05

        def _layernorm(x, g, b):
            mu = jnp.mean(x, axis=-1, keepdims=True)
            var = jnp.mean(jnp.square(x - mu), axis=-1, keepdims=True)
            return (x - mu) * jax.lax.rsqrt(var + EPS) * g + b

        def _mha(q, k, v, Wq, bq, Wk, bk, Wv, bv, Wo, bo):
            Bq, Lq, Dm = q.shape
            dh = Dm // H
            qh = (q @ Wq + bq).reshape(Bq, Lq, H, dh)
            kh = (k @ Wk + bk).reshape(Bq, -1, H, dh)
            vh = (v @ Wv + bv).reshape(Bq, -1, H, dh)
            scores = jnp.einsum('bqhd,bkhd->bhqk', qh, kh) / jnp.asarray(np.sqrt(dh), q.dtype)
            attn = jax.nn.softmax(scores, axis=-1)
            out = jnp.einsum('bhqk,bkhd->bqhd', attn, vh).reshape(Bq, Lq, Dm)
            return out @ Wo + bo
        Bx = x.shape[0]
        q = jnp.broadcast_to(slot_query, (Bx, NS, D))
        o = q + _mha(q, x, x, d_Wq, d_bq, d_Wk, d_bk, d_Wv, d_bv, d_Wo, d_bo)
        os = o.reshape(Bx, E, S, D)
        h = _layernorm(os, e_ln_g[None, :, None, :], e_ln_b[None, :, None, :])
        u = jax.nn.silu(jnp.einsum('besd,edf->besf', h, e_W1) + e_b1[None, :, None, :])
        g = jax.nn.silu(jnp.einsum('besd,edf->besf', h, e_Wg) + e_bg[None, :, None, :])
        y = jnp.einsum('besf,efd->besd', u * g, e_W2) + e_b2[None, :, None, :]
        o = o + y.reshape(Bx, NS, D)
        out = _mha(x, o, o, c_Wq, c_bq, c_Wk, c_bk, c_Wv, c_bv, c_Wo, c_bo)
        return out
    x = L0_attn_x
    x = _layernorm(x + _L0_attn_ref(x, L0_attn_u_w, L0_attn_u_b, L0_attn_v_w, L0_attn_v_b, L0_attn_o_w, L0_attn_o_b, L0_attn_pos_w, L0_attn_pos_b, L0_attn_lw0, L0_attn_lb0, L0_attn_lw1, L0_attn_lb1, L0_attn_lw2, L0_attn_lb2, L0_attn_out_w, L0_attn_out_b), axis=-1)
    x = _layernorm(x + _L0_ffn_ref(x, L0_ffn_slot_query, L0_ffn_d_Wq, L0_ffn_d_Wk, L0_ffn_d_Wv, L0_ffn_d_Wo, L0_ffn_d_bq, L0_ffn_d_bk, L0_ffn_d_bv, L0_ffn_d_bo, L0_ffn_c_Wq, L0_ffn_c_Wk, L0_ffn_c_Wv, L0_ffn_c_Wo, L0_ffn_c_bq, L0_ffn_c_bk, L0_ffn_c_bv, L0_ffn_c_bo, L0_ffn_e_ln_g, L0_ffn_e_ln_b, L0_ffn_e_W1, L0_ffn_e_b1, L0_ffn_e_Wg, L0_ffn_e_bg, L0_ffn_e_W2, L0_ffn_e_b2), axis=-1)
    return x

_drawn_inputs = setup_inputs


def setup_inputs(seed=0):
    import zlib

    import numpy as np

    out = dict(_drawn_inputs(seed))
    spreads = {'L0_ffn_d_bq': (0.0, 0.8),
     'L0_ffn_d_bk': (0.0, 2.0),
     'L0_ffn_d_bv': (0.0, 0.8),
     'L0_ffn_d_bo': (0.0, 0.8),
     'L0_ffn_c_bq': (0.0, 0.8),
     'L0_ffn_c_bk': (0.0, 2.0),
     'L0_ffn_c_bv': (0.0, 2.0),
     'L0_ffn_c_bo': (0.0, 0.8),
     'L0_ffn_e_ln_g': (1.0, 0.6),
     'L0_ffn_e_ln_b': (0.0, 0.8),
     'L0_ffn_e_b1': (0.0, 0.8),
     'L0_ffn_e_bg': (0.0, 0.8),
     'L0_ffn_e_b2': (0.0, 0.8)}
    factors = {'L0_attn_u_b': 3.253,
     'L0_attn_o_b': 8.0,
     'L0_ffn_slot_query': 8.0,
     'L0_ffn_d_Wq': 8.0,
     'L0_ffn_d_Wk': 8.0,
     'L0_ffn_d_Wv': 8.0,
     'L0_ffn_d_Wo': 8.0,
     'L0_ffn_c_Wq': 8.0,
     'L0_ffn_c_Wk': 8.0,
     'L0_ffn_c_Wv': 8.0,
     'L0_ffn_c_Wo': 2.984,
     'L0_ffn_e_W1': 8.0,
     'L0_ffn_e_Wg': 8.0,
     'L0_ffn_e_W2': 8.0}
    for name, (base, spread) in spreads.items():
        noise = np.random.default_rng([zlib.crc32(name.encode()), seed]).standard_normal(out[name].shape)
        drawn = base * np.exp(spread * noise) if base else spread * noise
        out[name] = jnp.asarray(drawn.astype(out[name].dtype))
    for name, factor in factors.items():
        out[name] = (out[name] * factor).astype(out[name].dtype)
    return out
```

```python
from contextlib import ExitStack

import numpy as np

import concourse.bass as bass
from concourse import mybir

F32 = mybir.dt.float32
BF16 = mybir.dt.bfloat16
ALU = mybir.AluOpType
ACT = mybir.ActivationFunctionType
AX = mybir.AxisListType

P = 128
B = 16
N = 256
D = 128
CH = 384
NC = CH // P
R = 64
NF = 256
NQ = NF // P
H = 16
DH = D // H
S = 16
HS = H * S
FF = 512
NFC = FF // P
LN_EPS = 1e-5
RMS_EPS = 1e-8
SCALE = float(1.0 / np.sqrt(DH))
SHARED = 10752
PAIRS = B // 2

W_MAIN = {"u_w": CH, "o_w": NC * D, "u_b": NC}
W_SLOT = {"d_Wq": D, "d_WkT": D, "d_Wv": D, "d_Wo": D, "c_Wq": D, "c_Wk": D, "c_Wv": D, "c_Wo": D,
          "slotT": S, "d_bq": 1, "d_bk": 1, "d_bv": 1, "d_bo": 1, "c_bq": 1, "c_bk": 1, "c_bv": 1,
          "ln_gT": S, "ln_bT": S, "b1T": S * NFC, "bgT": S * NFC, "b2T": S}
W_CONST = {"ident": P, "mean": P, "headmask": HS, "diagmask": 2 * D, "pick": S}
W_POS = {"pos_w": R, "pos_b": R, "index": 2, "decay": 2, "part": 3}
ROW_V, ROW_O, ROW_C = 0, CH, CH + D
ROWS = CH + 2 * D


def columns(widths):
    at, out = 0, {}
    for name, width in widths.items():
        out[name] = slice(at, at + width)
        at += width
    return out, at


def later(j, p, k):
    return j + (p + k) // 2, (p + k) % 2


def build(nc, xT, x, v_w, w_main, w_slot, w_const, w_pos, w_lin, rows, dft_t, dft_f, dft_i, experts, out):
    ctx = ExitStack()
    main_at, main_n = columns(W_MAIN)
    slot_at, slot_n = columns(W_SLOT)
    const_at, const_n = columns(W_CONST)
    pos_at, pos_n = columns(W_POS)
    with ctx:
        def sb(name, shape, dt=F32):
            return ctx.enter_context(nc.sbuf_tensor(name, shape, dt))

        def sem(name):
            return ctx.enter_context(nc.semaphore(name))

        shared = sb("shared", [P, SHARED])
        top = [0]

        def phase():
            top[0] = 0

        def part_of(shape):
            n = int(np.prod(shape))
            v = shared[:, top[0]:top[0] + n]
            top[0] += n
            assert top[0] <= SHARED
            if len(shape) == 1:
                return v
            names = "abcd"[:len(shape)]
            return v.rearrange(f"p ({' '.join(names)}) -> p {' '.join(names)}",
                               **dict(zip(names[1:], shape[1:])))

        vw_sb = sb("vw_sb", [P, CH])
        main_sb = sb("main_sb", [P, main_n])
        slot_sb = sb("slot_sb", [P, slot_n])
        const_sb = sb("const_sb", [P, const_n])
        pos_sb = sb("pos_sb", [P, pos_n])
        rows_sb = sb("rows_sb", [3, ROWS])
        dft_f_sb = sb("dft_f_sb", [P, 2, NF])
        dft_i_sb = sb("dft_i_sb", [P, NQ, 2, P])
        exp_sb = sb("exp_sb", [P, H, 3 * FF])

        def main(name):
            return main_sb[:, main_at[name]]

        def slot(name):
            return slot_sb[:, slot_at[name]]

        def const(name):
            return const_sb[:, const_at[name]]

        def pos(name):
            return pos_sb[:, pos_at[name]]

        ident = const("ident")
        minus_half = sb("minus_half", [P, S * B])
        plus_half = sb("plus_half", [P, 2])
        ve_sb = sb("ve_sb", [P, 2])
        ones_bf = sb("ones_bf", [P, P], BF16)
        row_parts = sb("row_parts", [P, ROWS], BF16)

        ph = sb("ph", [P, 2, R])
        psq = sb("psq", [P, 2, R])
        pss = sb("pss", [P, 2])
        prms = sb("prms", [P, 3, 2])
        pact = sb("pact", [P, 2, R])
        pactT = sb("pactT", [R + 1, 2, P])
        A_r = sb("A_r", [P, NQ, CH])
        A_i = sb("A_i", [P, NQ, CH])

        phase()
        xT_sb = sb("xT_sb", [P, 2, N])
        x_sb = sb("x_sb", [P, 2, N])
        v_sb = part_of([2, CH])
        vs_sb = part_of([2, CH])
        vd_sb = part_of([2, CH])
        u_sb = part_of([2, NC, N])
        rr = part_of([NQ, CH])
        ii = part_of([NQ, CH])
        ri = part_of([NQ, CH])
        ir = part_of([NQ, CH])
        Y_r = part_of([NQ, CH])
        Y_i = part_of([NQ, CH])
        odd_sb = part_of([NC, P])
        y_sb = part_of([NC, 2, P])
        g_sb = part_of([NC, 2, P])
        res_sb = sb("res_sb", [P, 2, D])
        st_sb = sb("st_sb", [P, 2, 6])
        mv_sb = sb("mv_sb", [P, 2, 2])
        rstd_sb = sb("rstd_sb", [P, 2])
        x1_sb = sb("x1_sb", [P, 2, 2, D])
        x1T_sb = sb("x1T_sb", [P, 2, N])
        v2_sb = sb("v2_sb", [P, 2, 2, D])
        flat_u = u_sb.rearrange("p a c n -> p (a c n)")
        dft_t_sb = flat_u[:, 0:4 * NF].rearrange("p (a b n) -> p a b n", a=2, b=2)
        coef = Y_r
        lin_sb = y_sb.rearrange("p c h n -> p (c h n)")[0:R + 1, 0:3 * R + CH]
        flat_g = g_sb.rearrange("p c h n -> p (c h n)")
        row_hi = flat_g[0:3, 0:ROWS // 2].bitcast(BF16)
        row_mid = flat_g[0:3, ROWS // 2:ROWS].bitcast(BF16)
        row_lo = odd_sb.rearrange("p c n -> p (c n)")[0:3, 0:ROWS // 2].bitcast(BF16)
        row_res = rr[0:3, :, :].rearrange("p a b -> p (a b)")[:, 0:ROWS]
        row_res2 = ii[0:3, :, :].rearrange("p a b -> p (a b)")[:, 0:ROWS]
        row_sum = ri[0:3, :, :].rearrange("p a b -> p (a b)")[:, 0:ROWS]
        row_sum2 = ir[0:3, :, :].rearrange("p a b -> p (a b)")[:, 0:ROWS]
        x1T_all = sb("x1T_all", [P, B, N])
        x1_out = nc.dram_tensor("x1_scratch", (B, P, N), F32, kind="Internal").ap()
        v2_out = nc.dram_tensor("v2_scratch", (B, P, N), F32, kind="Internal").ap()
        v2_in = sb("v2_in", [P, 2, N])
        x1_in = sb("x1_in", [P, 2, N])

        phase()
        dqT = sb("dqT", [P, S])
        dq_blocks = sb("dq_blocks", [P, H, S])
        dA = sb("dA", [P, HS])
        dc = sb("dc", [P, 2])
        dcs = sb("dcs", [P, 2])
        dmax = sb("dmax", [P, 2, 2])
        dmc = sb("dmc", [P, 2, 2])
        dnb = sb("dnb", [P, 2, 2])
        dP = part_of([2, 2, N])
        dsum = sb("dsum", [P, 2, 2])
        drec = sb("drec", [P, 2, 2])
        dPT = part_of([2, 2, HS])
        dZ = part_of([2, 2, D])
        dOT = sb("dOT", [P, B, S])

        phase()
        eo = sb("eo", [P, S, B])
        slot_b = sb("slot_b", [P, S])
        ecen = part_of([S, B])
        esq = part_of([S, B])
        erstd = part_of([S, B])
        eh1 = part_of([S, B])
        eh2 = part_of([S, B])
        eh = part_of([S, B])
        eu_in = part_of([S, NFC, B])
        eg_in = part_of([S, NFC, B])
        eug = part_of([S, NFC, B])
        ey = part_of([S, B])
        eo2 = part_of([S, B])
        ckT = sb("ckT", [P, B, S])
        cvT = sb("cvT", [P, B, S])

        phase()
        kb = part_of([2, H, S])
        vb = part_of([2, H, S])
        cqT = part_of([2, N])
        vo = part_of([2, 2, D])
        cmax = sb("cmax", [P, 2, 2 * H])
        cs = part_of([2, 2 * H, S])
        ce = part_of([2, 2 * H, S])
        csum = sb("csum", [P, 2, 2 * H])
        crec = sb("crec", [P, 2, 2 * H])
        cp = part_of([2, 2, HS])
        cPT = part_of([2, 2, N])
        cres = part_of([2, D])
        y_out = part_of([2, 2, D])

        bank = [ctx.enter_context(nc.psum_tensor(f"bank{i}", [P, 512], F32)) for i in range(8)]

        l_xT = [sem("l_xT0"), sem("l_xT1")]
        l_vw, l_pos, l_const, l_rows, l_lin = sem("l_vw"), sem("l_pos"), sem("l_const"), sem("l_rows"), sem("l_lin")
        l_main, l_slot, l_t, l_f, l_i, l_x = (sem("l_main"), sem("l_slot"), sem("l_t"), sem("l_f"), sem("l_i"),
                                             [sem("l_x0"), sem("l_x1")])
        l_v2 = [sem("l_v20"), sem("l_v21")]
        l_x1 = [sem("l_x10"), sem("l_x11")]
        l_exp = [sem("l_exp0"), sem("l_exp1")]
        st_x1 = [sem("st_x10"), sem("st_x11")]
        st_x1T = [sem("st_x1T0"), sem("st_x1T1")]
        st_v2 = [sem("st_v20"), sem("st_v21")]
        st_out = [sem("st_out0"), sem("st_out1")]
        s_ones, s_rowstep, s_rows = sem("s_ones"), sem("s_rowstep"), sem("s_rows")
        s_pchain, s_pact, s_ptr, s_pactT, s_plin = (sem("s_pchain"), sem("s_pact"), sem("s_ptr"), sem("s_pactT"),
                                                    sem("s_plin"))
        s_coef, s_Aps, s_A = sem("s_coef"), sem("s_Aps"), sem("s_A")
        s_pms, s_prms, s_half = sem("s_pms"), sem("s_prms"), sem("s_half")
        s_seen = sem("s_seen")
        s_ve, c_ve, e_ve, e_rstd = sem("s_ve"), sem("c_ve"), sem("e_ve"), sem("e_rstd")
        s_dq, s_dqb, s_dA, s_prep, s_pchain2 = sem("s_dq"), sem("s_dqb"), sem("s_dA"), sem("s_prep"), sem("s_pchain2")
        s_vps, s_v, s_sd = sem("s_vps"), sem("s_v"), sem("s_sd")
        s_fwd, s_prod, s_Y = sem("s_fwd"), sem("s_prod"), sem("s_Y")
        s_ups, s_u, s_inv, s_odd, s_y, s_g = (sem("s_ups"), sem("s_u"), sem("s_inv"), sem("s_odd"), sem("s_y"),
                                              sem("s_g"))
        s_ops, s_res, s_bn, s_mv, s_rstd, s_x1 = (sem("s_ops"), sem("s_res"), sem("s_bn"), sem("s_mv"),
                                                  sem("s_rstd"), sem("s_x1"))
        s_xtps, s_x1T, s_v2ps, s_v2 = sem("s_xtps"), sem("s_x1T"), sem("s_v2ps"), sem("s_v2")
        d_sps, d_max, d_mc, d_nb, d_p, d_tps, d_pT = (sem("d_sps"), sem("d_max"), sem("d_mc"), sem("d_nb"),
                                                      sem("d_p"), sem("d_tps"), sem("d_pT"))
        d_rec, d_zps, d_z, d_ops, d_o = sem("d_rec"), sem("d_zps"), sem("d_z"), sem("d_ops"), sem("d_o")
        e_pe, e_chain, e_in, e_act, e_ug = sem("e_pe"), sem("e_chain"), sem("e_in"), sem("e_act"), sem("e_ug")
        c_blk, c_qps, c_q, c_vops, c_vo = sem("c_blk"), sem("c_qps"), sem("c_q"), sem("c_vops"), sem("c_vo")
        c_sps, c_max, c_sub, c_exp, c_sum, c_rec, c_p = (sem("c_sps"), sem("c_max"), sem("c_sub"), sem("c_exp"),
                                                         sem("c_sum"), sem("c_rec"), sem("c_p"))
        c_tps, c_pT, c_ops, c_res, c_bn, c_mv, c_rstd, c_y = (sem("c_tps"), sem("c_pT"), sem("c_ops"), sem("c_res"),
                                                              sem("c_bn"), sem("c_mv"), sem("c_rstd"), sem("c_y"))

        def wait(eng, semaphore, n):
            if isinstance(n, int) and n <= 0:
                return
            eng.wait_ge(semaphore, n)

        def steps(eng, step, before, after, first, last):
            def one(t):
                step(t // 2, t % 2, lambda k: 0 <= t + k < B)
            lo = before // 2
            hi = (B - after) // 2
            for t in range(first, 2 * lo):
                one(t)
            with eng.Fori(lo, hi) as j:
                step(j, 0, lambda k: True)
                step(j, 1, lambda k: True)
            for t in range(2 * hi, last):
                one(t)

        block = ctx.enter_context(nc.Block())

        @block.sync
        def _(sp):
            sp.dma_start(pos_sb[:, :], w_pos).then_inc(l_pos, 16)
            sp.dma_start(xT_sb[:, 0, :], xT[0]).then_inc(l_xT[0], 16)
            sp.dma_start(vw_sb[:, :], v_w).then_inc(l_vw, 16)
            sp.dma_start(rows_sb[:, :], rows).then_inc(l_rows, 16)
            sp.dma_start(const_sb[:, :], w_const).then_inc(l_const, 16)
            sp.dma_start(lin_sb[:, :], w_lin).then_inc(l_lin, 16)
            sp.dma_start(xT_sb[:, 1, :], xT[1]).then_inc(l_xT[1], 16)
            sp.dma_start(dft_t_sb[:, :, :, :], dft_t).then_inc(l_t, 16)
            sp.dma_start(dft_f_sb[:, :, :], dft_f).then_inc(l_f, 16)
            sp.dma_start(main_sb[:, :], w_main).then_inc(l_main, 16)
            sp.dma_start(dft_i_sb[:, :, :, :], dft_i).then_inc(l_i, 16)
            sp.dma_start(slot_sb[:, :], w_slot).then_inc(l_slot, 16)

            def step(j, p, has):
                t = 2 * j + p
                ja, pa = later(j, p, -2)
                jb, pb = later(j, p, -1)
                if has(0):
                    wait(sp, l_exp[p], 16 * j)
                    sp.dma_start(exp_sb[:, bass.ds(t, 1), :].rearrange("p a f -> p (a f)"),
                                 experts[bass.ds(t, 1), :, :].rearrange("a p f -> p (a f)")).then_inc(l_exp[p], 16)
                if has(0):
                    wait(sp, s_res, t - 1)
                    sp.dma_start(x_sb[:, p, :], x[bass.ds(t, 1), :, :].rearrange("a p n -> p (a n)")
                                 ).then_inc(l_x[p], 16)
                if has(-2):
                    sp.wait_ge(s_v2, t - 1)
                    sp.dma_start(v2_out[bass.ds(2 * ja + pa, 1), :, :].rearrange("a p n -> p (a n)"),
                                 v2_sb[:, pa, :, :].rearrange("p h d -> p (h d)")).then_inc(st_v2[pa], 16)
                if has(2):
                    sp.wait_ge(s_ups, t + 1)
                    sp.dma_start(xT_sb[:, p, :], xT[bass.ds(t + 2, 1), :, :].rearrange("a p n -> p (a n)")
                                 ).then_inc(l_xT[p], 16)
                if has(-1):
                    sp.wait_ge(s_x1, t)
                    sp.dma_start(x1_out[bass.ds(2 * jb + pb, 1), :, :].rearrange("a p n -> p (a n)"),
                                 x1_sb[:, pb, :, :].rearrange("p h d -> p (h d)")).then_inc(st_x1[pb], 16)
                    sp.wait_ge(s_x1T, t)
                    sp.dma_start(x1T_all[:, bass.ds(2 * jb + pb, 1), :].rearrange("p a n -> p (a n)"),
                                 x1T_sb[:, pb, :]).then_inc(st_x1T[pb], 16)

            steps(sp, step, 4, 2, 0, B + 2)

            for p in range(2):
                sp.wait_ge(st_v2[p], 16 * PAIRS)
                sp.wait_ge(st_x1[p], 16 * PAIRS)

            def values(j, p, has):
                t = 2 * j + p
                wait(sp, d_zps, t - 1)
                sp.dma_start(v2_in[:, p, :], v2_out[bass.ds(t, 1), :, :].rearrange("a p n -> p (a n)")
                             ).then_inc(l_v2[p], 16)
            steps(sp, values, 4, 0, 0, B)

            def residuals(j, p, has):
                t = 2 * j + p
                if has(0):
                    wait(sp, c_res, t - 1)
                    sp.dma_start(x1_in[:, p, :], x1_out[bass.ds(t, 1), :, :].rearrange("a p n -> p (a n)")
                                 ).then_inc(l_x1[p], 16)
                if has(-2):
                    ja, pa = later(j, p, -2)
                    sp.wait_ge(c_y, t - 1)
                    sp.dma_start(out[bass.ds(2 * ja + pa, 1), :, :].rearrange("a p n -> p (a n)"),
                                 y_out[:, pa, :, :].rearrange("p h d -> p (h d)")).then_inc(st_out[pa], 16)
            steps(sp, residuals, 4, 0, 0, B + 2)
            for p in range(2):
                sp.wait_ge(st_out[p], 16 * PAIRS)

        @block.tensor
        def _(pe):
            mm = nc.tensor.matmul

            def project_v(j, p):
                for h in range(2):
                    mm(bank[h][:, 0:CH], xT_sb[:, p, h * P:(h + 1) * P], vw_sb[:, :], start=True, stop=False)
                    mm(bank[h][:, 0:CH], ones_bf[:, :], row_parts[:, ROW_V:ROW_V + CH],
                       start=False, stop=True).then_inc(s_vps, 1)

            pe.wait_ge(l_const, 16)
            pe.wait_ge(l_lin, 16)
            for layer in range(4):
                pe.wait_ge(s_pact, layer + 1)
                for c in range(2):
                    nc.tensor.transpose(bank[7][0:R, c * P:(c + 1) * P], pact[:, c, :], ident).then_inc(s_ptr, 1)
                if layer == 0:
                    pe.wait_ge(l_xT[0], 16)
                    pe.wait_ge(l_vw, 16)
                    pe.wait_ge(s_rows, 1)
                    pe.wait_ge(s_ones, 1)
                    project_v(0, 0)
                if layer == 1:
                    pe.wait_ge(l_slot, 16)
                    mm(bank[4][:, 0:S], slot("d_Wq"), slot("slotT"), start=True, stop=True).then_inc(s_dq, 1)
                if layer == 2:
                    pe.wait_ge(s_dqb, 1)
                    blocks = dq_blocks[:, :, :].rearrange("p h s -> p (h s)")
                    mm(bank[4][:, 0:HS], slot("d_WkT"), blocks, start=True, stop=True)
                    for c in range(2):
                        last = mm(bank[4][:, HS + c:HS + c + 1], blocks[:, c * P:(c + 1) * P], slot("d_bk"),
                                  start=True, stop=True)
                    last.then_inc(s_dA, 1)
                pe.wait_ge(s_pactT, layer + 1)
                w = lin_sb[:, layer * R:(layer + 1) * R] if layer < 3 else lin_sb[:, 3 * R:3 * R + CH]
                for c in range(2):
                    o = bank[5 + c][:, 0:R] if layer < 3 else bank[5 + c][:, 0:CH]
                    mm(o, pactT[:, c, :], w, start=True, stop=True).then_inc(s_plin, 1)
            pe.wait_ge(s_coef, 2)
            pe.wait_ge(l_t, 16)
            pe.wait_ge(s_prep, 1)
            for part in range(2):
                for q in range(NQ):
                    o = bank[4 + 2 * part + q][:, 0:CH]
                    mm(o, dft_t_sb[:, 0, part, q * P:(q + 1) * P], coef[:, 0, :], start=True, stop=False)
                    mm(o, dft_t_sb[:, 1, part, q * P:(q + 1) * P], coef[:, 1, :], start=False,
                       stop=True).then_inc(s_Aps, 1)

            def step(j, p, has):
                t = 2 * j + p
                if has(0):
                    pe.wait_ge(s_sd, t + 1)
                    if isinstance(t, int) and t == 0:
                        pe.wait_ge(s_A, 4)
                        pe.wait_ge(l_f, 16)
                    else:
                        pe.wait_ge(s_prod, 4 * t)
                    for q in range(NQ):
                        mm(bank[4 + q][:, 0:CH], dft_f_sb[:, 0, q * P:(q + 1) * P], vs_sb[:, p, :],
                           start=True, stop=True)
                    for q in range(NQ):
                        final = mm(bank[6 + q][:, 0:CH], dft_f_sb[:, 1, q * P:(q + 1) * P], vd_sb[:, p, :],
                                   start=True, stop=True)
                    final.then_inc(s_fwd, 1)
                if has(-2):
                    _, pa = later(j, p, -2)
                    pe.wait_ge(s_x1T, t - 1)
                    for h in range(2):
                        final = mm(bank[1][:, 256 + h * D:256 + (h + 1) * D], x1T_sb[:, pa, h * P:(h + 1) * P],
                                   slot("d_Wv"), start=True, stop=True)
                    final.then_inc(s_v2ps, 1)
                if has(1):
                    jn, pn = later(j, p, 1)
                    pe.wait_ge(l_xT[pn], 16 * (jn + 1))
                    pe.wait_ge(s_v, 2 * t + 2)
                    wait(pe, s_res, t - 1)
                    wait(pe, s_v2, t - 1)
                    project_v(jn, pn)
                if has(0):
                    if isinstance(t, int) and t == 0:
                        pe.wait_ge(l_main, 16)
                    wait(pe, s_y, 2 * t)
                    for c in range(NC):
                        o = bank[2 + c // 2][:, (c % 2) * N:(c % 2 + 1) * N]
                        mm(o, main("u_w")[:, c * P:(c + 1) * P], xT_sb[:, p, :], start=True,
                           stop=True).then_inc(s_ups, 1) if c == NC - 1 else \
                            mm(o, main("u_w")[:, c * P:(c + 1) * P], xT_sb[:, p, :], start=True, stop=True)
                if has(-1):
                    pe.wait_ge(s_g, t)
                    if has(1):
                        pe.wait_ge(s_v, 2 * t + 4)
                    wait(pe, s_res, t - 1)
                    for h in range(2):
                        o = bank[0][:, h * D:(h + 1) * D]
                        for c in range(NC):
                            mm(o, g_sb[:, c, h, :], main("o_w")[:, c * D:(c + 1) * D], start=(c == 0), stop=False)
                        final = mm(o, ones_bf[:, :], row_parts[:, ROW_O:ROW_O + D], start=False, stop=True)
                    final.then_inc(s_ops, 1)
                if has(0):
                    if isinstance(t, int) and t == 0:
                        pe.wait_ge(l_i, 16)
                    pe.wait_ge(s_u, t + 1)
                    pe.wait_ge(s_Y, 2 * t + 1)
                    for c in range(NC):
                        for q in range(NQ):
                            mm(bank[2][:, c * P:(c + 1) * P], Y_r[:, q, c * P:(c + 1) * P], dft_i_sb[:, q, 0, :],
                               start=(q == 0), stop=(q == NQ - 1))
                    pe.wait_ge(s_Y, 2 * t + 2)
                    for c in range(NC):
                        for q in range(NQ):
                            final = mm(bank[3][:, c * P:(c + 1) * P], Y_i[:, q, c * P:(c + 1) * P],
                                       dft_i_sb[:, q, 1, :], start=(q == 0), stop=(q == NQ - 1))
                    final.then_inc(s_inv, 1)
                if has(-1):
                    _, pb = later(j, p, -1)
                    pe.wait_ge(s_x1, t)
                    wait(pe, s_v2, t - 1)
                    for h in range(2):
                        final = nc.tensor.transpose(bank[1][:, h * P:(h + 1) * P], x1_sb[:, pb, h, :], ident)
                    final.then_inc(s_xtps, 1)

            steps(pe, step, 4, 2, 0, B + 2)

            def scores(j, p):
                t = 2 * j + p
                wait(pe, d_p, 2 * (t - 1))
                for c in range(2):
                    final = mm(bank[p][:, c * N:(c + 1) * N], dA[:, c * P:(c + 1) * P],
                               x1T_all[:, bass.ds(t, 1), :].rearrange("p a n -> p (a n)"), start=True, stop=True)
                final.then_inc(d_sps, 1)

            for p in range(2):
                pe.wait_ge(st_x1T[p], 16 * PAIRS)
            pe.wait_ge(s_res, B)
            pe.wait_ge(s_v2, B)
            scores(0, 0)

            def dispatch(j, p, has):
                t = 2 * j + p
                if has(1):
                    scores(*later(j, p, 1))
                if has(0):
                    pe.wait_ge(d_p, 2 * t + 2)
                    wait(pe, d_pT, t - 1)
                    for h in range(2):
                        for c in range(2):
                            final = nc.tensor.transpose(bank[2 + p][:, h * HS + c * P:h * HS + (c + 1) * P],
                                                        dP[:, p, c, h * P:(h + 1) * P], ident)
                    final.then_inc(d_tps, 1)
                if has(-1):
                    jb, pb = later(j, p, -1)
                    pe.wait_ge(d_pT, t)
                    pe.wait_ge(l_v2[pb], 16 * (jb + 1))
                    wait(pe, d_z, 2 * (t - 2))
                    for c in range(2):
                        for h in range(2):
                            final = mm(bank[4 + pb][:, c * D:(c + 1) * D], dPT[:, pb, h, c * P:(c + 1) * P],
                                       v2_in[:, pb, h * D:(h + 1) * D],
                                       start=(h == 0), stop=(h == 1))
                    final.then_inc(d_zps, 1)
                if has(-2):
                    _, pa = later(j, p, -2)
                    pe.wait_ge(d_z, 2 * (t - 1))
                    wait(pe, d_o, t - 3)
                    for c in range(2):
                        final = mm(bank[6 + pa][:, 0:S], dZ[:, pa, c, :], const("pick"), start=(c == 0), stop=(c == 1))
                    final.then_inc(d_ops, 1)

            steps(pe, dispatch, 4, 2, 0, B + 2)

            flat = "p s b -> p (s b)"
            pe.wait_ge(d_o, B)
            mm(bank[0][:, 0:S * B], slot("d_Wo"), dOT[:, :, :].rearrange("p b s -> p s b"), start=True,
               stop=True).then_inc(e_pe, 1)
            pe.wait_ge(e_chain, 2)
            mm(bank[1][:, 0:S * B], const("mean"), eo[:, :, :].rearrange(flat), start=True, stop=True).then_inc(e_pe, 1)
            pe.wait_ge(e_chain, 4)
            mm(bank[1][:, 0:S * B], const("mean"), esq[:, :, :].rearrange(flat), start=True,
               stop=True).then_inc(e_pe, 1)
            pe.wait_ge(e_chain, 7)
            for p in range(2):
                pe.wait_ge(l_exp[p], 16 * PAIRS)
            for half in range(2):
                for e in range(half * 8, half * 8 + 8):
                    for k, w0 in ((2, 0), (4, FF)):
                        for f in range(NFC):
                            o = bank[k + half][:, ((e % 8) * NFC + f) * B:((e % 8) * NFC + f + 1) * B]
                            final = mm(o, exp_sb[:, e, w0 + f * P:w0 + (f + 1) * P], eh[:, e, :], start=True, stop=True)
                final.then_inc(e_pe, 1)
            for half in range(2):
                pe.wait_ge(e_ug, half + 1)
                for e in range(half * 8, half * 8 + 8):
                    for f in range(NFC):
                        final = mm(bank[6][:, e * B:(e + 1) * B], exp_sb[:, e, 2 * FF + f * P:2 * FF + (f + 1) * P],
                                   eug[:, e, f, :], start=(f == 0), stop=(f == NFC - 1))
            final.then_inc(e_pe, 1)
            pe.wait_ge(e_chain, 9)
            mm(bank[0][:, 0:S * B], slot("c_Wk"), eo2[:, :, :].rearrange("p s b -> p b s"), start=True, stop=True)
            mm(bank[0][:, S * B:2 * S * B], slot("c_Wv"), eo2[:, :, :].rearrange("p s b -> p b s"), start=True,
               stop=True).then_inc(e_pe, 1)

            pe.wait_ge(e_chain, 11)

            def queries(j, p):
                t = 2 * j + p
                wait(pe, c_q, t)
                mm(bank[0][:, 0:N], slot("c_Wq"), x1T_all[:, bass.ds(t, 1), :].rearrange("p a n -> p (a n)"),
                   start=True, stop=True).then_inc(c_qps, 1)

            queries(0, 0)

            def combine(j, p, has):
                t = 2 * j + p
                if has(0):
                    pe.wait_ge(c_blk, 2 * t + 2)
                    wait(pe, c_vo, t)
                    for c in range(2):
                        final = mm(bank[1][:, c * D:(c + 1) * D],
                                   vb[:, p, :, :].rearrange("p h s -> p (h s)")[:, c * P:(c + 1) * P],
                                   slot("c_Wo"), start=True, stop=True)
                    final.then_inc(c_vops, 1)
                    pe.wait_ge(c_q, t + 1)
                    wait(pe, c_sub, t - 1)
                    for h in range(2):
                        final = mm(bank[2 + p][:, h * HS:(h + 1) * HS], cqT[:, p, h * P:(h + 1) * P],
                                   kb[:, p, :, :].rearrange("p h s -> p (h s)"), start=True, stop=True)
                    final.then_inc(c_sps, 1)
                if has(1):
                    queries(*later(j, p, 1))
                if has(-1):
                    _, pb = later(j, p, -1)
                    pe.wait_ge(c_p, t)
                    wait(pe, c_pT, t - 2)
                    for c in range(2):
                        for h in range(2):
                            final = nc.tensor.transpose(bank[4 + pb][:, c * N + h * P:c * N + (h + 1) * P],
                                                        cp[:, pb, h, c * P:(c + 1) * P], ident)
                    final.then_inc(c_tps, 1)
                if has(-2):
                    _, pa = later(j, p, -2)
                    pe.wait_ge(c_pT, t - 1)
                    pe.wait_ge(c_vo, t - 1)
                    wait(pe, c_res, t - 3)
                    for h in range(2):
                        o = bank[6 + pa][:, h * D:(h + 1) * D]
                        for c in range(2):
                            mm(o, cPT[:, pa, c, h * P:(h + 1) * P], vo[:, pa, c, :], start=(c == 0), stop=False)
                        final = mm(o, ones_bf[:, :], row_parts[:, ROW_C:ROW_C + D], start=False, stop=True)
                    final.then_inc(c_ops, 1)

            steps(pe, combine, 4, 2, 0, B + 2)

        @block.scalar
        def _(act):
            def silu_v():
                pass

            def v_of(j, p):
                t = 2 * j + p
                for h in range(2):
                    act.wait_ge(s_vps, 2 * t + h + 1)
                    if h == 0:
                        wait(act, s_sd, t)
                    nc.scalar.activation(v_sb[:, h, :], bank[h][:, 0:CH], ACT.Silu).then_inc(s_v, 1)

            v_of(0, 0)

            def step(j, p, has):
                t = 2 * j + p
                if has(-2):
                    ja, pa = later(j, p, -2)
                    act.wait_ge(s_v2ps, t - 1)
                    wait(act, st_v2[pa], 16 * ja)
                    nc.scalar.activation(v2_sb[:, pa, :, :].rearrange("p h d -> p (h d)"), bank[1][:, 256:512],
                                         ACT.Copy).then_inc(s_v2, 1)
                if has(1):
                    v_of(*later(j, p, 1))
                if has(0):
                    act.wait_ge(s_ups, t + 1)
                    wait(act, s_g, t - 1)
                    for c in range(NC):
                        final = nc.scalar.activation(u_sb[:, p, c, :],
                                                     bank[2 + c // 2][:, (c % 2) * N:(c % 2 + 1) * N],
                                                     ACT.Silu, bias=main("u_b")[:, c:c + 1])
                    final.then_inc(s_u, 1)
                    act.wait_ge(s_inv, t + 1)
                    wait(act, s_y, 2 * t)
                    nc.scalar.activation(odd_sb[:, :, :].rearrange("p c n -> p (c n)"), bank[3][:, 0:CH],
                                         ACT.Copy).then_inc(s_odd, 1)
                if has(-1):
                    jb, pb = later(j, p, -1)
                    act.wait_ge(s_xtps, t)
                    wait(act, st_x1T[pb], 16 * jb)
                    nc.scalar.activation(x1T_sb[:, pb, :], bank[1][:, 0:N], ACT.Copy).then_inc(s_x1T, 1)

            steps(act, step, 4, 2, 0, B + 2)

            def dispatch(j, p, has):
                t = 2 * j + p
                if has(0):
                    act.wait_ge(d_nb, t + 1)
                    wait(act, d_tps, t - 1)
                    wait(act, d_rec, t - 1)
                    for c in range(2):
                        nc.scalar.activation(dP[:, p, c, :], bank[p][:, c * N:(c + 1) * N], ACT.Exp,
                                             bias=dnb[:, p, c:c + 1], scale=SCALE,
                                             accum_out=dsum[:, p, c:c + 1]).then_inc(d_p, 1)
                    act.wait_ge(d_tps, t + 1)
                    wait(act, d_zps, t - 1)
                    nc.scalar.activation(dPT[:, p, :, :].rearrange("p h s -> p (h s)"), bank[2 + p][:, :],
                                         ACT.Copy).then_inc(d_pT, 1)

            steps(act, dispatch, 4, 0, 0, B)

            for half in range(2):
                es = slice(half * 8, half * 8 + 8)
                for k, buf in ((0, eu_in), (1, eg_in)):
                    act.wait_ge(e_in, 2 * half + k + 1)
                    v = buf[:, es, :, :].rearrange("p e f b -> p (e f b)")
                    nc.scalar.activation(v, v, ACT.Silu).then_inc(e_act, 1)

            def q_out(j, p):
                t = 2 * j + p
                act.wait_ge(c_qps, t + 1)
                wait(act, c_sps, t - 1)
                nc.scalar.activation(cqT[:, p, :], bank[0][:, 0:N], ACT.Identity, bias=slot("c_bq")).then_inc(c_q, 1)

            q_out(0, 0)

            def combine(j, p, has):
                t = 2 * j + p
                if has(0):
                    act.wait_ge(c_vops, t + 1)
                    wait(act, c_ops, t - 1)
                    nc.scalar.activation(vo[:, p, :, :].rearrange("p c d -> p (c d)"), bank[1][:, 0:2 * D],
                                         ACT.Copy).then_inc(c_vo, 1)
                if has(1):
                    q_out(*later(j, p, 1))
                if has(0):
                    act.wait_ge(c_sub, t + 1)
                    wait(act, c_p, t - 1)
                    nc.scalar.activation(ce[:, p, :, :].rearrange("p h s -> p (h s)"),
                                         cs[:, p, :, :].rearrange("p h s -> p (h s)"), ACT.Exp,
                                         scale=SCALE).then_inc(c_exp, 1)
                if has(-1):
                    _, pb = later(j, p, -1)
                    act.wait_ge(c_tps, t)
                    wait(act, c_ops, t - 2)
                    nc.scalar.activation(cPT[:, pb, :, :].rearrange("p c n -> p (c n)"), bank[4 + pb][:, :],
                                         ACT.Copy).then_inc(c_pT, 1)

            steps(act, combine, 4, 2, 0, B + 1)

        @block.gpsimd
        def _(pool):
            tt = nc.gpsimd.tensor_tensor
            nc.gpsimd.memset(ones_bf[:, :], 1.0).then_inc(s_ones, 1)
            nc.gpsimd.memset(plus_half[:, :], 0.5).then_inc(s_half, 1)
            nc.gpsimd.memset(minus_half[:, :], -0.5).then_inc(s_half, 1)
            pool.wait_ge(s_half, 2)
            for layer in range(4):
                pool.wait_ge(s_pms, layer + 1)
                tt(prms[:, 1, :], prms[:, 0, :], plus_half[:, :], ALU.pow).then_inc(s_prms, 1)

            def sums(j, p):
                t = 2 * j + p
                pool.wait_ge(s_v, 2 * t + 2)
                wait(pool, s_fwd, t - 1)
                tt(vs_sb[:, p, :], v_sb[:, 0, :], v_sb[:, 1, :], ALU.add)
                tt(vd_sb[:, p, :], v_sb[:, 0, :], v_sb[:, 1, :], ALU.subtract).then_inc(s_sd, 1)

            sums(0, 0)

            def step(j, p, has):
                t = 2 * j + p
                if has(-1):
                    _, pb = later(j, p, -1)
                    pool.wait_ge(s_y, 2 * t)
                    pool.wait_ge(s_u, t)
                    wait(pool, s_ops, t - 1)
                    tt(g_sb[:, :, :, :].rearrange("p c h n -> p c (h n)"),
                       y_sb[:, :, :, :].rearrange("p c h n -> p c (h n)"), u_sb[:, pb, :, :],
                       ALU.mult).then_inc(s_g, 1)
                if has(0):
                    wait(pool, s_inv, t)
                    pool.wait_ge(s_prod, 4 * t + 2)
                    tt(Y_r[:, :, :], rr[:, :, :], ii[:, :, :], ALU.subtract).then_inc(s_Y, 1)
                    pool.wait_ge(s_prod, 4 * t + 4)
                    tt(Y_i[:, :, :], ri[:, :, :], ir[:, :, :], ALU.add).then_inc(s_Y, 1)
                if has(-1):
                    pool.wait_ge(s_ve, t)
                    tt(rstd_sb[:, :], ve_sb[:, :], minus_half[:, 0:2], ALU.pow).then_inc(s_rstd, 1)
                if has(1):
                    sums(*later(j, p, 1))

            steps(pool, step, 4, 2, 0, B + 1)

            pool.wait_ge(e_ve, 1)
            tt(erstd.rearrange("p s b -> p (s b)"), eh2.rearrange("p s b -> p (s b)"), minus_half[:, :],
               ALU.pow).then_inc(e_rstd, 1)
            mask = const("headmask").rearrange("p (h s) -> p h s", h=H)
            pool.wait_ge(e_chain, 11)

            def blocks(j, p):
                t = 2 * j + p
                wait(pool, c_sps, t - 1)
                tt(kb[:, p, :, :], ckT[:, bass.ds(t, 1), :].to_broadcast([P, H, S]), mask, ALU.mult).then_inc(c_blk, 1)
                wait(pool, c_vops, t - 1)
                tt(vb[:, p, :, :], cvT[:, bass.ds(t, 1), :].to_broadcast([P, H, S]), mask, ALU.mult).then_inc(c_blk, 1)

            blocks(0, 0)

            def combine(j, p, has):
                t = 2 * j + p
                if has(1):
                    blocks(*later(j, p, 1))
                if has(-2):
                    pool.wait_ge(c_ve, t - 1)
                    tt(rstd_sb[:, :], ve_sb[:, :], minus_half[:, 0:2], ALU.pow).then_inc(c_rstd, 1)
                if has(0):
                    pool.wait_ge(c_rec, t + 1)
                    wait(pool, c_tps, t - 1)
                    tt(cp[:, p, :, :].rearrange("p h (g s) -> p (h g) s", s=S), ce[:, p, :, :],
                       crec[:, p, :].unsqueeze(2).to_broadcast([P, 2 * H, S]), ALU.mult).then_inc(c_p, 1)

            steps(pool, combine, 4, 2, 0, B + 2)

        @block.vector
        def _(dve):
            tt = nc.vector.tensor_tensor
            ts = nc.vector.tensor_scalar
            stt = nc.vector.scalar_tensor_tensor
            copy = nc.vector.tensor_copy

            nc.vector.memset(row_parts[:, :], 0.0).then_inc(s_rowstep, 1)
            nc.vector.memset(pactT[R:R + 1, :, :], 1.0).then_inc(s_rowstep, 1)
            dve.wait_ge(l_rows, 16)
            dve.wait_ge(l_pos, 16)
            copy(row_hi[:, :], rows_sb[:, :]).then_inc(s_rowstep, 1)
            dve.wait_ge(s_rowstep, 3)
            tt(row_res, rows_sb[:, :], row_hi[:, :], ALU.subtract).then_inc(s_rowstep, 1)
            dve.wait_ge(s_rowstep, 4)
            copy(row_mid[:, :], row_res).then_inc(s_rowstep, 1)
            dve.wait_ge(s_rowstep, 5)
            tt(row_res2, row_res, row_mid[:, :], ALU.subtract).then_inc(s_rowstep, 1)
            dve.wait_ge(s_rowstep, 6)
            copy(row_lo[:, :], row_res2).then_inc(s_rowstep, 1)
            part = pos("part")[0:3, :]
            ts(row_sum, row_hi[:, :], part[:, 0:1], None, ALU.mult).then_inc(s_rowstep, 1)
            dve.wait_ge(s_rowstep, 8)
            stt(row_sum2, row_mid[:, :], part[:, 1:2], row_sum, ALU.mult,
                ALU.add).then_inc(s_rowstep, 1)
            dve.wait_ge(s_rowstep, 9)
            stt(row_parts[0:3, :], row_lo[:, :], part[:, 2:3], row_sum2, ALU.mult, ALU.add).then_inc(s_rows, 1)

            chain = [0]

            def link(ins):
                chain[0] += 1
                ins.then_inc(s_pchain, 1)
                dve.wait_ge(s_pchain, chain[0])

            for c in range(2):
                first = stt(ph[:, c, :], pos("pos_w"), pos("index")[:, c:c + 1], pos("pos_b"), ALU.mult, ALU.add)
                if c == 1:
                    link(first)
            for layer in range(4):
                link(tt(psq[:, :, :], ph[:, :, :], ph[:, :, :], ALU.mult))
                link(nc.vector.tensor_reduce(pss[:, :], psq[:, :, :], AX.X, ALU.add))
                ts(prms[:, 0, :], pss[:, :], 1.0 / R, None, ALU.mult).then_inc(s_pms, 1)
                dve.wait_ge(s_prms, layer + 1)
                link(ts(prms[:, 2, :], prms[:, 1, :], RMS_EPS, None, ALU.add))
                link(nc.vector.reciprocal(pss[:, :], prms[:, 2, :]))
                wait(dve, s_ptr, 2 * layer)
                for c in range(2):
                    last = ts(pact[:, c, :], ph[:, c, :], pss[:, c:c + 1], 0.0, ALU.mult, ALU.max)
                last.then_inc(s_pact, 1)
                dve.wait_ge(s_ptr, 2 * layer + 2)
                wait(dve, s_plin, 2 * layer)
                copy(pactT[0:R, :, :].rearrange("p c n -> p (c n)"), bank[7][0:R, 0:2 * P]).then_inc(s_pactT, 1)
                if layer == 1:
                    dve.wait_ge(s_dq, 1)
                    link(ts(dqT[:, :], bank[4][:, 0:S], slot("d_bq"), None, ALU.add))
                    tt(dq_blocks[:, :, :], dqT[:, :].unsqueeze(1).to_broadcast([P, H, S]),
                       const("headmask").rearrange("p (h s) -> p h s", h=H), ALU.mult).then_inc(s_dqb, 1)
                if layer == 2:
                    dve.wait_ge(s_dA, 1)
                    copy(dA[:, :], bank[4][:, 0:HS])
                    copy(dc[:, :], bank[4][:, HS:HS + 2]).then_inc(s_prep, 1)
                dve.wait_ge(s_plin, 2 * layer + 2)
                for c in range(2):
                    if layer < 3:
                        last = copy(ph[:, c, :], bank[5 + c][:, 0:R])
                        if c == 1:
                            link(last)
                    else:
                        ts(coef[:, c, :], bank[5 + c][:, 0:CH], pos("decay")[:, c:c + 1], None,
                           ALU.mult).then_inc(s_coef, 1)
            dve.wait_ge(s_prep, 1)
            ts(dcs[:, :], dc[:, :], SCALE, None, ALU.mult)
            ts(slot_b[:, :], slot("slotT"), slot("d_bo"), None, ALU.add)
            for part in range(2):
                for q in range(NQ):
                    dve.wait_ge(s_Aps, 2 * part + q + 1)
                    copy((A_r, A_i)[part][:, q, :], bank[4 + 2 * part + q][:, 0:CH]).then_inc(s_A, 1)
            dve.wait_ge(s_A, 4)

            def statistics(src, n, s_src, s_stats, s_mean, s_eps):
                dve.wait_ge(s_src, n + 1)
                for h in range(2):
                    last = nc.vector.bn_stats(st_sb[:, h, :], src[:, h, :])
                last.then_inc(s_stats, 1)
                dve.wait_ge(s_stats, n + 1)
                dve.sem_inc(s_seen, 1)
                for h in range(2):
                    last = nc.vector.bn_aggr(mv_sb[:, h, :], st_sb[:, h, :])
                last.then_inc(s_mean, 1)
                dve.wait_ge(s_mean, n + 1)
                ts(ve_sb[:, :], mv_sb[:, :, 1], LN_EPS, None, ALU.add).then_inc(s_eps, 1)

            def normalise(src, dst, n, s_inverse, s_dst):
                dve.wait_ge(s_inverse, n + 1)
                for h in range(2):
                    last = ts(dst[:, h, :], src[:, h, :], mv_sb[:, h, 0:1], rstd_sb[:, h:h + 1], ALU.subtract,
                              ALU.mult)
                last.then_inc(s_dst, 1)

            def step(j, p, has):
                t = 2 * j + p
                if has(0):
                    dve.wait_ge(s_fwd, t + 1)
                    wait(dve, s_Y, 2 * t)
                    for q in range(NQ):
                        last = tt(rr[:, q, :], bank[4 + q][:, 0:CH], A_r[:, q, :], ALU.mult)
                    last.then_inc(s_prod, 1)
                    for q in range(NQ):
                        last = tt(ii[:, q, :], bank[6 + q][:, 0:CH], A_i[:, q, :], ALU.mult)
                    last.then_inc(s_prod, 1)
                    for q in range(NQ):
                        last = tt(ri[:, q, :], bank[6 + q][:, 0:CH], A_r[:, q, :], ALU.mult)
                    last.then_inc(s_prod, 1)
                    for q in range(NQ):
                        last = tt(ir[:, q, :], bank[4 + q][:, 0:CH], A_i[:, q, :], ALU.mult)
                    last.then_inc(s_prod, 1)
                if has(-1):
                    jb, pb = later(j, p, -1)
                    dve.wait_ge(l_x[pb], 16 * (jb + 1))
                    wait(dve, s_x1, t - 1)
                    dve.wait_ge(s_ops, t)
                    tt(res_sb[:, :, :].rearrange("p h d -> p (h d)"), bank[0][:, 0:2 * D],
                       x_sb[:, pb, :], ALU.add).then_inc(s_res, 1)
                    wait(dve, st_x1[pb], 16 * jb)
                    wait(dve, s_xtps, t - 2)
                    statistics(res_sb, t - 1, s_res, s_bn, s_mv, s_ve)
                    normalise(res_sb, x1_sb[:, pb, :, :], t - 1, s_rstd, s_x1)
                if has(0):
                    dve.wait_ge(s_odd, t + 1)
                    wait(dve, s_g, t)
                    even = bank[2][:, 0:CH].rearrange("p (c n) -> p c n", c=NC)
                    tt(y_sb[:, :, 0, :], even, odd_sb[:, :, :], ALU.add).then_inc(s_y, 1)
                    tt(y_sb[:, :, 1, :], even, odd_sb[:, :, :], ALU.subtract).then_inc(s_y, 1)

            steps(dve, step, 4, 2, 0, B + 1)

            def dispatch(j, p, has):
                t = 2 * j + p
                if has(0):
                    dve.wait_ge(d_sps, t + 1)
                    nc.vector.tensor_reduce(dmax[:, p, :], bank[p][:, :].rearrange("p (c n) -> p c n", c=2), AX.X,
                                            ALU.max).then_inc(d_max, 1)
                    dve.wait_ge(d_max, t + 1)
                    tt(dmc[:, p, :], dmax[:, p, :], dc[:, :], ALU.add).then_inc(d_mc, 1)
                    dve.wait_ge(d_mc, t + 1)
                    stt(dnb[:, p, :], dmc[:, p, :], -SCALE, dcs[:, :], ALU.mult, ALU.add).then_inc(d_nb, 1)
                if has(-1):
                    _, pb = later(j, p, -1)
                    dve.wait_ge(d_p, 2 * t)
                    nc.vector.reciprocal(drec[:, pb, :], dsum[:, pb, :]).then_inc(d_rec, 1)
                    dve.wait_ge(d_rec, t)
                    dve.wait_ge(d_zps, t)
                    wait(dve, d_ops, t - 2)
                    for c in range(2):
                        stt(dZ[:, pb, c, :], bank[4 + pb][:, c * D:(c + 1) * D], drec[:, pb, c:c + 1],
                            const("diagmask")[:, c * D:(c + 1) * D], ALU.mult, ALU.mult).then_inc(d_z, 1)
                if has(-2):
                    ja, pa = later(j, p, -2)
                    dve.wait_ge(d_ops, t - 1)
                    ts(dOT[:, bass.ds(2 * ja + pa, 1), :].rearrange("p a s -> p (a s)"), bank[6 + pa][:, 0:S],
                       slot("d_bv"), None, ALU.add).then_inc(d_o, 1)

            steps(dve, dispatch, 4, 2, 0, B + 2)

            def bcast(ap):
                return ap.unsqueeze(2).to_broadcast([P, ap.shape[1], B])

            en = [0]

            def elink(ins):
                en[0] += 1
                ins.then_inc(e_chain, 1)
                dve.wait_ge(e_chain, en[0])

            def grid(ap):
                return ap.rearrange("p (s b) -> p s b", b=B)

            dve.wait_ge(e_pe, 1)
            elink(copy(eh1[:, :, :], grid(bank[0][:, 0:S * B])))
            elink(tt(eo[:, :, :], eh1[:, :, :], bcast(slot_b[:, :]), ALU.add))
            dve.wait_ge(e_pe, 2)
            elink(tt(ecen[:, :, :], eo[:, :, :], grid(bank[1][:, 0:S * B]), ALU.subtract))
            elink(tt(esq[:, :, :], ecen[:, :, :], ecen[:, :, :], ALU.mult))
            dve.wait_ge(e_pe, 3)
            ts(eh2[:, :, :], grid(bank[1][:, 0:S * B]), LN_EPS, None, ALU.add).then_inc(e_ve, 1)
            dve.wait_ge(e_rstd, 1)
            elink(tt(eh1[:, :, :], ecen[:, :, :], erstd[:, :, :], ALU.mult))
            elink(tt(eh2[:, :, :], eh1[:, :, :], bcast(slot("ln_gT")), ALU.mult))
            elink(tt(eh[:, :, :], eh2[:, :, :], bcast(slot("ln_bT")), ALU.add))
            for half in range(2):
                dve.wait_ge(e_pe, 4 + half)
                cols = slice(half * 8 * NFC, (half + 1) * 8 * NFC)
                es = slice(half * 8, half * 8 + 8)
                for k, buf, name in ((2, eu_in, "b1T"), (4, eg_in, "bgT")):
                    tt(buf[:, es, :, :].rearrange("p e f b -> p (e f) b"), grid(bank[k + half][:, :]),
                       bcast(slot(name)[:, cols]), ALU.add).then_inc(e_in, 1)
            for half in range(2):
                dve.wait_ge(e_act, 2 * half + 2)
                es = slice(half * 8, half * 8 + 8)
                tt(eug[:, es, :, :].rearrange("p e f b -> p (e f b)"),
                   eu_in[:, es, :, :].rearrange("p e f b -> p (e f b)"),
                   eg_in[:, es, :, :].rearrange("p e f b -> p (e f b)"), ALU.mult).then_inc(e_ug, 1)
            dve.wait_ge(e_pe, 6)
            elink(tt(ey[:, :, :], eo[:, :, :], grid(bank[6][:, 0:S * B]), ALU.add))
            elink(tt(eo2[:, :, :], ey[:, :, :], bcast(slot("b2T")), ALU.add))
            dve.wait_ge(e_pe, 7)
            elink(ts(ckT[:, :, :].rearrange("p b s -> p (b s)"), bank[0][:, 0:S * B], slot("c_bk"), None, ALU.add))
            elink(ts(cvT[:, :, :].rearrange("p b s -> p (b s)"), bank[0][:, S * B:2 * S * B], slot("c_bv"), None,
                     ALU.add))

            def combine(j, p, has):
                t = 2 * j + p
                if has(0):
                    dve.wait_ge(c_sps, t + 1)
                    s = bank[2 + p][:, :].rearrange("p (h s) -> p h s", s=S)
                    nc.vector.tensor_reduce(cmax[:, p, :], s, AX.X, ALU.max).then_inc(c_max, 1)
                    dve.wait_ge(c_max, t + 1)
                    wait(dve, c_exp, t - 1)
                    tt(cs[:, p, :, :], s, cmax[:, p, :].unsqueeze(2).to_broadcast([P, 2 * H, S]),
                       ALU.subtract).then_inc(c_sub, 1)
                if has(-2):
                    ja, pa = later(j, p, -2)
                    dve.wait_ge(c_ops, t - 1)
                    dve.wait_ge(l_x1[pa], 16 * (ja + 1))
                    wait(dve, c_y, t - 2)
                    tt(cres[:, :, :].rearrange("p h d -> p (h d)"), bank[6 + pa][:, 0:2 * D],
                       x1_in[:, pa, :], ALU.add).then_inc(c_res, 1)
                    wait(dve, st_out[pa], 16 * ja)
                    statistics(cres, t - 2, c_res, c_bn, c_mv, c_ve)
                if has(0):
                    dve.wait_ge(c_exp, t + 1)
                    wait(dve, c_p, t - 1)
                    nc.vector.tensor_reduce(csum[:, p, :], ce[:, p, :, :], AX.X, ALU.add).then_inc(c_sum, 1)
                    dve.wait_ge(c_sum, t + 1)
                    nc.vector.reciprocal(crec[:, p, :], csum[:, p, :]).then_inc(c_rec, 1)
                if has(-2):
                    _, pa = later(j, p, -2)
                    normalise(cres, y_out[:, pa, :, :], t - 2, c_rstd, c_y)

            steps(dve, combine, 4, 2, 0, B + 2)


def constants():
    theta = np.pi * (2 * np.arange(NF) + 1) / (2 * NF)
    centre = np.arange(P) - (N - 1) / 2
    t = np.arange(N)
    dft_f = np.stack([np.cos(np.outer(centre, theta)), -np.sin(np.outer(centre, theta))], 1)
    dft_t = np.stack([np.cos(np.outer(t, theta)), -np.sin(np.outer(t, theta))], 1).reshape(2, P, 2, NF)
    dft_i = np.stack([np.cos(np.outer(theta, centre)), -np.sin(np.outer(theta, centre))], 1) / NF
    row = np.arange(P)
    of_head = (row[:, None] // DH == np.arange(H)[None, :])
    headmask = np.repeat(of_head[:, :, None], S, 2).reshape(P, HS)
    diag = np.stack([(c * (P // S) + row[:, None] // S) == (np.arange(D)[None, :] // DH) for c in range(2)], 1)
    pick = (row[:, None] % S) == np.arange(S)[None, :]
    const = np.concatenate([np.eye(P), np.full((P, P), 1.0 / D), headmask, diag.reshape(P, 2 * D), pick], 1)
    decay = np.float32(0.99) ** t.astype(np.float32)
    f = lambda a: np.ascontiguousarray(a, dtype=np.float32)
    return dict(dft_f=f(dft_f), dft_t=f(dft_t.transpose(1, 0, 2, 3)),
                dft_i=f(dft_i.reshape(NQ, P, 2, P).transpose(1, 0, 2, 3)), const=f(const),
                index=f(t.reshape(2, P).T), decay=f(decay.reshape(2, P).T), part=f(row[:, None] == np.arange(3)))


def kernel(**inputs):
    import concourse.bacc as bacc
    from concourse.bass_utils import run_bass_kernel_spmd

    a = {k.removeprefix("L0_"): np.asarray(v) for k, v in inputs.items()}
    cat = lambda *parts: np.ascontiguousarray(np.concatenate(parts, 1))
    col = lambda v: v.reshape(-1, P).T
    c = constants()
    x = np.stack([a["attn_x"][:, :P], a["attn_x"][:, P:][:, ::-1]], 1)
    arrays = {
        "xT": x.transpose(0, 3, 1, 2).reshape(B, D, N),
        "x": x.transpose(0, 2, 1, 3).reshape(B, P, N),
        "v_w": a["attn_v_w"],
        "w_main": cat(a["attn_u_w"], a["attn_o_w"].reshape(NC, P, D).transpose(1, 0, 2).reshape(P, NC * D),
                      col(a["attn_u_b"])),
        "w_slot": cat(a["ffn_d_Wq"], a["ffn_d_Wk"].T, a["ffn_d_Wv"], a["ffn_d_Wo"], a["ffn_c_Wq"], a["ffn_c_Wk"],
                      a["ffn_c_Wv"], a["ffn_c_Wo"], a["ffn_slot_query"][0].T, col(a["ffn_d_bq"]), col(a["ffn_d_bk"]),
                      col(a["ffn_d_bv"]), col(a["ffn_d_bo"]), col(a["ffn_c_bq"]), col(a["ffn_c_bk"]),
                      col(a["ffn_c_bv"]), a["ffn_e_ln_g"].T, a["ffn_e_ln_b"].T, col(a["ffn_e_b1"]),
                      col(a["ffn_e_bg"]), a["ffn_e_b2"].T),
        "w_const": c["const"],
        "w_pos": cat(np.broadcast_to(a["attn_pos_w"], (P, R)), np.broadcast_to(a["attn_pos_b"][None], (P, R)),
                     c["index"], c["decay"], c["part"]),
        "w_lin": np.concatenate([cat(a["attn_lw0"], a["attn_lw1"], a["attn_lw2"], a["attn_out_w"]),
                                 cat(a["attn_lb0"][None], a["attn_lb1"][None], a["attn_lb2"][None],
                                     a["attn_out_b"][None])], 0),
        "rows": np.broadcast_to(cat(a["attn_v_b"][None], a["attn_o_b"][None], a["ffn_c_bo"][None]), (3, ROWS)),
        "dft_t": c["dft_t"], "dft_f": c["dft_f"], "dft_i": c["dft_i"],
        "experts": np.concatenate([a["ffn_e_W1"], a["ffn_e_Wg"],
                                   a["ffn_e_W2"].reshape(H, NFC, P, D).transpose(0, 2, 1, 3).reshape(H, P, FF)], 2),
    }
    arrays = {k: np.ascontiguousarray(v) for k, v in arrays.items()}
    nc = bacc.Bacc("TRN2", target_bir_lowering=False, num_devices=1)
    args = [nc.dram_tensor(k, v.shape, F32, kind="ExternalInput").ap() for k, v in arrays.items()]
    args.append(nc.dram_tensor("out", (B, P, N), F32, kind="ExternalOutput").ap())
    build(nc, *args)
    r = run_bass_kernel_spmd(nc, [arrays], core_ids=[0]).results[0]["out"]
    y = r.reshape(B, P, 2, D).transpose(0, 2, 1, 3)
    return np.ascontiguousarray(np.concatenate([y[:, 0], y[:, 1, ::-1]], 1))
```

```python
from contextlib import ExitStack

import numpy as np

import concourse.bass as bass
from concourse import mybir

F32 = mybir.dt.float32
BF16 = mybir.dt.bfloat16
ALU = mybir.AluOpType
ACT = mybir.ActivationFunctionType
AX = mybir.AxisListType

P = 128
B = 16
N = 256
D = 128
CH = 384
NC = CH // P
R = 64
NF = 256
NQ = NF // P
H = 16
DH = D // H
S = 16
HS = H * S
FF = 512
NFC = FF // P
ROW = 32
EG = P // ROW
GROUPS = H // EG
LN_EPS = 1e-5
RMS_EPS = 1e-8
SCALE = float(1.0 / np.sqrt(DH))
SHARED = 10752
PAIRS = B // 2

W_MAIN = {"u_w": CH, "o_w": NC * D, "u_b": NC}
W_SLOT = {"d_Wq": D, "d_WkT": D, "d_Wv": D, "d_Wo": D, "c_Wq": D, "c_Wk": D, "c_Wv": D, "c_Wo": D,
          "slotT": S, "d_bq": 1, "d_bk": 1, "d_bv": 1, "d_bo": 1, "c_bq": 1, "c_bk": 1, "c_bv": 1,
          "ln_gT": S, "ln_bT": S, "b2T": S}
W_CONST = {"ident": P, "mean": P, "headmask": HS, "diagmask": 2 * D, "pick": S}
W_POS = {"pos_w": R, "pos_b": R, "index": 2, "decay": 2, "part": 3}
ROW_V, ROW_O, ROW_C = 0, CH, CH + D
ROWS = CH + 2 * D


def columns(widths):
    at, out = 0, {}
    for name, width in widths.items():
        out[name] = slice(at, at + width)
        at += width
    return out, at


def later(j, p, k):
    return j + (p + k) // 2, (p + k) % 2


def build(nc, xT, x, v_w, w_main, w_slot, w_const, w_pos, w_lin, rows, dft_t, dft_f, dft_i, experts, bias_1, bias_g, out):
    ctx = ExitStack()
    main_at, main_n = columns(W_MAIN)
    slot_at, slot_n = columns(W_SLOT)
    const_at, const_n = columns(W_CONST)
    pos_at, pos_n = columns(W_POS)
    with ctx:
        def sb(name, shape, dt=F32):
            return ctx.enter_context(nc.sbuf_tensor(name, shape, dt))

        def sem(name):
            return ctx.enter_context(nc.semaphore(name))

        shared = sb("shared", [P, SHARED])
        top = [0]

        def phase():
            top[0] = 0

        def part_of(shape):
            n = int(np.prod(shape))
            v = shared[:, top[0]:top[0] + n]
            top[0] += n
            assert top[0] <= SHARED
            if len(shape) == 1:
                return v
            names = "abcd"[:len(shape)]
            return v.rearrange(f"p ({' '.join(names)}) -> p {' '.join(names)}",
                               **dict(zip(names[1:], shape[1:])))

        vw_sb = sb("vw_sb", [P, CH])
        main_sb = sb("main_sb", [P, main_n])
        slot_sb = sb("slot_sb", [P, slot_n])
        const_sb = sb("const_sb", [P, const_n])
        pos_sb = sb("pos_sb", [P, pos_n])
        rows_sb = sb("rows_sb", [3, ROWS])
        dft_f_sb = sb("dft_f_sb", [P, 2, NF])
        dft_i_sb = sb("dft_i_sb", [P, NQ, 2, P])
        exp_sb = sb("exp_sb", [P, H, 3 * FF])

        def main(name):
            return main_sb[:, main_at[name]]

        def slot(name):
            return slot_sb[:, slot_at[name]]

        def const(name):
            return const_sb[:, const_at[name]]

        def pos(name):
            return pos_sb[:, pos_at[name]]

        ident = const("ident")
        minus_half = sb("minus_half", [P, 2])
        plus_half = sb("plus_half", [P, 2])
        ve_sb = sb("ve_sb", [P, 2])
        ones_bf = sb("ones_bf", [P, P], BF16)
        row_parts = sb("row_parts", [P, ROWS], BF16)

        ph = sb("ph", [P, 2, R])
        psq = sb("psq", [P, 2, R])
        pss = sb("pss", [P, 2])
        prms = sb("prms", [P, 3, 2])
        pact = sb("pact", [P, 2, R])
        pactT = sb("pactT", [R + 1, 2, P])
        A_r = sb("A_r", [P, NQ, CH])
        A_i = sb("A_i", [P, NQ, CH])

        phase()
        xT_sb = sb("xT_sb", [P, 2, N])
        x_sb = sb("x_sb", [P, 2, N])
        v_sb = part_of([2, CH])
        vs_sb = part_of([2, CH])
        vd_sb = part_of([2, CH])
        u_sb = part_of([2, NC, N])
        rr = part_of([NQ, CH])
        ii = part_of([NQ, CH])
        ri = part_of([NQ, CH])
        ir = part_of([NQ, CH])
        Y_r = part_of([NQ, CH])
        Y_i = part_of([NQ, CH])
        odd_sb = part_of([NC, P])
        y_sb = part_of([NC, 2, P])
        g_sb = part_of([NC, 2, P])
        res_sb = sb("res_sb", [P, 2, D])
        st_sb = sb("st_sb", [P, 2, 6])
        mv_sb = sb("mv_sb", [P, 2, 2])
        rstd_sb = sb("rstd_sb", [P, 2])
        x1_sb = sb("x1_sb", [P, 2, 2, D])
        x1T_sb = sb("x1T_sb", [P, 2, N])
        v2_sb = sb("v2_sb", [P, 2, 2, D])
        flat_u = u_sb.rearrange("p a c n -> p (a c n)")
        dft_t_sb = flat_u[:, 0:4 * NF].rearrange("p (a b n) -> p a b n", a=2, b=2)
        coef = Y_r
        lin_sb = y_sb.rearrange("p c h n -> p (c h n)")[0:R + 1, 0:3 * R + CH]
        flat_g = g_sb.rearrange("p c h n -> p (c h n)")
        row_hi = flat_g[0:3, 0:ROWS // 2].bitcast(BF16)
        row_mid = flat_g[0:3, ROWS // 2:ROWS].bitcast(BF16)
        row_lo = odd_sb.rearrange("p c n -> p (c n)")[0:3, 0:ROWS // 2].bitcast(BF16)
        row_res = rr[0:3, :, :].rearrange("p a b -> p (a b)")[:, 0:ROWS]
        row_res2 = ii[0:3, :, :].rearrange("p a b -> p (a b)")[:, 0:ROWS]
        row_sum = ri[0:3, :, :].rearrange("p a b -> p (a b)")[:, 0:ROWS]
        row_sum2 = ir[0:3, :, :].rearrange("p a b -> p (a b)")[:, 0:ROWS]
        x1T_all = sb("x1T_all", [P, B, N])
        x1_out = nc.dram_tensor("x1_scratch", (B, P, N), F32, kind="Internal").ap()
        v2_out = nc.dram_tensor("v2_scratch", (B, P, N), F32, kind="Internal").ap()
        v2_in = sb("v2_in", [P, 2, N])
        x1_in = sb("x1_in", [P, 2, N])

        phase()
        dqT = sb("dqT", [P, S])
        dq_blocks = sb("dq_blocks", [P, H, S])
        dA = sb("dA", [P, HS])
        dc = sb("dc", [P, 2])
        dcs = sb("dcs", [P, 2])
        dmax = sb("dmax", [P, 2, 2])
        dmc = sb("dmc", [P, 2, 2])
        dnb = sb("dnb", [P, 2, 2])
        dP = part_of([2, 2, N])
        dsum = sb("dsum", [P, 2, 2])
        drec = sb("drec", [P, 2, 2])
        dPT = part_of([2, 2, HS])
        dZ = part_of([2, 2, D])
        dOT = sb("dOT", [P, B, S])

        phase()
        ecen = part_of([S, B])
        esq = part_of([S, B])
        ediag = part_of([2, P])
        eh1 = part_of([S, B])
        eh2 = part_of([S, B])
        ey = part_of([S, B])
        eo2 = part_of([S, B])
        eu_in = part_of([2, FF])
        eg_in = part_of([2, FF])
        eug = part_of([2, FF])
        eugT = part_of([2, FF])
        eyr = part_of([GROUPS, D])
        top[0] = SHARED - 2 * GROUPS * FF
        eb1 = part_of([GROUPS, FF])
        ebg = part_of([GROUPS, FF])
        eh = sb("eh", [P, S, ROW])
        eo = sb("eo", [P, S, B])
        slot_b = sb("slot_b", [P, S])
        eve = sb("eve", [P, 2])
        erstd = sb("erstd", [P, 2])
        ones_f = sb("ones_f", [P, P])
        ckT = sb("ckT", [P, B, S])
        cvT = sb("cvT", [P, B, S])

        phase()
        kb = part_of([2, H, S])
        vb = part_of([2, H, S])
        cqT = part_of([2, N])
        vo = part_of([2, 2, D])
        cmax = sb("cmax", [P, 2, 2 * H])
        cs = part_of([2, 2 * H, S])
        ce = part_of([2, 2 * H, S])
        csum = sb("csum", [P, 2, 2 * H])
        crec = sb("crec", [P, 2, 2 * H])
        cp = part_of([2, 2, HS])
        cPT = part_of([2, 2, N])
        cres = part_of([2, D])
        y_out = part_of([2, 2, D])

        bank = [ctx.enter_context(nc.psum_tensor(f"bank{i}", [P, 512], F32)) for i in range(8)]

        l_xT = [sem("l_xT0"), sem("l_xT1")]
        l_vw, l_pos, l_const, l_rows, l_lin = sem("l_vw"), sem("l_pos"), sem("l_const"), sem("l_rows"), sem("l_lin")
        l_main, l_slot, l_t, l_f, l_i, l_x = (sem("l_main"), sem("l_slot"), sem("l_t"), sem("l_f"), sem("l_i"),
                                             [sem("l_x0"), sem("l_x1")])
        l_v2 = [sem("l_v20"), sem("l_v21")]
        l_x1 = [sem("l_x10"), sem("l_x11")]
        l_exp = [sem("l_exp0"), sem("l_exp1")]
        st_x1 = [sem("st_x10"), sem("st_x11")]
        st_x1T = [sem("st_x1T0"), sem("st_x1T1")]
        st_v2 = [sem("st_v20"), sem("st_v21")]
        st_out = [sem("st_out0"), sem("st_out1")]
        s_ones, s_rowstep, s_rows = sem("s_ones"), sem("s_rowstep"), sem("s_rows")
        s_pchain, s_pact, s_ptr, s_pactT, s_plin = (sem("s_pchain"), sem("s_pact"), sem("s_ptr"), sem("s_pactT"),
                                                    sem("s_plin"))
        s_coef, s_Aps, s_A = sem("s_coef"), sem("s_Aps"), sem("s_A")
        s_pms, s_prms, s_half = sem("s_pms"), sem("s_prms"), sem("s_half")
        s_seen = sem("s_seen")
        s_ve, c_ve, e_ve, e_rstd = sem("s_ve"), sem("c_ve"), sem("e_ve"), sem("e_rstd")
        s_dq, s_dqb, s_dA, s_prep, s_pchain2 = sem("s_dq"), sem("s_dqb"), sem("s_dA"), sem("s_prep"), sem("s_pchain2")
        s_vps, s_v, s_sum, s_diff = sem("s_vps"), sem("s_v"), sem("s_sum"), sem("s_diff")
        s_fwd, s_prod, s_Y = sem("s_fwd"), sem("s_prod"), sem("s_Y")
        s_ups, s_u, s_inv, s_odd, s_y, s_g = (sem("s_ups"), sem("s_u"), sem("s_inv"), sem("s_odd"), sem("s_y"),
                                              sem("s_g"))
        s_ops, s_res, s_bn, s_mv, s_rstd, s_x1 = (sem("s_ops"), sem("s_res"), sem("s_bn"), sem("s_mv"),
                                                  sem("s_rstd"), sem("s_x1"))
        s_xtps, s_x1T, s_v2ps, s_v2 = sem("s_xtps"), sem("s_x1T"), sem("s_v2ps"), sem("s_v2")
        d_sps, d_max, d_mc, d_nb, d_p, d_tps, d_pT = (sem("d_sps"), sem("d_max"), sem("d_mc"), sem("d_nb"),
                                                      sem("d_p"), sem("d_tps"), sem("d_pT"))
        d_rec, d_zps, d_z, d_ops, d_o = sem("d_rec"), sem("d_zps"), sem("d_z"), sem("d_ops"), sem("d_o")
        e_pe, e_chain, e_in, e_act, e_ug = sem("e_pe"), sem("e_chain"), sem("e_in"), sem("e_act"), sem("e_ug")
        e_up, e_tr, e_ugT, e_y, e_zero = sem("e_up"), sem("e_tr"), sem("e_ugT"), sem("e_y"), sem("e_zero")
        l_bias = [sem("l_bias1"), sem("l_biasg")]
        c_blk, c_qps, c_q, c_vops, c_vo = sem("c_blk"), sem("c_qps"), sem("c_q"), sem("c_vops"), sem("c_vo")
        c_sps, c_max, c_sub, c_exp, c_sum, c_rec, c_p = (sem("c_sps"), sem("c_max"), sem("c_sub"), sem("c_exp"),
                                                         sem("c_sum"), sem("c_rec"), sem("c_p"))
        c_tps, c_pT, c_ops, c_res, c_bn, c_mv, c_rstd, c_y = (sem("c_tps"), sem("c_pT"), sem("c_ops"), sem("c_res"),
                                                              sem("c_bn"), sem("c_mv"), sem("c_rstd"), sem("c_y"))

        def wait(eng, semaphore, n):
            if isinstance(n, int) and n <= 0:
                return
            eng.wait_ge(semaphore, n)

        def steps(eng, step, before, after, first, last):
            def one(t):
                step(t // 2, t % 2, lambda k: 0 <= t + k < B)
            lo = before // 2
            hi = (B - after) // 2
            for t in range(first, 2 * lo):
                one(t)
            with eng.Fori(lo, hi) as j:
                step(j, 0, lambda k: True)
                step(j, 1, lambda k: True)
            for t in range(2 * hi, last):
                one(t)

        block = ctx.enter_context(nc.Block())

        @block.sync
        def _(sp):
            sp.dma_start(pos_sb[:, :], w_pos).then_inc(l_pos, 16)
            sp.dma_start(xT_sb[:, 0, :], xT[0]).then_inc(l_xT[0], 16)
            sp.dma_start(vw_sb[:, :], v_w).then_inc(l_vw, 16)
            sp.dma_start(rows_sb[:, :], rows).then_inc(l_rows, 16)
            sp.dma_start(const_sb[:, :], w_const).then_inc(l_const, 16)
            sp.dma_start(lin_sb[:, :], w_lin).then_inc(l_lin, 16)
            sp.dma_start(xT_sb[:, 1, :], xT[1]).then_inc(l_xT[1], 16)
            sp.dma_start(dft_t_sb[:, :, :, :], dft_t).then_inc(l_t, 16)
            sp.dma_start(dft_f_sb[:, :, :], dft_f).then_inc(l_f, 16)
            sp.dma_start(main_sb[:, :], w_main).then_inc(l_main, 16)
            sp.dma_start(dft_i_sb[:, :, :, :], dft_i).then_inc(l_i, 16)
            sp.dma_start(slot_sb[:, :], w_slot).then_inc(l_slot, 16)

            def step(j, p, has):
                t = 2 * j + p
                ja, pa = later(j, p, -2)
                jb, pb = later(j, p, -1)
                if has(0):
                    wait(sp, l_exp[p], 16 * j)
                    sp.dma_start(exp_sb[:, bass.ds(t, 1), :].rearrange("p a f -> p (a f)"),
                                 experts[bass.ds(t, 1), :, :].rearrange("a p f -> p (a f)")).then_inc(l_exp[p], 16)
                if has(0):
                    wait(sp, s_res, t - 1)
                    sp.dma_start(x_sb[:, p, :], x[bass.ds(t, 1), :, :].rearrange("a p n -> p (a n)")
                                 ).then_inc(l_x[p], 16)
                if has(-2):
                    sp.wait_ge(s_x1T, t - 1)
                    sp.dma_start(x1T_all[:, bass.ds(2 * ja + pa, 1), :].rearrange("p a n -> p (a n)"),
                                 x1T_sb[:, pa, :]).then_inc(st_x1T[pa], 16)
                    sp.wait_ge(s_v2, t - 1)
                    sp.dma_start(v2_out[bass.ds(2 * ja + pa, 1), :, :].rearrange("a p n -> p (a n)"),
                                 v2_sb[:, pa, :, :].rearrange("p h d -> p (h d)")).then_inc(st_v2[pa], 16)
                if has(2):
                    sp.wait_ge(s_ups, t + 1)
                    sp.dma_start(xT_sb[:, p, :], xT[bass.ds(t + 2, 1), :, :].rearrange("a p n -> p (a n)")
                                 ).then_inc(l_xT[p], 16)
                if has(-1):
                    jb, pb = later(j, p, -1)
                    sp.wait_ge(s_x1, t)
                    sp.dma_start(x1_out[bass.ds(2 * jb + pb, 1), :, :].rearrange("a p n -> p (a n)"),
                                 x1_sb[:, pb, :, :].rearrange("p h d -> p (h d)")).then_inc(st_x1[pb], 16)

            steps(sp, step, 4, 2, 0, B + 2)

            for p in range(2):
                sp.wait_ge(st_v2[p], 16 * PAIRS)
                sp.wait_ge(st_x1[p], 16 * PAIRS)
            sp.dma_start(eb1, bias_1).then_inc(l_bias[0], 16)
            sp.dma_start(ebg, bias_g).then_inc(l_bias[1], 16)

            def values(j, p, has):
                t = 2 * j + p
                wait(sp, d_zps, t - 1)
                sp.dma_start(v2_in[:, p, :], v2_out[bass.ds(t, 1), :, :].rearrange("a p n -> p (a n)")
                             ).then_inc(l_v2[p], 16)
            steps(sp, values, 4, 0, 0, B)

            def residuals(j, p, has):
                t = 2 * j + p
                if has(0):
                    wait(sp, c_res, t - 1)
                    sp.dma_start(x1_in[:, p, :], x1_out[bass.ds(t, 1), :, :].rearrange("a p n -> p (a n)")
                                 ).then_inc(l_x1[p], 16)
                if has(-2):
                    ja, pa = later(j, p, -2)
                    sp.wait_ge(c_y, t - 1)
                    sp.dma_start(out[bass.ds(2 * ja + pa, 1), :, :].rearrange("a p n -> p (a n)"),
                                 y_out[:, pa, :, :].rearrange("p h d -> p (h d)")).then_inc(st_out[pa], 16)
            steps(sp, residuals, 4, 0, 0, B + 2)
            for p in range(2):
                sp.wait_ge(st_out[p], 16 * PAIRS)

        @block.tensor
        def _(pe):
            mm = nc.tensor.matmul

            def project_v(j, p, before):
                for h in range(2):
                    if h == 1:
                        wait(pe, s_x1T, before)
                    mm(bank[h][:, 0:CH], xT_sb[:, p, h * P:(h + 1) * P], vw_sb[:, :], start=True, stop=False)
                    mm(bank[h][:, 0:CH], ones_bf[:, :], row_parts[:, ROW_V:ROW_V + CH],
                       start=False, stop=True).then_inc(s_vps, 1)

            pe.wait_ge(l_const, 16)
            pe.wait_ge(l_lin, 16)
            for layer in range(4):
                pe.wait_ge(s_pact, layer + 1)
                for c in range(2):
                    nc.tensor.transpose(bank[7][0:R, c * P:(c + 1) * P], pact[:, c, :], ident).then_inc(s_ptr, 1)
                if layer == 0:
                    pe.wait_ge(l_xT[0], 16)
                    pe.wait_ge(l_vw, 16)
                    pe.wait_ge(s_rows, 1)
                    pe.wait_ge(s_ones, 1)
                    project_v(0, 0, 0)
                if layer == 1:
                    pe.wait_ge(l_slot, 16)
                    mm(bank[4][:, 0:S], slot("d_Wq"), slot("slotT"), start=True, stop=True).then_inc(s_dq, 1)
                if layer == 2:
                    pe.wait_ge(s_dqb, 1)
                    blocks = dq_blocks[:, :, :].rearrange("p h s -> p (h s)")
                    mm(bank[4][:, 0:HS], slot("d_WkT"), blocks, start=True, stop=True)
                    for c in range(2):
                        last = mm(bank[4][:, HS + c:HS + c + 1], blocks[:, c * P:(c + 1) * P], slot("d_bk"),
                                  start=True, stop=True)
                    last.then_inc(s_dA, 1)
                pe.wait_ge(s_pactT, layer + 1)
                w = lin_sb[:, layer * R:(layer + 1) * R] if layer < 3 else lin_sb[:, 3 * R:3 * R + CH]
                for c in range(2):
                    o = bank[5 + c][:, 0:R] if layer < 3 else bank[5 + c][:, 0:CH]
                    mm(o, pactT[:, c, :], w, start=True, stop=True).then_inc(s_plin, 1)
            pe.wait_ge(s_coef, 2)
            pe.wait_ge(l_t, 16)
            pe.wait_ge(s_prep, 1)
            for part in range(2):
                for q in range(NQ):
                    o = bank[4 + 2 * part + q][:, 0:CH]
                    mm(o, dft_t_sb[:, 0, part, q * P:(q + 1) * P], coef[:, 0, :], start=True, stop=False)
                    mm(o, dft_t_sb[:, 1, part, q * P:(q + 1) * P], coef[:, 1, :], start=False,
                       stop=True).then_inc(s_Aps, 1)

            def step(j, p, has):
                t = 2 * j + p
                if has(0):
                    if isinstance(t, int) and t == 0:
                        pe.wait_ge(s_A, 4)
                        pe.wait_ge(l_f, 16)
                    else:
                        pe.wait_ge(s_prod, 4 * t)
                    pe.wait_ge(s_sum, t + 1)
                    for q in range(NQ):
                        final = mm(bank[4 + q][:, 0:CH], dft_f_sb[:, 0, q * P:(q + 1) * P], vs_sb[:, p, :],
                                   start=True, stop=True)
                    final.then_inc(s_fwd, 1)
                    pe.wait_ge(s_diff, t + 1)
                    for q in range(NQ):
                        final = mm(bank[6 + q][:, 0:CH], dft_f_sb[:, 1, q * P:(q + 1) * P], vd_sb[:, p, :],
                                   start=True, stop=True)
                    final.then_inc(s_fwd, 1)
                if has(-2):
                    _, pa = later(j, p, -2)
                    pe.wait_ge(s_x1, t - 1)
                    wait(pe, s_v2, t - 2)
                    for h in range(2):
                        final = nc.tensor.transpose(bank[1][:, h * P:(h + 1) * P], x1_sb[:, pa, h, :], ident)
                    final.then_inc(s_xtps, 1)
                if has(1):
                    jn, pn = later(j, p, 1)
                    pe.wait_ge(l_xT[pn], 16 * (jn + 1))
                    pe.wait_ge(s_v, 2 * t + 2)
                    wait(pe, s_res, t - 1)
                    project_v(jn, pn, t - 1)
                if has(0):
                    if isinstance(t, int) and t == 0:
                        pe.wait_ge(l_main, 16)
                    wait(pe, s_y, 2 * t)
                    for c in range(NC):
                        final = mm(bank[2 + c // 2][:, (c % 2) * N:(c % 2 + 1) * N],
                                   main("u_w")[:, c * P:(c + 1) * P], xT_sb[:, p, :], start=True, stop=True)
                    final.then_inc(s_ups, 1)
                if has(-1):
                    pe.wait_ge(s_g, t)
                    if has(1):
                        pe.wait_ge(s_v, 2 * t + 4)
                    wait(pe, s_res, t - 1)
                    for h in range(2):
                        o = bank[0][:, h * D:(h + 1) * D]
                        for c in range(NC):
                            mm(o, g_sb[:, c, h, :], main("o_w")[:, c * D:(c + 1) * D], start=(c == 0), stop=False)
                        final = mm(o, ones_bf[:, :], row_parts[:, ROW_O:ROW_O + D], start=False, stop=True)
                    final.then_inc(s_ops, 1)
                if has(-2):
                    _, pa = later(j, p, -2)
                    pe.wait_ge(s_x1T, t - 1)
                    for h in range(2):
                        final = mm(bank[1][:, 256 + h * D:256 + (h + 1) * D], x1T_sb[:, pa, h * P:(h + 1) * P],
                                   slot("d_Wv"), start=True, stop=True)
                    final.then_inc(s_v2ps, 1)
                if has(0):
                    if isinstance(t, int) and t == 0:
                        pe.wait_ge(l_i, 16)
                    pe.wait_ge(s_u, t + 1)
                    pe.wait_ge(s_Y, 2 * t + 1)
                    for c in range(NC):
                        for q in range(NQ):
                            mm(bank[2][:, c * P:(c + 1) * P], Y_r[:, q, c * P:(c + 1) * P], dft_i_sb[:, q, 0, :],
                               start=(q == 0), stop=(q == NQ - 1))
                    pe.wait_ge(s_Y, 2 * t + 2)
                    for c in range(NC):
                        for q in range(NQ):
                            final = mm(bank[3][:, c * P:(c + 1) * P], Y_i[:, q, c * P:(c + 1) * P],
                                       dft_i_sb[:, q, 1, :], start=(q == 0), stop=(q == NQ - 1))
                    final.then_inc(s_inv, 1)

            steps(pe, step, 4, 2, 0, B + 2)

            def scores(j, p):
                t = 2 * j + p
                wait(pe, d_p, 2 * (t - 1))
                for c in range(2):
                    final = mm(bank[p][:, c * N:(c + 1) * N], dA[:, c * P:(c + 1) * P],
                               x1T_all[:, bass.ds(t, 1), :].rearrange("p a n -> p (a n)"), start=True, stop=True)
                final.then_inc(d_sps, 1)

            for p in range(2):
                pe.wait_ge(st_x1T[p], 16 * PAIRS)
            pe.wait_ge(s_res, B)
            pe.wait_ge(s_v2, B)
            scores(0, 0)
            scores(0, 1)

            def dispatch(j, p, has):
                t = 2 * j + p
                if has(0):
                    pe.wait_ge(d_p, 2 * t + 2)
                    wait(pe, d_pT, t - 1)
                    for h in range(2):
                        for c in range(2):
                            final = nc.tensor.transpose(bank[2 + p][:, h * HS + c * P:h * HS + (c + 1) * P],
                                                        dP[:, p, c, h * P:(h + 1) * P], ident)
                    final.then_inc(d_tps, 1)
                if has(2):
                    scores(*later(j, p, 2))
                if has(-1):
                    jb, pb = later(j, p, -1)
                    pe.wait_ge(d_pT, t)
                    pe.wait_ge(l_v2[pb], 16 * (jb + 1))
                    wait(pe, d_z, 2 * (t - 2))
                    for c in range(2):
                        for h in range(2):
                            final = mm(bank[4 + pb][:, c * D:(c + 1) * D], dPT[:, pb, h, c * P:(c + 1) * P],
                                       v2_in[:, pb, h * D:(h + 1) * D],
                                       start=(h == 0), stop=(h == 1))
                    final.then_inc(d_zps, 1)
                if has(-2):
                    _, pa = later(j, p, -2)
                    pe.wait_ge(d_z, 2 * (t - 1))
                    wait(pe, d_o, t - 3)
                    for c in range(2):
                        final = mm(bank[6 + pa][:, 0:S], dZ[:, pa, c, :], const("pick"), start=(c == 0), stop=(c == 1))
                    final.then_inc(d_ops, 1)

            steps(pe, dispatch, 4, 2, 0, B + 2)

            flat = "p s b -> p (s b)"
            pe.wait_ge(d_o, B)
            mm(bank[0][:, 0:S * B], slot("d_Wo"), dOT[:, :, :].rearrange("p b s -> p s b"), start=True,
               stop=True).then_inc(e_pe, 1)
            pe.wait_ge(e_chain, 2)
            mm(bank[1][:, 0:S * B], const("mean"), eo[:, :, :].rearrange(flat), start=True, stop=True).then_inc(e_pe, 1)
            pe.wait_ge(e_chain, 4)
            for c in range(2):
                final = mm(bank[1][:, c:c + 1], esq.rearrange(flat)[:, c * P:(c + 1) * P], const("mean")[:, 0:1],
                           start=True, stop=True)
            final.then_inc(e_pe, 1)
            pe.wait_ge(e_chain, 5)
            pe.wait_ge(e_zero, 2)
            mm(bank[1][:, 0:S * B], ones_f[:, :], ediag.rearrange("p c n -> p (c n)"), start=True,
               stop=True).then_inc(e_pe, 1)
            pe.wait_ge(e_chain, 8)
            for p in range(2):
                pe.wait_ge(l_exp[p], 16 * PAIRS)

            def up(g):
                wait(pe, e_in, 2 * (g - 1))
                for k, w0 in ((2, 0), (4, FF)):
                    for e in range(EG):
                        final = mm(bank[k + g % 2][e * ROW:(e + 1) * ROW, :], eh[:, g * EG + e, :],
                                   exp_sb[:, g * EG + e, w0:w0 + FF], start=True, stop=True)
                    final.then_inc(e_up, 1)

            def flip(g):
                pe.wait_ge(e_ug, g + 1)
                wait(pe, e_ugT, g - 1)
                for f in range(NFC):
                    final = nc.tensor.transpose(bank[6 + g % 2][:, f * P:(f + 1) * P], eug[:, g % 2, f * P:(f + 1) * P],
                                                ident)
                final.then_inc(e_tr, 1)

            def down(g):
                pe.wait_ge(e_ugT, g + 1)
                for f in range(NFC):
                    for e in range(EG):
                        w0 = 2 * FF + f * P
                        final = mm(bank[0][e * ROW:(e + 1) * ROW, g * D:(g + 1) * D],
                                   eugT[:, g % 2, f * P + e * ROW:f * P + (e + 1) * ROW],
                                   exp_sb[:, g * EG + e, w0:w0 + P], start=(f == 0), stop=(f == NFC - 1))
                final.then_inc(e_y, 1)

            for g in range(GROUPS + 2):
                if g < GROUPS:
                    up(g)
                if 1 <= g <= GROUPS:
                    flip(g - 1)
                if g >= 2:
                    down(g - 2)
            pe.wait_ge(e_chain, 9)
            for g in range(GROUPS):
                final = nc.tensor.transpose(bank[1][:, g * P:(g + 1) * P], eyr[:, g, :], ident)
            final.then_inc(e_pe, 1)
            pe.wait_ge(e_chain, 11)
            mm(bank[0][:, 0:S * B], slot("c_Wk"), eo2[:, :, :].rearrange("p s b -> p b s"), start=True, stop=True)
            mm(bank[0][:, S * B:2 * S * B], slot("c_Wv"), eo2[:, :, :].rearrange("p s b -> p b s"), start=True,
               stop=True).then_inc(e_pe, 1)

            pe.wait_ge(e_chain, 13)

            def queries(j, p):
                t = 2 * j + p
                wait(pe, c_q, t)
                mm(bank[0][:, 0:N], slot("c_Wq"), x1T_all[:, bass.ds(t, 1), :].rearrange("p a n -> p (a n)"),
                   start=True, stop=True).then_inc(c_qps, 1)

            queries(0, 0)

            def combine(j, p, has):
                t = 2 * j + p
                if has(0):
                    pe.wait_ge(c_blk, 2 * t + 2)
                    wait(pe, c_vo, t)
                    for c in range(2):
                        final = mm(bank[1][:, c * D:(c + 1) * D],
                                   vb[:, p, :, :].rearrange("p h s -> p (h s)")[:, c * P:(c + 1) * P],
                                   slot("c_Wo"), start=True, stop=True)
                    final.then_inc(c_vops, 1)
                    pe.wait_ge(c_q, t + 1)
                    wait(pe, c_sub, t - 1)
                    for h in range(2):
                        final = mm(bank[2 + p][:, h * HS:(h + 1) * HS], cqT[:, p, h * P:(h + 1) * P],
                                   kb[:, p, :, :].rearrange("p h s -> p (h s)"), start=True, stop=True)
                    final.then_inc(c_sps, 1)
                if has(1):
                    queries(*later(j, p, 1))
                if has(-1):
                    _, pb = later(j, p, -1)
                    pe.wait_ge(c_p, t)
                    wait(pe, c_pT, t - 2)
                    for c in range(2):
                        for h in range(2):
                            final = nc.tensor.transpose(bank[4 + pb][:, c * N + h * P:c * N + (h + 1) * P],
                                                        cp[:, pb, h, c * P:(c + 1) * P], ident)
                    final.then_inc(c_tps, 1)
                if has(-2):
                    _, pa = later(j, p, -2)
                    pe.wait_ge(c_pT, t - 1)
                    pe.wait_ge(c_vo, t - 1)
                    wait(pe, c_res, t - 3)
                    for h in range(2):
                        o = bank[6 + pa][:, h * D:(h + 1) * D]
                        for c in range(2):
                            mm(o, cPT[:, pa, c, h * P:(h + 1) * P], vo[:, pa, c, :], start=(c == 0), stop=False)
                        final = mm(o, ones_bf[:, :], row_parts[:, ROW_C:ROW_C + D], start=False, stop=True)
                    final.then_inc(c_ops, 1)

            steps(pe, combine, 4, 2, 0, B + 2)

        @block.scalar
        def _(act):
            def silu_v():
                pass

            def v_of(j, p):
                t = 2 * j + p
                for h in range(2):
                    act.wait_ge(s_vps, 2 * t + h + 1)
                    if h == 0:
                        wait(act, s_sum, t)
                        wait(act, s_diff, t)
                    nc.scalar.activation(v_sb[:, h, :], bank[h][:, 0:CH], ACT.Silu).then_inc(s_v, 1)

            v_of(0, 0)

            def step(j, p, has):
                t = 2 * j + p
                if has(-1):
                    act.wait_ge(s_inv, t)
                    wait(act, s_y, 2 * t - 2)
                    nc.scalar.activation(odd_sb[:, :, :].rearrange("p c n -> p (c n)"), bank[3][:, 0:CH],
                                         ACT.Copy).then_inc(s_odd, 1)
                if has(-2):
                    ja, pa = later(j, p, -2)
                    act.wait_ge(s_xtps, t - 1)
                    wait(act, st_x1T[pa], 16 * ja)
                    wait(act, s_v2ps, t - 3)
                    nc.scalar.activation(x1T_sb[:, pa, :], bank[1][:, 0:N], ACT.Copy).then_inc(s_x1T, 1)
                if has(1):
                    v_of(*later(j, p, 1))
                if has(0):
                    act.wait_ge(s_ups, t + 1)
                    wait(act, s_g, t - 1)
                    for c in range(NC):
                        final = nc.scalar.activation(u_sb[:, p, c, :],
                                                     bank[2 + c // 2][:, (c % 2) * N:(c % 2 + 1) * N],
                                                     ACT.Silu, bias=main("u_b")[:, c:c + 1])
                    final.then_inc(s_u, 1)
                if has(-2):
                    ja, pa = later(j, p, -2)
                    act.wait_ge(s_v2ps, t - 1)
                    wait(act, st_v2[pa], 16 * ja)
                    nc.scalar.activation(v2_sb[:, pa, :, :].rearrange("p h d -> p (h d)"), bank[1][:, 256:512],
                                         ACT.Copy).then_inc(s_v2, 1)

            steps(act, step, 4, 2, 0, B + 2)

            def weights(j, p):
                t = 2 * j + p
                act.wait_ge(d_nb, t + 1)
                wait(act, d_tps, t - 1)
                wait(act, d_rec, t - 1)
                for c in range(2):
                    nc.scalar.activation(dP[:, p, c, :], bank[p][:, c * N:(c + 1) * N], ACT.Exp,
                                         bias=dnb[:, p, c:c + 1], scale=SCALE,
                                         accum_out=dsum[:, p, c:c + 1]).then_inc(d_p, 1)

            weights(0, 0)

            def dispatch(j, p, has):
                t = 2 * j + p
                if has(1):
                    weights(*later(j, p, 1))
                if has(0):
                    act.wait_ge(d_tps, t + 1)
                    wait(act, d_zps, t - 1)
                    nc.scalar.activation(dPT[:, p, :, :].rearrange("p h s -> p (h s)"), bank[2 + p][:, :],
                                         ACT.Copy).then_inc(d_pT, 1)

            steps(act, dispatch, 4, 2, 0, B)

            def silus(g):
                for k, buf in ((0, eu_in), (1, eg_in)):
                    act.wait_ge(e_in, 2 * g + k + 1)
                    nc.scalar.activation(buf[:, g % 2, :], buf[:, g % 2, :], ACT.Silu).then_inc(e_act, 1)

            for g in range(GROUPS + 1):
                if g < GROUPS:
                    silus(g)
                if g >= 1:
                    act.wait_ge(e_tr, g)
                    wait(act, e_y, g - 2)
                    nc.scalar.activation(eugT[:, (g - 1) % 2, :], bank[6 + (g - 1) % 2][:, :],
                                         ACT.Copy).then_inc(e_ugT, 1)

            def q_out(j, p):
                t = 2 * j + p
                act.wait_ge(c_qps, t + 1)
                wait(act, c_sps, t - 1)
                nc.scalar.activation(cqT[:, p, :], bank[0][:, 0:N], ACT.Identity, bias=slot("c_bq")).then_inc(c_q, 1)

            q_out(0, 0)

            def combine(j, p, has):
                t = 2 * j + p
                if has(0):
                    act.wait_ge(c_vops, t + 1)
                    wait(act, c_ops, t - 1)
                    nc.scalar.activation(vo[:, p, :, :].rearrange("p c d -> p (c d)"), bank[1][:, 0:2 * D],
                                         ACT.Copy).then_inc(c_vo, 1)
                if has(1):
                    q_out(*later(j, p, 1))
                if has(0):
                    act.wait_ge(c_sub, t + 1)
                    wait(act, c_p, t - 1)
                    nc.scalar.activation(ce[:, p, :, :].rearrange("p h s -> p (h s)"),
                                         cs[:, p, :, :].rearrange("p h s -> p (h s)"), ACT.Exp,
                                         scale=SCALE).then_inc(c_exp, 1)
                if has(-1):
                    _, pb = later(j, p, -1)
                    act.wait_ge(c_tps, t)
                    wait(act, c_ops, t - 2)
                    nc.scalar.activation(cPT[:, pb, :, :].rearrange("p c n -> p (c n)"), bank[4 + pb][:, :],
                                         ACT.Copy).then_inc(c_pT, 1)

            steps(act, combine, 4, 2, 0, B + 1)

        @block.gpsimd
        def _(pool):
            tt = nc.gpsimd.tensor_tensor
            nc.gpsimd.memset(ones_bf[:, :], 1.0).then_inc(s_ones, 1)
            nc.gpsimd.memset(plus_half[:, :], 0.5).then_inc(s_half, 1)
            nc.gpsimd.memset(minus_half[:, :], -0.5).then_inc(s_half, 1)
            nc.gpsimd.memset(eh[:, :, :], 0.0).then_inc(e_zero, 1)
            nc.gpsimd.memset(ones_f[:, :], 1.0).then_inc(e_zero, 1)
            pool.wait_ge(s_half, 2)
            for layer in range(4):
                pool.wait_ge(s_pms, layer + 1)
                tt(prms[:, 1, :], prms[:, 0, :], plus_half[:, :], ALU.pow).then_inc(s_prms, 1)

            def sums(j, p):
                t = 2 * j + p
                pool.wait_ge(s_v, 2 * t + 2)
                wait(pool, s_fwd, 2 * (t - 2) + 1)
                tt(vs_sb[:, p, :], v_sb[:, 0, :], v_sb[:, 1, :], ALU.add).then_inc(s_sum, 1)

            sums(0, 0)

            def step(j, p, has):
                t = 2 * j + p
                if has(-1):
                    _, pb = later(j, p, -1)
                    pool.wait_ge(s_y, 2 * t)
                    pool.wait_ge(s_u, t)
                    wait(pool, s_ops, t - 1)
                    tt(g_sb[:, :, :, :].rearrange("p c h n -> p c (h n)"),
                       y_sb[:, :, :, :].rearrange("p c h n -> p c (h n)"), u_sb[:, pb, :, :],
                       ALU.mult).then_inc(s_g, 1)
                if has(0):
                    wait(pool, s_inv, t)
                    pool.wait_ge(s_prod, 4 * t + 3)
                    tt(Y_r[:, :, :], rr[:, :, :], ii[:, :, :], ALU.subtract).then_inc(s_Y, 1)
                    pool.wait_ge(s_prod, 4 * t + 4)
                    tt(Y_i[:, :, :], ri[:, :, :], ir[:, :, :], ALU.add).then_inc(s_Y, 1)
                if has(1):
                    sums(*later(j, p, 1))
                if has(-1):
                    pool.wait_ge(s_ve, t)
                    tt(rstd_sb[:, :], ve_sb[:, :], minus_half[:, :], ALU.pow).then_inc(s_rstd, 1)

            steps(pool, step, 4, 2, 0, B + 1)

            pool.wait_ge(e_ve, 1)
            tt(erstd[:, :], eve[:, :], minus_half[:, :], ALU.pow).then_inc(e_rstd, 1)
            mask = const("headmask").rearrange("p (h s) -> p h s", h=H)
            pool.wait_ge(e_chain, 13)

            def blocks(j, p):
                t = 2 * j + p
                wait(pool, c_sps, t - 1)
                tt(kb[:, p, :, :], ckT[:, bass.ds(t, 1), :].to_broadcast([P, H, S]), mask, ALU.mult).then_inc(c_blk, 1)
                wait(pool, c_vops, t - 1)
                tt(vb[:, p, :, :], cvT[:, bass.ds(t, 1), :].to_broadcast([P, H, S]), mask, ALU.mult).then_inc(c_blk, 1)

            blocks(0, 0)

            def combine(j, p, has):
                t = 2 * j + p
                if has(1):
                    blocks(*later(j, p, 1))
                if has(-2):
                    pool.wait_ge(c_ve, t - 1)
                    tt(rstd_sb[:, :], ve_sb[:, :], minus_half[:, :], ALU.pow).then_inc(c_rstd, 1)
                if has(0):
                    pool.wait_ge(c_rec, t + 1)
                    wait(pool, c_tps, t - 1)
                    tt(cp[:, p, :, :].rearrange("p h (g s) -> p (h g) s", s=S), ce[:, p, :, :],
                       crec[:, p, :].unsqueeze(2).to_broadcast([P, 2 * H, S]), ALU.mult).then_inc(c_p, 1)

            steps(pool, combine, 4, 2, 0, B + 2)

        @block.vector
        def _(dve):
            tt = nc.vector.tensor_tensor
            ts = nc.vector.tensor_scalar
            stt = nc.vector.scalar_tensor_tensor
            copy = nc.vector.tensor_copy

            nc.vector.memset(row_parts[:, :], 0.0).then_inc(s_rowstep, 1)
            nc.vector.memset(pactT[R:R + 1, :, :], 1.0).then_inc(s_rowstep, 1)
            dve.wait_ge(l_rows, 16)
            dve.wait_ge(l_pos, 16)
            copy(row_hi[:, :], rows_sb[:, :]).then_inc(s_rowstep, 1)
            dve.wait_ge(s_rowstep, 3)
            tt(row_res, rows_sb[:, :], row_hi[:, :], ALU.subtract).then_inc(s_rowstep, 1)
            dve.wait_ge(s_rowstep, 4)
            copy(row_mid[:, :], row_res).then_inc(s_rowstep, 1)
            dve.wait_ge(s_rowstep, 5)
            tt(row_res2, row_res, row_mid[:, :], ALU.subtract).then_inc(s_rowstep, 1)
            dve.wait_ge(s_rowstep, 6)
            copy(row_lo[:, :], row_res2).then_inc(s_rowstep, 1)
            part = pos("part")[0:3, :]
            ts(row_sum, row_hi[:, :], part[:, 0:1], None, ALU.mult).then_inc(s_rowstep, 1)
            dve.wait_ge(s_rowstep, 8)
            stt(row_sum2, row_mid[:, :], part[:, 1:2], row_sum, ALU.mult,
                ALU.add).then_inc(s_rowstep, 1)
            dve.wait_ge(s_rowstep, 9)
            stt(row_parts[0:3, :], row_lo[:, :], part[:, 2:3], row_sum2, ALU.mult, ALU.add).then_inc(s_rows, 1)

            chain = [0]

            def link(ins):
                chain[0] += 1
                ins.then_inc(s_pchain, 1)
                dve.wait_ge(s_pchain, chain[0])

            for c in range(2):
                first = stt(ph[:, c, :], pos("pos_w"), pos("index")[:, c:c + 1], pos("pos_b"), ALU.mult, ALU.add)
                if c == 1:
                    link(first)
            for layer in range(4):
                link(tt(psq[:, :, :], ph[:, :, :], ph[:, :, :], ALU.mult))
                link(nc.vector.tensor_reduce(pss[:, :], psq[:, :, :], AX.X, ALU.add))
                ts(prms[:, 0, :], pss[:, :], 1.0 / R, None, ALU.mult).then_inc(s_pms, 1)
                dve.wait_ge(s_prms, layer + 1)
                link(ts(prms[:, 2, :], prms[:, 1, :], RMS_EPS, None, ALU.add))
                link(nc.vector.reciprocal(pss[:, :], prms[:, 2, :]))
                wait(dve, s_ptr, 2 * layer)
                for c in range(2):
                    last = ts(pact[:, c, :], ph[:, c, :], pss[:, c:c + 1], 0.0, ALU.mult, ALU.max)
                last.then_inc(s_pact, 1)
                dve.wait_ge(s_ptr, 2 * layer + 2)
                wait(dve, s_plin, 2 * layer)
                copy(pactT[0:R, :, :].rearrange("p c n -> p (c n)"), bank[7][0:R, 0:2 * P]).then_inc(s_pactT, 1)
                if layer == 1:
                    dve.wait_ge(s_dq, 1)
                    link(ts(dqT[:, :], bank[4][:, 0:S], slot("d_bq"), None, ALU.add))
                    tt(dq_blocks[:, :, :], dqT[:, :].unsqueeze(1).to_broadcast([P, H, S]),
                       const("headmask").rearrange("p (h s) -> p h s", h=H), ALU.mult).then_inc(s_dqb, 1)
                if layer == 2:
                    dve.wait_ge(s_dA, 1)
                    copy(dA[:, :], bank[4][:, 0:HS])
                    copy(dc[:, :], bank[4][:, HS:HS + 2]).then_inc(s_prep, 1)
                dve.wait_ge(s_plin, 2 * layer + 2)
                for c in range(2):
                    if layer < 3:
                        last = copy(ph[:, c, :], bank[5 + c][:, 0:R])
                        if c == 1:
                            link(last)
                    else:
                        ts(coef[:, c, :], bank[5 + c][:, 0:CH], pos("decay")[:, c:c + 1], None,
                           ALU.mult).then_inc(s_coef, 1)
            dve.wait_ge(s_prep, 1)
            ts(dcs[:, :], dc[:, :], SCALE, None, ALU.mult)
            ts(slot_b[:, :], slot("slotT"), slot("d_bo"), None, ALU.add)
            for part in range(2):
                for q in range(NQ):
                    dve.wait_ge(s_Aps, 2 * part + q + 1)
                    copy((A_r, A_i)[part][:, q, :], bank[4 + 2 * part + q][:, 0:CH]).then_inc(s_A, 1)
            dve.wait_ge(s_A, 4)

            def statistics(src, n, s_src, s_stats, s_mean, s_eps):
                dve.wait_ge(s_src, n + 1)
                for h in range(2):
                    last = nc.vector.bn_stats(st_sb[:, h, :], src[:, h, :])
                last.then_inc(s_stats, 1)
                dve.wait_ge(s_stats, n + 1)
                dve.sem_inc(s_seen, 1)
                for h in range(2):
                    last = nc.vector.bn_aggr(mv_sb[:, h, :], st_sb[:, h, :])
                last.then_inc(s_mean, 1)
                dve.wait_ge(s_mean, n + 1)
                ts(ve_sb[:, :], mv_sb[:, :, 1], LN_EPS, None, ALU.add).then_inc(s_eps, 1)

            def normalise(src, dst, n, s_inverse, s_dst):
                dve.wait_ge(s_inverse, n + 1)
                for h in range(2):
                    last = ts(dst[:, h, :], src[:, h, :], mv_sb[:, h, 0:1], rstd_sb[:, h:h + 1], ALU.subtract,
                              ALU.mult)
                last.then_inc(s_dst, 1)

            def difference(j, p):
                t = 2 * j + p
                dve.wait_ge(s_v, 2 * t + 2)
                wait(dve, s_fwd, 2 * (t - 1))
                tt(vd_sb[:, p, :], v_sb[:, 0, :], v_sb[:, 1, :], ALU.subtract).then_inc(s_diff, 1)

            difference(0, 0)

            def unfold(t):
                dve.wait_ge(s_odd, t)
                wait(dve, s_g, t - 1)
                even = bank[2][:, 0:CH].rearrange("p (c n) -> p c n", c=NC)
                tt(y_sb[:, :, 0, :], even, odd_sb[:, :, :], ALU.add).then_inc(s_y, 1)
                tt(y_sb[:, :, 1, :], even, odd_sb[:, :, :], ALU.subtract).then_inc(s_y, 1)

            def step(j, p, has):
                t = 2 * j + p
                if has(-2):
                    ja, pa = later(j, p, -2)
                    wait(dve, st_x1[pa], 16 * ja)
                    wait(dve, s_xtps, t - 3)
                    normalise(res_sb, x1_sb[:, pa, :, :], t - 2, s_rstd, s_x1)
                if has(-1):
                    unfold(t)
                if has(0):
                    wait(dve, s_Y, 2 * t)
                    for n, (o, b, a) in enumerate(((rr, 4, A_r), (ir, 4, A_i), (ii, 6, A_i), (ri, 6, A_r))):
                        dve.wait_ge(s_fwd, 2 * t + 1 + n // 2)
                        for q in range(NQ):
                            last = tt(o[:, q, :], bank[b + q][:, 0:CH], a[:, q, :], ALU.mult)
                        last.then_inc(s_prod, 1)
                if has(1):
                    difference(*later(j, p, 1))
                if has(-1):
                    jb, pb = later(j, p, -1)
                    dve.wait_ge(l_x[pb], 16 * (jb + 1))
                    wait(dve, s_x1, t - 1)
                    dve.wait_ge(s_ops, t)
                    tt(res_sb[:, :, :].rearrange("p h d -> p (h d)"), bank[0][:, 0:2 * D],
                       x_sb[:, pb, :], ALU.add).then_inc(s_res, 1)
                    statistics(res_sb, t - 1, s_res, s_bn, s_mv, s_ve)

            steps(dve, step, 4, 2, 0, B + 2)

            def bias(j, p):
                t = 2 * j + p
                dve.wait_ge(d_sps, t + 1)
                wait(dve, d_p, 2 * (t - 1))
                nc.vector.tensor_reduce(dmax[:, p, :], bank[p][:, :].rearrange("p (c n) -> p c n", c=2), AX.X,
                                        ALU.max).then_inc(d_max, 1)
                dve.wait_ge(d_max, t + 1)
                tt(dmc[:, p, :], dmax[:, p, :], dc[:, :], ALU.add).then_inc(d_mc, 1)
                dve.wait_ge(d_mc, t + 1)
                stt(dnb[:, p, :], dmc[:, p, :], -SCALE, dcs[:, :], ALU.mult, ALU.add).then_inc(d_nb, 1)

            bias(0, 0)
            bias(0, 1)

            def dispatch(j, p, has):
                t = 2 * j + p
                if has(0):
                    dve.wait_ge(d_p, 2 * t + 2)
                    wait(dve, d_z, 2 * (t - 1))
                    nc.vector.reciprocal(drec[:, p, :], dsum[:, p, :]).then_inc(d_rec, 1)
                if has(2):
                    bias(*later(j, p, 2))
                if has(-1):
                    _, pb = later(j, p, -1)
                    dve.wait_ge(d_rec, t)
                    dve.wait_ge(d_zps, t)
                    wait(dve, d_ops, t - 2)
                    for c in range(2):
                        stt(dZ[:, pb, c, :], bank[4 + pb][:, c * D:(c + 1) * D], drec[:, pb, c:c + 1],
                            const("diagmask")[:, c * D:(c + 1) * D], ALU.mult, ALU.mult).then_inc(d_z, 1)
                if has(-2):
                    ja, pa = later(j, p, -2)
                    dve.wait_ge(d_ops, t - 1)
                    ts(dOT[:, bass.ds(2 * ja + pa, 1), :].rearrange("p a s -> p (a s)"), bank[6 + pa][:, 0:S],
                       slot("d_bv"), None, ALU.add).then_inc(d_o, 1)

            steps(dve, dispatch, 4, 2, 0, B + 2)

            def bcast(ap):
                return ap.unsqueeze(2).to_broadcast([P, ap.shape[1], B])

            en = [0]

            def elink(ins):
                en[0] += 1
                ins.then_inc(e_chain, 1)
                dve.wait_ge(e_chain, en[0])

            def grid(ap):
                return ap.rearrange("p (s b) -> p s b", b=B)

            dve.wait_ge(e_pe, 1)
            elink(copy(eh1[:, :, :], grid(bank[0][:, 0:S * B])))
            elink(tt(eo[:, :, :], eh1[:, :, :], bcast(slot_b[:, :]), ALU.add))
            dve.wait_ge(e_pe, 2)
            elink(tt(ecen[:, :, :], eo[:, :, :], grid(bank[1][:, 0:S * B]), ALU.subtract))
            elink(tt(esq[:, :, :], ecen[:, :, :], ecen[:, :, :], ALU.mult))
            dve.wait_ge(e_pe, 3)
            ts(eve[:, :], bank[1][:, 0:2], LN_EPS, None, ALU.add).then_inc(e_ve, 1)
            dve.wait_ge(e_rstd, 1)
            elink(tt(ediag[:, :, :], ident.unsqueeze(1).to_broadcast([P, 2, P]),
                     erstd[:, :].unsqueeze(2).to_broadcast([P, 2, P]), ALU.mult))
            dve.wait_ge(e_pe, 4)
            elink(tt(eh1[:, :, :], ecen[:, :, :], grid(bank[1][:, 0:S * B]), ALU.mult))
            elink(tt(eh2[:, :, :], eh1[:, :, :], bcast(slot("ln_gT")), ALU.mult))
            dve.wait_ge(e_zero, 1)
            elink(tt(eh[:, :, 0:B], eh2[:, :, :], bcast(slot("ln_bT")), ALU.add))

            def biased(g):
                for k, buf, bias in ((2, eu_in, eb1), (4, eg_in, ebg)):
                    dve.wait_ge(e_up, 2 * g + k // 2)
                    wait(dve, e_ug, g - 1)
                    tt(buf[:, g % 2, :], bank[k + g % 2][:, :], bias[:, g, :], ALU.add).then_inc(e_in, 1)

            def products(g):
                dve.wait_ge(e_act, 2 * g + 2)
                wait(dve, e_tr, g - 1)
                tt(eug[:, g % 2, :], eu_in[:, g % 2, :], eg_in[:, g % 2, :], ALU.mult).then_inc(e_ug, 1)

            for k in range(2):
                dve.wait_ge(l_bias[k], 16)
            for g in range(GROUPS + 1):
                if g < GROUPS:
                    biased(g)
                if g >= 1:
                    products(g - 1)
            dve.wait_ge(e_y, GROUPS)
            elink(copy(eyr.rearrange("p g d -> p (g d)"), bank[0][:, :]))
            dve.wait_ge(e_pe, 5)
            rows_of = bank[1][:, :].rearrange("p (s r) -> p s r", r=ROW)[:, :, 0:B]
            elink(tt(ey[:, :, :], eo[:, :, :], rows_of, ALU.add))
            elink(tt(eo2[:, :, :], ey[:, :, :], bcast(slot("b2T")), ALU.add))
            dve.wait_ge(e_pe, 6)
            elink(ts(ckT[:, :, :].rearrange("p b s -> p (b s)"), bank[0][:, 0:S * B], slot("c_bk"), None, ALU.add))
            elink(ts(cvT[:, :, :].rearrange("p b s -> p (b s)"), bank[0][:, S * B:2 * S * B], slot("c_bv"), None,
                     ALU.add))

            def combine(j, p, has):
                t = 2 * j + p
                if has(0):
                    dve.wait_ge(c_sps, t + 1)
                    s = bank[2 + p][:, :].rearrange("p (h s) -> p h s", s=S)
                    nc.vector.tensor_reduce(cmax[:, p, :], s, AX.X, ALU.max).then_inc(c_max, 1)
                    dve.wait_ge(c_max, t + 1)
                    wait(dve, c_exp, t - 1)
                    tt(cs[:, p, :, :], s, cmax[:, p, :].unsqueeze(2).to_broadcast([P, 2 * H, S]),
                       ALU.subtract).then_inc(c_sub, 1)
                if has(-2):
                    ja, pa = later(j, p, -2)
                    dve.wait_ge(c_ops, t - 1)
                    dve.wait_ge(l_x1[pa], 16 * (ja + 1))
                    wait(dve, c_y, t - 2)
                    tt(cres[:, :, :].rearrange("p h d -> p (h d)"), bank[6 + pa][:, 0:2 * D],
                       x1_in[:, pa, :], ALU.add).then_inc(c_res, 1)
                    wait(dve, st_out[pa], 16 * ja)
                    statistics(cres, t - 2, c_res, c_bn, c_mv, c_ve)
                if has(0):
                    dve.wait_ge(c_exp, t + 1)
                    wait(dve, c_p, t - 1)
                    nc.vector.tensor_reduce(csum[:, p, :], ce[:, p, :, :], AX.X, ALU.add).then_inc(c_sum, 1)
                    dve.wait_ge(c_sum, t + 1)
                    nc.vector.reciprocal(crec[:, p, :], csum[:, p, :]).then_inc(c_rec, 1)
                if has(-2):
                    _, pa = later(j, p, -2)
                    normalise(cres, y_out[:, pa, :, :], t - 2, c_rstd, c_y)

            steps(dve, combine, 4, 2, 0, B + 2)


def constants():
    theta = np.pi * (2 * np.arange(NF) + 1) / (2 * NF)
    centre = np.arange(P) - (N - 1) / 2
    t = np.arange(N)
    dft_f = np.stack([np.cos(np.outer(centre, theta)), -np.sin(np.outer(centre, theta))], 1)
    dft_t = np.stack([np.cos(np.outer(t, theta)), -np.sin(np.outer(t, theta))], 1).reshape(2, P, 2, NF)
    dft_i = np.stack([np.cos(np.outer(theta, centre)), -np.sin(np.outer(theta, centre))], 1) / NF
    row = np.arange(P)
    of_head = (row[:, None] // DH == np.arange(H)[None, :])
    headmask = np.repeat(of_head[:, :, None], S, 2).reshape(P, HS)
    diag = np.stack([(c * (P // S) + row[:, None] // S) == (np.arange(D)[None, :] // DH) for c in range(2)], 1)
    pick = (row[:, None] % S) == np.arange(S)[None, :]
    const = np.concatenate([np.eye(P), np.full((P, P), 1.0 / D), headmask, diag.reshape(P, 2 * D), pick], 1)
    decay = np.float32(0.99) ** t.astype(np.float32)
    f = lambda a: np.ascontiguousarray(a, dtype=np.float32)
    return dict(dft_f=f(dft_f), dft_t=f(dft_t.transpose(1, 0, 2, 3)),
                dft_i=f(dft_i.reshape(NQ, P, 2, P).transpose(1, 0, 2, 3)), const=f(const),
                index=f(t.reshape(2, P).T), decay=f(decay.reshape(2, P).T), part=f(row[:, None] == np.arange(3)))


def kernel(**inputs):
    import concourse.bacc as bacc
    from concourse.bass_utils import run_bass_kernel_spmd

    a = {k.removeprefix("L0_"): np.asarray(v) for k, v in inputs.items()}
    cat = lambda *parts: np.ascontiguousarray(np.concatenate(parts, 1))
    col = lambda v: v.reshape(-1, P).T
    c = constants()
    x = np.stack([a["attn_x"][:, :P], a["attn_x"][:, P:][:, ::-1]], 1)
    arrays = {
        "xT": x.transpose(0, 3, 1, 2).reshape(B, D, N),
        "x": x.transpose(0, 2, 1, 3).reshape(B, P, N),
        "v_w": a["attn_v_w"],
        "w_main": cat(a["attn_u_w"], a["attn_o_w"].reshape(NC, P, D).transpose(1, 0, 2).reshape(P, NC * D),
                      col(a["attn_u_b"])),
        "w_slot": cat(a["ffn_d_Wq"], a["ffn_d_Wk"].T, a["ffn_d_Wv"], a["ffn_d_Wo"], a["ffn_c_Wq"], a["ffn_c_Wk"],
                      a["ffn_c_Wv"], a["ffn_c_Wo"], a["ffn_slot_query"][0].T, col(a["ffn_d_bq"]), col(a["ffn_d_bk"]),
                      col(a["ffn_d_bv"]), col(a["ffn_d_bo"]), col(a["ffn_c_bq"]), col(a["ffn_c_bk"]),
                      col(a["ffn_c_bv"]), a["ffn_e_ln_g"].T, a["ffn_e_ln_b"].T, a["ffn_e_b2"].T),
        "w_const": c["const"],
        "w_pos": cat(np.broadcast_to(a["attn_pos_w"], (P, R)), np.broadcast_to(a["attn_pos_b"][None], (P, R)),
                     c["index"], c["decay"], c["part"]),
        "w_lin": np.concatenate([cat(a["attn_lw0"], a["attn_lw1"], a["attn_lw2"], a["attn_out_w"]),
                                 cat(a["attn_lb0"][None], a["attn_lb1"][None], a["attn_lb2"][None],
                                     a["attn_out_b"][None])], 0),
        "rows": np.broadcast_to(cat(a["attn_v_b"][None], a["attn_o_b"][None], a["ffn_c_bo"][None]), (3, ROWS)),
        "dft_t": c["dft_t"], "dft_f": c["dft_f"], "dft_i": c["dft_i"],
        "experts": np.concatenate([a["ffn_e_W1"], a["ffn_e_Wg"],
                                   a["ffn_e_W2"].reshape(H, NFC, P, D).transpose(0, 2, 1, 3).reshape(H, P, FF)], 2),
        "bias_1": np.broadcast_to(a["ffn_e_b1"].reshape(GROUPS, EG, 1, FF).transpose(1, 2, 0, 3),
                                  (EG, ROW, GROUPS, FF)).reshape(P, GROUPS, FF),
        "bias_g": np.broadcast_to(a["ffn_e_bg"].reshape(GROUPS, EG, 1, FF).transpose(1, 2, 0, 3),
                                  (EG, ROW, GROUPS, FF)).reshape(P, GROUPS, FF),
    }
    arrays = {k: np.ascontiguousarray(v) for k, v in arrays.items()}
    nc = bacc.Bacc("TRN2", target_bir_lowering=False, num_devices=1)
    args = [nc.dram_tensor(k, v.shape, F32, kind="ExternalInput").ap() for k, v in arrays.items()]
    args.append(nc.dram_tensor("out", (B, P, N), F32, kind="ExternalOutput").ap())
    build(nc, *args)
    r = run_bass_kernel_spmd(nc, [arrays], core_ids=[0]).results[0]["out"]
    y = r.reshape(B, P, 2, D).transpose(0, 2, 1, 3)
    return np.ascontiguousarray(np.concatenate([y[:, 0], y[:, 1, ::-1]], 1))
```

```python
from contextlib import ExitStack
from itertools import islice

import numpy as np

import concourse.bass as bass
from concourse import mybir

F32 = mybir.dt.float32
BF16 = mybir.dt.bfloat16
F32R = mybir.dt.float32r
ALU = mybir.AluOpType
ACT = mybir.ActivationFunctionType
AX = mybir.AxisListType

P = 128
B = 16
N = 256
D = 128
CH = 384
NC = CH // P
R = 64
NF = 256
NQ = NF // P
H = 16
DH = D // H
S = 16
HS = H * S
FF = 512
NFC = FF // P
ROW = 32
EG = P // ROW
GROUPS = H // EG
LN_EPS = 1e-5
RMS_EPS = 1e-8
SCALE = float(1.0 / np.sqrt(DH))
SHARED = 10752
PAIRS = B // 2

ROW_V, ROW_O, ROW_C = 0, CH, CH + D
ROWS = CH + 2 * D
W_MAIN = {"o_w": NC * D, "u_b": NC}
W_SLOT = {"d_Wq": D, "d_WkT": D, "d_Wv": D, "d_Wo": D, "c_Wq": D, "c_Wk": D, "c_Wv": D, "c_Wo": D,
          "slotT": S, "d_bq": 1, "d_bk": 1, "d_bv": 1, "d_bo": 1, "c_bq": 1, "c_bk": 1, "c_bv": 1,
          "ln_gT": S, "ln_bT": S, "b2T": S}
W_CONST = {"ident": P, "mean": P, "headmask": HS, "diagmask": 2 * D, "pick": S}
W_POS = {"pos_w": R, "pos_b": R, "index": 2, "decay": 2, "lin_b": 3 * R, "out_b": CH, "rows": ROWS // P}

def columns(widths):
    at, out = 0, {}
    for name, width in widths.items():
        out[name] = slice(at, at + width)
        at += width
    return out, at

def later(j, p, k):
    return j + (p + k) // 2, (p + k) % 2

def build(nc, xT, x, w_vu, w_main, w_slot, w_const, w_pos, w_lin, dft_t, dft_f, dft_i, experts, bias_1, bias_g, out):
    ctx = ExitStack()
    main_at, main_n = columns(W_MAIN)
    slot_at, slot_n = columns(W_SLOT)
    const_at, const_n = columns(W_CONST)
    pos_at, pos_n = columns(W_POS)
    with ctx:
        def sb(name, shape, dt=F32):
            return ctx.enter_context(nc.sbuf_tensor(name, shape, dt))

        def sem(name):
            return ctx.enter_context(nc.semaphore(name))

        shared = sb("shared", [P, SHARED])
        top = [0]

        def phase():
            top[0] = 0

        def part_of(shape):
            n = int(np.prod(shape))
            v = shared[:, top[0]:top[0] + n]
            top[0] += n
            assert top[0] <= SHARED
            if len(shape) == 1:
                return v
            names = "abcd"[:len(shape)]
            return v.rearrange(f"p ({' '.join(names)}) -> p {' '.join(names)}",
                               **dict(zip(names[1:], shape[1:])))

        vu_hi = sb("vu_hi", [P, 2 * CH], F32R)
        vu_lo = sb("vu_lo", [P, 2 * CH], F32R)
        main_sb = sb("main_sb", [P, main_n])
        slot_sb = sb("slot_sb", [P, slot_n])
        const_sb = sb("const_sb", [P, const_n])
        dft_hi = sb("dft_hi", [P, 2, NF], F32R)
        dft_lo = sb("dft_lo", [P, 2, NF], F32R)
        dft_i_sb = sb("dft_i_sb", [P, NQ, 2, P])
        exp_sb = sb("exp_sb", [P, H, 3 * FF])

        def main(name):
            return main_sb[:, main_at[name]]

        def slot(name):
            return slot_sb[:, slot_at[name]]

        def const(name):
            return const_sb[:, const_at[name]]

        def pos(name):
            return pos_sb[:, pos_at[name]]

        ident = const("ident")
        minus_half = sb("minus_half", [P, 2])
        plus_half = sb("plus_half", [P, 2])
        ve_sb = sb("ve_sb", [P, 2])
        early = sb("early", [P, 1])
        row_split = sb("row_split", [P, 3, ROWS // P], BF16)
        row_res = sb("row_res", [P, 2, ROWS // P])
        row_out = nc.dram_tensor("row_scratch", (3, ROWS), BF16, kind="Internal").ap()
        ones_bf = sb("ones_bf", [P, P], BF16)
        row_parts = sb("row_parts", [P, ROWS], BF16)

        pss = sb("pss", [P, 2])
        prms = sb("prms", [P, 2])
        pss2 = sb("pss2", [P, 2])
        prec = sb("prec", [P, 2])
        prd = sb("prd", [P, 2])
        A_r = sb("A_r", [P, NQ, CH])
        A_i = sb("A_i", [P, NQ, CH])

        phase()
        xT_sb = sb("xT_sb", [P, 2, N])
        vs_hi = sb("vs_hi", [P, CH], F32R)
        vs_lo = sb("vs_lo", [P, CH], F32R)
        vd_hi = sb("vd_hi", [P, CH], F32R)
        vd_lo = sb("vd_lo", [P, CH], F32R)
        x_hi = sb("x_hi", [P, 2, N], F32R)
        x_lo = sb("x_lo", [P, 2, N], F32R)
        x_sb = sb("x_sb", [P, 2, N])
        v_sb = part_of([2, CH])
        vsd_sb = part_of([2, 2, CH])
        vs_sb = vsd_sb[:, :, 0, :]
        vd_sb = vsd_sb[:, :, 1, :]
        u_sb = part_of([2, NC, N])
        rr = part_of([NQ, CH])
        ii = part_of([NQ, CH])
        ri = part_of([NQ, CH])
        ir = part_of([NQ, CH])
        Y_r = part_of([NQ, CH])
        Y_i = part_of([NQ, CH])
        even_sb = part_of([NC, P])
        y_sb = part_of([NC, 2, P])
        g_sb = part_of([NC, 2, P])
        res_sb = sb("res_sb", [P, 2, D])
        st_sb = sb("st_sb", [P, 2, 6])
        mv_sb = sb("mv_sb", [P, 2, 2])
        rstd_sb = sb("rstd_sb", [P, 2])
        x1_sb = sb("x1_sb", [P, 2, 2, D])
        flat_u = u_sb.rearrange("p a c n -> p (a c n)")
        dft_t_sb = flat_u[:, 0:4 * NF].rearrange("p (a b n) -> p a b n", a=2, b=2)
        coef = Y_r
        vu_sb = rr.rearrange("p q c -> p (q c)")
        dft_f_sb = ii.rearrange("p q c -> p (q c)")[:, 0:2 * NF].rearrange("p (a n) -> p a n", a=2)
        flat_even = even_sb.rearrange("p c n -> p (c n)")
        ph, psq, pact = (flat_even[:, k * P:(k + 1) * P].rearrange("p (c r) -> p c r", c=2) for k in range(3))
        pactT = g_sb.rearrange("p c h n -> p (c h n)")[0:R, 0:2 * P].rearrange("p (c n) -> p c n", c=2)
        pos_sb = vsd_sb[:, 1, :, :].rearrange("p a c -> p (a c)")[:, 0:pos_n]
        pbd = Y_i
        lin_sb = y_sb.rearrange("p c h n -> p (c h n)")[0:R, 0:3 * R + CH]
        x1T_all = sb("x1T_all", [P, B, N])
        x1_out = nc.dram_tensor("x1_scratch", (B, P, N), F32, kind="Internal").ap()
        tokens_in = sb("tokens_in", [P, 2, N])
        x1_in = x_sb

        phase()
        dqT = sb("dqT", [P, S])
        dq_blocks = ir.rearrange("p q c -> p (q c)")[:, 0:HS].rearrange("p (h s) -> p h s", h=H)
        dA = sb("dA", [P, HS])
        dc = sb("dc", [P, 2])
        dcs = sb("dcs", [P, 2])
        dmax = sb("dmax", [P, 2, 2])
        dmc = sb("dmc", [P, 2, 2])
        dnb = sb("dnb", [P, 2, 2])
        dP = part_of([2, 2, N])
        dsum = sb("dsum", [P, 2, 2])
        drec = sb("drec", [P, 2, B])
        values_w = sb("values_w", [P, EG, D])
        dPT = part_of([2, 2, HS])
        dZ = part_of([H, B, S])
        rec_pick = part_of([2, B, S])
        drecT = dP[:, 0, 0, :]
        dOT = sb("dOT", [P, B, S])

        phase()
        ecen = part_of([S, B])
        esq = part_of([S, B])
        ediag = part_of([2, P])
        eh1 = part_of([S, B])
        eh2 = part_of([S, B])
        ey = part_of([S, B])
        eo2 = part_of([S, B])
        eu_in = part_of([2, FF])
        eg_in = part_of([2, FF])
        eug = part_of([2, FF])
        eugT = part_of([2, FF])
        eyr = part_of([GROUPS, D])
        top[0] = SHARED - 2 * GROUPS * FF
        eb1 = part_of([GROUPS, FF])
        ebg = part_of([GROUPS, FF])
        eh = A_r.rearrange("p q c -> p (q c)")[:, 0:S * ROW].rearrange("p (s r) -> p s r", r=ROW)
        eo = A_i.rearrange("p q c -> p (q c)")[:, 2 * B * S:3 * B * S].rearrange("p (s b) -> p s b", b=B)
        slot_b = sb("slot_b", [P, S])
        eve = sb("eve", [P, 2])
        erstd = sb("erstd", [P, 2])
        ones_f = sb("ones_f", [P, P])
        ckT, cvT = (A_i.rearrange("p q c -> p (q c)")[:, k * B * S:(k + 1) * B * S].rearrange(
            "p (b s) -> p b s", s=S) for k in range(2))

        phase()
        kb = part_of([2, H, S])
        vb = part_of([2, H, S])
        vo = part_of([2, 2, D])
        top[0] = 7 * S * B
        cqT = part_of([2, N])
        cmax = sb("cmax", [P, 2, 2 * H])
        cs = part_of([2, 2 * H, S])
        ce = part_of([2, 2 * H, S])
        cmv = sb("cmv", [P, 2, 2, 2])
        cve = sb("cve", [P, 2, 2])
        crstd = sb("crstd", [P, 2, 2])
        cnb = sb("cnb", [P, 2, 2])
        csum = sb("csum", [P, 2, 2 * H])
        crec = sb("crec", [P, 2, 2 * H])
        cp = part_of([2, 2, HS])
        cPT = part_of([2, 2, N])
        cres = part_of([2, 2, D])
        y_out = part_of([2, 2, D])

        bank = [ctx.enter_context(nc.psum_tensor(f"bank{i}", [P, 512], F32)) for i in range(8)]

        l_xT = [sem("l_xT0"), sem("l_xT1")]
        s_sumhi, s_sumlo = sem("s_sumhi"), sem("s_sumlo")
        s_dhi, s_dlo, s_dft_hi, s_dft_lo = sem("s_dhi"), sem("s_dlo"), sem("s_dft_hi"), sem("s_dft_lo")
        s_xhi, s_xlo, s_whi, s_wlo = sem("s_xhi"), sem("s_xlo"), sem("s_whi"), sem("s_wlo")
        l_vw, l_pos, l_const, l_rows, l_lin = sem("l_vw"), sem("l_pos"), sem("l_const"), sem("l_rows"), sem("l_lin")
        l_main, l_slot, l_t, l_f, l_i, l_x = (sem("l_main"), sem("l_slot"), sem("l_t"), sem("l_f"), sem("l_i"),
                                             [sem("l_x0"), sem("l_x1")])
        l_tokens = [sem("l_tokens0"), sem("l_tokens1")]
        l_x1 = [sem("l_x10"), sem("l_x11")]
        l_exp = [sem("l_exp0"), sem("l_exp1")]
        st_x1 = [sem("st_x10"), sem("st_x11")]
        st_out = [sem("st_out0"), sem("st_out1")]
        s_ones, s_rows = sem("s_ones"), sem("s_rows")
        s_pchain, s_pact, s_ptr, s_pactT, s_plin = (sem("s_pchain"), sem("s_pact"), sem("s_ptr"), sem("s_pactT"),
                                                    sem("s_plin"))
        s_coef, s_Aps, s_A = sem("s_coef"), sem("s_Aps"), sem("s_A")
        s_zero, st_rows = sem("s_zero"), sem("st_rows")
        s_pms, s_prms, s_half = sem("s_pms"), sem("s_prms"), sem("s_half")
        s_seen = sem("s_seen")
        s_ve, c_ve, e_ve, e_rstd = sem("s_ve"), sem("c_ve"), sem("e_ve"), sem("e_rstd")
        s_dq, s_dqb, s_dA, s_prep = sem("s_dq"), sem("s_dqb"), sem("s_dA"), sem("s_prep")
        s_evenps = sem("s_evenps")
        s_vps, s_v, s_sum, s_diff = sem("s_vps"), sem("s_v"), sem("s_sum"), sem("s_diff")
        s_fwd, s_prod, s_Y = sem("s_fwd"), sem("s_prod"), sem("s_Y")
        s_ups, s_u, s_inv, s_even, s_y, s_g = (sem("s_ups"), sem("s_u"), sem("s_inv"), sem("s_even"), sem("s_y"),
                                              sem("s_g"))
        s_ops, s_res, s_bn, s_mv, s_rstd, s_x1 = (sem("s_ops"), sem("s_res"), sem("s_bn"), sem("s_mv"),
                                                  sem("s_rstd"), sem("s_x1"))
        s_xtps, s_x1T = sem("s_xtps"), sem("s_x1T")
        d_sps, d_max, d_mc, d_nb, d_p, d_tps, d_pT = (sem("d_sps"), sem("d_max"), sem("d_mc"), sem("d_nb"),
                                                      sem("d_p"), sem("d_tps"), sem("d_pT"))
        d_rec, d_zps, d_z, d_ops, d_o = sem("d_rec"), sem("d_zps"), sem("d_z"), sem("d_ops"), sem("d_o")
        d_zero, s_values_w = sem("d_zero"), sem("s_values_w")
        d_pick, d_divps, d_div = sem("d_pick"), sem("d_divps"), sem("d_div")
        e_pe, e_chain, e_in, e_act, e_ug = sem("e_pe"), sem("e_chain"), sem("e_in"), sem("e_act"), sem("e_ug")
        e_up, e_tr, e_ugT, e_y, e_zero = sem("e_up"), sem("e_tr"), sem("e_ugT"), sem("e_y"), sem("e_zero")
        l_bias = [sem("l_bias1"), sem("l_biasg")]
        c_kb, c_vb, c_nb = sem("c_kb"), sem("c_vb"), sem("c_nb")
        c_qps, c_q, c_vops, c_vo = sem("c_qps"), sem("c_q"), sem("c_vops"), sem("c_vo")
        c_sps, c_max, c_sub, c_exp, c_sum, c_rec, c_p = (sem("c_sps"), sem("c_max"), sem("c_sub"), sem("c_exp"),
                                                         sem("c_sum"), sem("c_rec"), sem("c_p"))
        c_tps, c_pT, c_ops, c_res, c_bn, c_mv, c_rstd, c_y = (sem("c_tps"), sem("c_pT"), sem("c_ops"), sem("c_res"),
                                                              sem("c_bn"), sem("c_mv"), sem("c_rstd"), sem("c_y"))

        def wait(eng, semaphore, n):
            if isinstance(n, int) and n <= 0:
                return
            eng.wait_ge(semaphore, n)

        def steps(eng, step, before, after, first, last, between=None):
            def one(t):
                step(t // 2, t % 2, lambda k: 0 <= t + k < B)
            lo = before // 2
            hi = (B - after) // 2
            for t in range(first, 2 * lo):
                one(t)
            with eng.Fori(lo, hi) as j:
                step(j, 0, lambda k: True)
                step(j, 1, lambda k: True)
            for t in range(2 * hi, last):
                one(t)
                if between:
                    between(t)

        block = ctx.enter_context(nc.Block())

        @block.sync
        def _(sp):
            sp.dma_start(pos_sb[:, :], w_pos).then_inc(l_pos, 16)
            sp.dma_start(const_sb[:, :], w_const).then_inc(l_const, 16)
            sp.dma_start(lin_sb[:, :], w_lin).then_inc(l_lin, 16)
            sp.dma_start(xT_sb[:, 0, :], xT[0]).then_inc(l_xT[0], 16)
            sp.dma_start(vu_sb, w_vu).then_inc(l_vw, 16)
            sp.dma_start(xT_sb[:, 1, :], xT[1]).then_inc(l_xT[1], 16)
            sp.dma_start(dft_t_sb[:, :, :, :], dft_t).then_inc(l_t, 16)
            sp.dma_start(slot_sb[:, :], w_slot).then_inc(l_slot, 16)
            sp.wait_ge(s_rows, 1)
            sp.dma_start(row_out.rearrange("a (p k) -> p a k", p=P), row_split[:, :, :]).then_inc(st_rows, 16)
            sp.wait_ge(st_rows, 16)
            sp.wait_ge(s_zero, 1)
            sp.dma_start(row_parts[0:3, :], row_out).then_inc(l_rows, 16)
            sp.dma_start(dft_f_sb[:, :, :], dft_f).then_inc(l_f, 16)
            sp.dma_start(main_sb[:, :], w_main).then_inc(l_main, 16)
            sp.dma_start(dft_i_sb[:, :, :, :], dft_i).then_inc(l_i, 16)

            def step(j, p, has):
                t = 2 * j + p
                jb, pb = later(j, p, -1)
                if has(0):
                    wait(sp, l_exp[p], 16 * j)
                    sp.dma_start(exp_sb[:, bass.ds(t, 1), :].rearrange("p a f -> p (a f)"),
                                 experts[bass.ds(t, 1), :, :].rearrange("a p f -> p (a f)")).then_inc(l_exp[p], 16)
                if has(0):
                    wait(sp, s_res, t - 1)
                    sp.dma_start(x_sb[:, p, :], x[bass.ds(t, 1), :, :].rearrange("a p n -> p (a n)")
                                 ).then_inc(l_x[p], 16)
                if has(2):
                    sp.wait_ge(s_xhi, t + 1)
                    sp.wait_ge(s_xlo, t + 1)
                    sp.dma_start(xT_sb[:, p, :], xT[bass.ds(t + 2, 1), :, :].rearrange("a p n -> p (a n)")
                                 ).then_inc(l_xT[p], 16)
                if has(-2):
                    jb, pb = later(j, p, -2)
                    sp.wait_ge(s_x1, t - 1)
                    sp.dma_start(x1_out[bass.ds(2 * jb + pb, 1), :, :].rearrange("a p n -> p (a n)"),
                                 x1_sb[:, pb, :, :].rearrange("p h d -> p (h d)")).then_inc(st_x1[pb], 16)

            def tokens(j, p, has):
                t = 2 * j + p
                sp.wait_ge(st_x1[p], 16 * (j + 1))
                wait(sp, d_zps, t - 1)
                sp.dma_start(tokens_in[:, p, :], x1_out[bass.ds(t, 1), :, :].rearrange("a p n -> p (a n)")
                             ).then_inc(l_tokens[p], 16)

            def between(t):
                if t == B - 1:
                    tokens(0, 0, None)
                    tokens(0, 1, None)

            steps(sp, step, 4, 2, 0, B + 2, between)
            for p in range(2):
                sp.wait_ge(st_x1[p], 16 * PAIRS)

            def tokens_and_bias(j, p, has):
                tokens(j, p, has)
                sp.dma_start((eb1, ebg)[p][:, bass.ds(j - 2, 1), :], (bias_1, bias_g)[p][:, bass.ds(j - 2, 1), :]
                             ).then_inc(l_bias[p], 16)

            tokens(1, 0, None)
            tokens(1, 1, None)
            steps(sp, tokens_and_bias, 4, B - 4 - 2 * GROUPS, 4, 4 + 2 * GROUPS)
            steps(sp, tokens, 4 + 2 * GROUPS, 0, 4 + 2 * GROUPS, B)

            def residuals(j, p, has):
                t = 2 * j + p
                if has(-4):
                    sp.wait_ge(c_y, t - 3)
                    sp.dma_start(out[bass.ds(t - 4, 1), :, :].rearrange("a p n -> p (a n)"),
                                 y_out[:, p, :, :].rearrange("p h d -> p (h d)")).then_inc(st_out[p], 16)
                if has(0):
                    wait(sp, c_res, t - 1)
                    sp.dma_start(x1_in[:, p, :], x1_out[bass.ds(t, 1), :, :].rearrange("a p n -> p (a n)")
                                 ).then_inc(l_x1[p], 16)
            steps(sp, residuals, 6, 0, 0, B + 4)
            for p in range(2):
                sp.wait_ge(st_out[p], 16 * PAIRS)

        @block.tensor
        def _(pe):
            mm = nc.tensor.matmul

            def project_v(j, p, before):
                for h in range(2):
                    if h == 1:
                        wait(pe, s_x1T, before)
                    tile = slice(h * P, (h + 1) * P)
                    mm(bank[h][:, 0:CH], x_hi[:, p, tile], vu_hi[:, 0:CH], start=True, stop=False)
                    mm(bank[h][:, 0:CH], x_hi[:, p, tile], vu_lo[:, 0:CH], start=False, stop=False)
                    mm(bank[h][:, 0:CH], x_lo[:, p, tile], vu_hi[:, 0:CH], start=False, stop=False)
                    mm(bank[h][:, 0:CH], ones_bf[:, :], row_parts[:, ROW_V:ROW_V + CH],
                       start=False, stop=True).then_inc(s_vps, 1)

            def keep_warm(n):
                for _ in range(n):
                    mm(bank[7][:, 256:512], ones_bf[:, :], row_parts[:, 0:256], start=True, stop=True)

            pieces = iter([(h, c) for h in range(2) for c in range(NC)] + [None])

            def first_v(n):
                for piece in islice(pieces, n):
                    if piece is None:
                        pe.wait_ge(l_rows, 16)
                        pe.wait_ge(s_ones, 1)
                        for h in range(2):
                            mm(bank[h][:, 0:CH], ones_bf[:, :], row_parts[:, ROW_V:ROW_V + CH],
                               start=False, stop=True).then_inc(s_vps, 1)
                        continue
                    h, c = piece
                    if piece == (0, 0):
                        pe.wait_ge(l_xT[0], 16)
                        pe.wait_ge(l_vw, 16)
                    mm(bank[h][:, c * P:(c + 1) * P], xT_sb[:, 0, h * P:(h + 1) * P], vu_sb[:, c * P:(c + 1) * P],
                       start=(c == 0), stop=False)

            pe.wait_ge(l_const, 16)
            pe.wait_ge(l_lin, 16)
            for layer in range(4):
                pe.wait_ge(s_pact, layer + 1)
                for c in range(2):
                    nc.tensor.transpose(bank[7][0:R, c * P:(c + 1) * P], pact[:, c, :], ident).then_inc(s_ptr, 1)
                if layer >= 1:
                    first_v(1)
                pe.wait_ge(s_pactT, layer + 1)
                w = lin_sb[:, layer * R:(layer + 1) * R] if layer < 3 else lin_sb[:, 3 * R:3 * R + CH]
                for c in range(2):
                    o = bank[5 + c][:, 0:R] if layer < 3 else bank[5 + c][:, 0:CH]
                    mm(o, pactT[:, c, :], w, start=True, stop=True).then_inc(s_plin, 1)
                if layer >= 1:
                    first_v(2)
            pe.wait_ge(l_slot, 16)
            mm(bank[4][:, 0:S], slot("d_Wq"), slot("slotT"), start=True, stop=True).then_inc(s_dq, 1)
            pe.wait_ge(s_coef, 1)
            pe.wait_ge(l_t, 16)
            pe.wait_ge(s_v, 2)
            for part in range(2):
                for q in range(NQ):
                    o = bank[2 * part + q][:, 0:CH]
                    mm(o, dft_t_sb[:, 0, part, q * P:(q + 1) * P], coef[:, 0, :], start=True, stop=False)
                    if part == 0 and q == 0:
                        pe.wait_ge(s_coef, 2)
                    mm(o, dft_t_sb[:, 1, part, q * P:(q + 1) * P], coef[:, 1, :], start=False,
                       stop=True).then_inc(s_Aps, 1)
                    if part == 0 and q == 0:
                        pe.wait_ge(s_dqb, 1)
                        blocks = dq_blocks[:, :, :].rearrange("p h s -> p (h s)")
                        mm(bank[4][:, 0:HS], slot("d_WkT"), blocks, start=True, stop=True)
                        for c in range(2):
                            last = mm(bank[4][:, HS + c:HS + c + 1], blocks[:, c * P:(c + 1) * P], slot("d_bk"),
                                      start=True, stop=True)
                        last.then_inc(s_dA, 1)

            def forward(part, b, hi, lo, s_lo, n):
                for w in (dft_hi, dft_lo):
                    for q in range(NQ):
                        mm(bank[b + q][:, 0:CH], w[:, part, q * P:(q + 1) * P], hi[:, :], start=(w is dft_hi),
                           stop=False)
                pe.wait_ge(s_lo, n)
                for q in range(NQ):
                    final = mm(bank[b + q][:, 0:CH], dft_hi[:, part, q * P:(q + 1) * P], lo[:, :], start=False,
                               stop=True)
                final.then_inc(s_fwd, 1)

            def step(j, p, has):
                t = 2 * j + p
                if has(0):
                    if isinstance(t, int) and t == 0:
                        pe.wait_ge(s_prep, 1)
                        pe.wait_ge(s_dft_hi, 1)
                        pe.wait_ge(s_dft_lo, 1)
                    else:
                        pe.wait_ge(s_prod, 4 * t)
                    pe.wait_ge(s_dhi, t + 1)
                    forward(1, 6, vd_hi, vd_lo, s_dlo, t + 1)
                    pe.wait_ge(s_sumhi, t + 1)
                    forward(0, 4, vs_hi, vs_lo, s_sumlo, t + 1)
                if has(1):
                    jn, pn = later(j, p, 1)
                    pe.wait_ge(s_xhi, t + 2)
                    pe.wait_ge(s_xlo, t + 2)
                    if isinstance(t, int) and t == 0:
                        pe.wait_ge(s_whi, 1)
                        pe.wait_ge(s_wlo, 1)
                        pe.wait_ge(s_A, 4)
                    pe.wait_ge(s_v, 2 * t + 2)
                    wait(pe, s_res, t - 1)
                    project_v(jn, pn, t - 2)
                if has(0):
                    if isinstance(t, int) and t == 0:
                        pe.wait_ge(l_main, 16)
                    wait(pe, s_y, 2 * t)
                    for c in range(NC):
                        o = bank[2 + c // 2][:, (c % 2) * N:(c % 2 + 1) * N]
                        w = slice(CH + c * P, CH + (c + 1) * P)
                        mm(o, vu_hi[:, w], x_hi[:, p, :], start=True, stop=False)
                        mm(o, vu_hi[:, w], x_lo[:, p, :], start=False, stop=False)
                        final = mm(o, vu_lo[:, w], x_hi[:, p, :], start=False, stop=True)
                    final.then_inc(s_ups, 1)
                if has(-1):
                    pe.wait_ge(s_g, t)
                    if has(1):
                        pe.wait_ge(s_v, 2 * t + 4)
                    wait(pe, s_res, t - 1)
                    for h in range(2):
                        o = bank[0][:, h * D:(h + 1) * D]
                        for c in range(NC):
                            mm(o, g_sb[:, c, h, :], main("o_w")[:, c * D:(c + 1) * D], start=(c == 0), stop=False)
                        final = mm(o, ones_bf[:, :], row_parts[:, ROW_O:ROW_O + D], start=False, stop=True)
                    final.then_inc(s_ops, 1)
                if has(0):
                    if isinstance(t, int) and t == 0:
                        pe.wait_ge(l_i, 16)
                    pe.wait_ge(s_u, t + 1)
                    pe.wait_ge(s_Y, 2 * t + 1)
                    for c in range(NC):
                        for q in range(NQ):
                            final = mm(bank[2][:, c * P:(c + 1) * P], Y_r[:, q, c * P:(c + 1) * P],
                                       dft_i_sb[:, q, 0, :], start=(q == 0), stop=(q == NQ - 1))
                    final.then_inc(s_evenps, 1)
                    pe.wait_ge(s_Y, 2 * t + 2)
                    for c in range(NC):
                        for q in range(NQ):
                            final = mm(bank[3][:, c * P:(c + 1) * P], Y_i[:, q, c * P:(c + 1) * P],
                                       dft_i_sb[:, q, 1, :], start=(q == 0), stop=(q == NQ - 1))
                    final.then_inc(s_inv, 1)
                if has(-2):
                    _, pa = later(j, p, -2)
                    pe.wait_ge(s_x1, t - 1)
                    wait(pe, s_x1T, t - 2)
                    for h in range(2):
                        final = nc.tensor.transpose(bank[1][:, h * P:(h + 1) * P], x1_sb[:, pa, h, :], ident)
                    final.then_inc(s_xtps, 1)

            def scores(j, p):
                t = 2 * j + p
                pe.wait_ge(s_x1T, t + 1)
                wait(pe, d_p, 2 * (t - 1))
                for c in range(2):
                    final = mm(bank[4 + p][:, c * N:(c + 1) * N], dA[:, c * P:(c + 1) * P],
                               x1T_all[:, bass.ds(t, 1), :].rearrange("p a n -> p (a n)"), start=True, stop=True)
                final.then_inc(d_sps, 1)

            def dispatch(j, p, has):
                t = 2 * j + p
                if has(0):
                    pe.wait_ge(d_p, 2 * t + 2)
                    wait(pe, d_pT, t - 1)
                    for h in range(2):
                        for c in range(2):
                            final = nc.tensor.transpose(bank[6 + p][:, h * HS + c * P:h * HS + (c + 1) * P],
                                                        dP[:, p, c, h * P:(h + 1) * P], ident)
                    final.then_inc(d_tps, 1)
                if has(2):
                    scores(*later(j, p, 2))
                if has(-1):
                    jb, pb = later(j, p, -1)
                    pe.wait_ge(d_pT, t)
                    pe.wait_ge(l_tokens[pb], 16 * (jb + 1))
                    wait(pe, d_z, t - 2)
                    for h in range(2):
                        final = mm(bank[2 + pb][:, 0:HS], tokens_in[:, pb, h * D:(h + 1) * D], dPT[:, pb, h, :],
                                   start=(h == 0), stop=(h == 1))
                    final.then_inc(d_zps, 1)

            def between(t):
                if t == B - 1:
                    pe.wait_ge(s_prod, 4 * B)
                    scores(0, 0)
                    scores(0, 1)
                if t == B:
                    pe.wait_ge(s_y, 2 * B)
                    dispatch(0, 0, lambda k: k >= 0)
                    dispatch(0, 1, lambda k: k >= -1)

            steps(pe, step, 4, 2, 0, B + 2, between)
            steps(pe, dispatch, 4, 2, 2, B + 1)
            pe.wait_ge(d_pick, 2)
            pe.wait_ge(d_pT, B)
            for c in range(2):
                final = mm(bank[6][:, 0:B * S], const("diagmask")[:, c * D:(c + 1) * D],
                           rec_pick[:, c, :, :].rearrange("p b s -> p (b s)"), start=(c == 0), stop=(c == 1))
            final.then_inc(d_divps, 1)
            pe.wait_ge(d_p, 2 * B)
            pe.wait_ge(d_z, B)
            pe.wait_ge(s_values_w, 1)
            for k in range(EG):
                for g in range(H // EG):
                    w0 = g * EG * DH
                    final = mm(bank[4][w0:w0 + EG * DH, 0:B * S], values_w[:, k, w0:w0 + EG * DH],
                               dZ[:, g * EG + k, :, :].rearrange("p b s -> p (b s)"), start=(k == 0),
                               stop=(k == EG - 1))
            final.then_inc(d_ops, 1)

            flat = "p s b -> p (s b)"
            pe.wait_ge(d_o, 2)
            pe.wait_ge(s_res, B)
            pe.wait_ge(s_x1T, B)
            mm(bank[0][:, 0:S * B], slot("d_Wo"), dOT[:, :, :].rearrange("p b s -> p s b"), start=True,
               stop=True).then_inc(e_pe, 1)
            keep_warm(4)
            pe.wait_ge(e_chain, 1)
            mm(bank[1][:, 0:S * B], const("mean"), eo[:, :, :].rearrange(flat), start=True, stop=True).then_inc(e_pe, 1)
            keep_warm(6)
            pe.wait_ge(e_chain, 3)
            for c in range(2):
                final = mm(bank[1][:, c:c + 1], esq.rearrange(flat)[:, c * P:(c + 1) * P], const("mean")[:, 0:1],
                           start=True, stop=True)
            final.then_inc(e_pe, 1)
            keep_warm(12)
            pe.wait_ge(e_chain, 5)
            pe.wait_ge(e_zero, 1)
            mm(bank[1][:, 0:S * B], ones_f[:, :], ediag.rearrange("p c n -> p (c n)"), start=True,
               stop=True).then_inc(e_pe, 1)
            keep_warm(4)
            pe.wait_ge(e_chain, 7)
            for p in range(2):
                pe.wait_ge(l_exp[p], 16 * PAIRS)

            def up(g):
                wait(pe, e_in, 2 * (g - 1))
                for k, w0 in ((2, 0), (4, FF)):
                    for e in range(EG):
                        final = mm(bank[k + g % 2][e * ROW:(e + 1) * ROW, :], eh[:, g * EG + e, :],
                                   exp_sb[:, g * EG + e, w0:w0 + FF], start=True, stop=True)
                    final.then_inc(e_up, 1)

            def flip(g):
                pe.wait_ge(e_ug, g + 1)
                wait(pe, e_ugT, g - 1)
                for f in range(NFC):
                    final = nc.tensor.transpose(bank[6 + g % 2][:, f * P:(f + 1) * P], eug[:, g % 2, f * P:(f + 1) * P],
                                                ident)
                final.then_inc(e_tr, 1)

            def down(g):
                pe.wait_ge(e_ugT, g + 1)
                for f in range(NFC):
                    for e in range(EG):
                        w0 = 2 * FF + f * P
                        final = mm(bank[0][e * ROW:(e + 1) * ROW, g * D:(g + 1) * D],
                                   eugT[:, g % 2, f * P + e * ROW:f * P + (e + 1) * ROW],
                                   exp_sb[:, g * EG + e, w0:w0 + P], start=(f == 0), stop=(f == NFC - 1))
                final.then_inc(e_y, 1)

            for g in range(3):
                up(g)
            flip(0)
            for g in range(3, GROUPS):
                up(g)
            flip(1)
            for g in range(GROUPS):
                down(g)
                if g + 2 < GROUPS:
                    flip(g + 2)
            def queries(j, p, o):
                t = 2 * j + p
                wait(pe, c_q, t)
                mm(o[:, 0:N], slot("c_Wq"), x1T_all[:, bass.ds(t, 1), :].rearrange("p a n -> p (a n)"),
                   start=True, stop=True).then_inc(c_qps, 1)

            pe.wait_ge(e_in, 2 * GROUPS)
            queries(0, 0, bank[2])
            keep_warm(3)
            pe.wait_ge(e_chain, 8)
            for g in range(GROUPS):
                final = nc.tensor.transpose(bank[1][:, g * P:(g + 1) * P], eyr[:, g, :], ident)
            final.then_inc(e_pe, 1)
            keep_warm(3)
            pe.wait_ge(e_chain, 9)
            mm(bank[0][:, 0:S * B], slot("c_Wk"), eo2[:, :, :].rearrange("p s b -> p b s"), start=True, stop=True)
            mm(bank[0][:, S * B:2 * S * B], slot("c_Wv"), eo2[:, :, :].rearrange("p s b -> p b s"), start=True,
               stop=True).then_inc(e_pe, 1)

            keep_warm(5)
            pe.wait_ge(e_chain, 11)

            def combine(j, p, has):
                t = 2 * j + p
                if has(0):
                    pe.wait_ge(c_q, t + 1)
                    pe.wait_ge(c_kb, t + 1)
                    wait(pe, c_sub, t - 1)
                    for h in range(2):
                        final = mm(bank[2 + p][:, h * HS:(h + 1) * HS], cqT[:, p, h * P:(h + 1) * P],
                                   kb[:, p, :, :].rearrange("p h s -> p (h s)"), start=True, stop=True)
                    final.then_inc(c_sps, 1)
                if has(1):
                    queries(*later(j, p, 1), bank[0])
                if has(-3):
                    _, pc = later(j, p, -3)
                    pe.wait_ge(c_pT, t - 2)
                    pe.wait_ge(c_vo, t - 2)
                    wait(pe, c_res, t - 4)
                    for h in range(2):
                        o = bank[6 + pc][:, h * D:(h + 1) * D]
                        for c in range(2):
                            mm(o, cPT[:, pc, c, h * P:(h + 1) * P], vo[:, pc, c, :], start=(c == 0), stop=False)
                        final = mm(o, ones_bf[:, :], row_parts[:, ROW_C:ROW_C + D], start=False, stop=True)
                    final.then_inc(c_ops, 1)
                if has(-2):
                    pe.wait_ge(c_p, t - 1)
                    wait(pe, c_pT, t - 3)
                    for c in range(2):
                        for h in range(2):
                            final = nc.tensor.transpose(bank[4 + p][:, c * N + h * P:c * N + (h + 1) * P],
                                                        cp[:, p, h, c * P:(c + 1) * P], ident)
                    final.then_inc(c_tps, 1)
                    pe.wait_ge(c_vb, t - 1)
                    wait(pe, c_vo, t - 2)
                    for c in range(2):
                        final = mm(bank[1][:, c * D:(c + 1) * D],
                                   vb[:, p, :, :].rearrange("p h s -> p (h s)")[:, c * P:(c + 1) * P],
                                   slot("c_Wo"), start=True, stop=True)
                    final.then_inc(c_vops, 1)

            steps(pe, combine, 6, 2, 0, B + 3)

        @block.scalar
        def _(act):
            def v_of(j, p):
                t = 2 * j + p
                for h in range(2):
                    act.wait_ge(s_vps, 2 * t + h + 1)
                    if h == 0:
                        wait(act, s_sum, t)
                        wait(act, s_diff, t)
                    nc.scalar.activation(v_sb[:, h, :], bank[h][:, 0:CH], ACT.Silu).then_inc(s_v, 1)

            def leading(j, p):
                act.wait_ge(l_xT[p], 16 * (j + 1))
                nc.scalar.activation(x_hi[:, p, :], xT_sb[:, p, :], ACT.Copy).then_inc(s_xhi, 1)

            act.wait_ge(l_vw, 16)
            nc.scalar.activation(vu_hi[:, :], vu_sb, ACT.Copy).then_inc(s_whi, 1)
            leading(0, 0)
            leading(0, 1)
            v_of(0, 0)

            def leading_difference(j, p):
                t = 2 * j + p
                act.wait_ge(s_diff, t + 1)
                wait(act, s_fwd, 2 * t)
                nc.scalar.activation(vd_hi[:, :], vd_sb[:, p, :], ACT.Copy).then_inc(s_dhi, 1)

            def leading_sum(j, p):
                t = 2 * j + p
                act.wait_ge(s_sum, t + 1)
                wait(act, s_fwd, 2 * t)
                nc.scalar.activation(vs_hi[:, :], vs_sb[:, p, :], ACT.Copy).then_inc(s_sumhi, 1)

            act.wait_ge(l_f, 16)
            nc.scalar.activation(dft_hi[:, :, :], dft_f_sb, ACT.Copy).then_inc(s_dft_hi, 1)
            leading_difference(0, 0)

            def step(j, p, has):
                t = 2 * j + p
                if has(-1):
                    act.wait_ge(s_evenps, t)
                    wait(act, s_y, 2 * t - 2)
                    nc.scalar.activation(even_sb[:, :, :].rearrange("p c n -> p (c n)"), bank[2][:, 0:CH],
                                         ACT.Copy).then_inc(s_even, 1)
                if has(0):
                    leading_sum(j, p)
                if has(-3):
                    ja, pa = later(j, p, -3)
                    act.wait_ge(s_xtps, t - 2)
                    nc.scalar.activation(x1T_all[:, bass.ds(2 * ja + pa, 1), :].rearrange("p a n -> p (a n)"),
                                         bank[1][:, 0:N], ACT.Copy).then_inc(s_x1T, 1)
                if has(1):
                    v_of(*later(j, p, 1))
                if has(0):
                    act.wait_ge(s_ups, t + 1)
                    wait(act, s_g, t - 1)
                    for c in range(NC):
                        final = nc.scalar.activation(u_sb[:, p, c, :],
                                                     bank[2 + c // 2][:, (c % 2) * N:(c % 2 + 1) * N],
                                                     ACT.Silu, bias=main("u_b")[:, c:c + 1])
                    final.then_inc(s_u, 1)
                if has(1):
                    leading_difference(*later(j, p, 1))
                if has(2):
                    leading(*later(j, p, 2))

            def weights(j, p):
                t = 2 * j + p
                act.wait_ge(d_nb, t + 1)
                wait(act, d_tps, t - 1)
                wait(act, d_rec, t - 1)
                for c in range(2):
                    nc.scalar.activation(dP[:, p, c, :], bank[4 + p][:, c * N:(c + 1) * N], ACT.Exp,
                                         bias=dnb[:, p, c:c + 1], scale=SCALE,
                                         accum_out=dsum[:, p, c:c + 1]).then_inc(d_p, 1)

            def dispatch(j, p, has):
                t = 2 * j + p
                if has(1):
                    weights(*later(j, p, 1))
                if has(0):
                    act.wait_ge(d_tps, t + 1)
                    wait(act, d_zps, t - 1)
                    nc.scalar.activation(dPT[:, p, :, :].rearrange("p h s -> p (h s)"), bank[6 + p][:, :],
                                         ACT.Copy).then_inc(d_pT, 1)

            def between(t):
                if t == B - 1:
                    act.wait_ge(s_half, 2)
                    nc.scalar.activation(early[:, :], minus_half[:, 0:1], ACT.Exp)
                if t == B:
                    weights(0, 0)
                    dispatch(0, 0, lambda k: k >= 0)
                    dispatch(0, 1, lambda k: k >= -1)

            steps(act, step, 4, 2, 0, B + 3, between)
            steps(act, dispatch, 4, 2, 2, B)

            def silus(g):
                for k, buf in ((0, eu_in), (1, eg_in)):
                    act.wait_ge(e_in, 2 * g + k + 1)
                    nc.scalar.activation(buf[:, g % 2, :], buf[:, g % 2, :], ACT.Silu).then_inc(e_act, 1)

            for g in range(GROUPS + 1):
                if g < GROUPS:
                    silus(g)
                if g >= 1:
                    act.wait_ge(e_tr, g)
                    wait(act, e_y, g - 2)
                    nc.scalar.activation(eugT[:, (g - 1) % 2, :], bank[6 + (g - 1) % 2][:, :],
                                         ACT.Copy).then_inc(e_ugT, 1)

            nc.scalar.activation(early[:, :], minus_half[:, 0:1], ACT.Exp)

            def q_out(j, p, q):
                t = 2 * j + p
                act.wait_ge(c_qps, t + 1)
                wait(act, c_sps, t - 1)
                nc.scalar.activation(cqT[:, p, :], q[:, 0:N], ACT.Identity, bias=slot("c_bq")).then_inc(c_q, 1)

            q_out(0, 0, bank[2])

            def combine(j, p, has):
                t = 2 * j + p
                if has(1):
                    q_out(*later(j, p, 1), bank[0])
                if has(-2):
                    act.wait_ge(c_tps, t - 1)
                    wait(act, c_ops, t - 3)
                    nc.scalar.activation(cPT[:, p, :, :].rearrange("p c n -> p (c n)"), bank[4 + p][:, :],
                                         ACT.Copy).then_inc(c_pT, 1)
                    act.wait_ge(c_vops, t - 1)
                    nc.scalar.activation(vo[:, p, :, :].rearrange("p c d -> p (c d)"), bank[1][:, 0:2 * D],
                                         ACT.Copy).then_inc(c_vo, 1)
                if has(0):
                    act.wait_ge(c_sub, t + 1)
                    wait(act, c_p, t - 1)
                    nc.scalar.activation(ce[:, p, :, :].rearrange("p h s -> p (h s)"),
                                         cs[:, p, :, :].rearrange("p h s -> p (h s)"), ACT.Exp,
                                         scale=SCALE).then_inc(c_exp, 1)
                if has(-4):
                    act.wait_ge(c_nb, t - 3)
                    wait(act, st_out[p], 16 * (j - 2))
                    for h in range(2):
                        final = nc.scalar.activation(y_out[:, p, h, :], cres[:, p, h, :], ACT.Identity,
                                                     bias=cnb[:, p, h:h + 1], scale=crstd[:, p, h:h + 1])
                    final.then_inc(c_y, 1)

            steps(act, combine, 6, 2, 0, B + 4)

        @block.gpsimd
        def _(pool):
            tt = nc.gpsimd.tensor_tensor
            nc.gpsimd.memset(ones_bf[:, :], 1.0).then_inc(s_ones, 1)
            nc.gpsimd.memset(plus_half[:, :], 0.5).then_inc(s_half, 1)
            nc.gpsimd.memset(minus_half[:, :], -0.5).then_inc(s_half, 1)
            nc.gpsimd.memset(ones_f[:, :], 1.0).then_inc(e_zero, 1)
            nc.gpsimd.memset(values_w[:, :, :], 0.0).then_inc(d_zero, 1)
            pool.wait_ge(s_half, 2)
            for layer in range(4):
                pool.wait_ge(s_pms, layer + 1)
                tt(pss2[:, :], pss[:, :], plus_half[:, :], ALU.pow).then_inc(s_prms, 1)

            pool.wait_ge(s_whi, 1)
            tt(vu_lo[:, :], vu_sb, vu_hi[:, :], ALU.subtract).then_inc(s_wlo, 1)

            def sums(j, p):
                t = 2 * j + p
                pool.wait_ge(s_v, 2 * t + 2)
                tt(vs_sb[:, p, :], v_sb[:, 0, :], v_sb[:, 1, :], ALU.add).then_inc(s_sum, 1)

            sums(0, 0)

            def step(j, p, has):
                t = 2 * j + p
                if has(0):
                    pool.wait_ge(s_sumhi, t + 1)
                    wait(pool, s_fwd, 2 * t)
                    tt(vs_lo[:, :], vs_sb[:, p, :], vs_hi[:, :], ALU.subtract).then_inc(s_sumlo, 1)
                if has(-1):
                    _, pb = later(j, p, -1)
                    pool.wait_ge(s_y, 2 * t)
                    pool.wait_ge(s_u, t)
                    wait(pool, s_ops, t - 1)
                    tt(g_sb[:, :, :, :].rearrange("p c h n -> p c (h n)"),
                       y_sb[:, :, :, :].rearrange("p c h n -> p c (h n)"), u_sb[:, pb, :, :],
                       ALU.mult).then_inc(s_g, 1)
                if has(0):
                    wait(pool, s_inv, t)
                    pool.wait_ge(s_prod, 4 * t + 2)
                    tt(Y_r[:, :, :], rr[:, :, :], ii[:, :, :], ALU.subtract).then_inc(s_Y, 1)
                    pool.wait_ge(s_prod, 4 * t + 4)
                    tt(Y_i[:, :, :], ri[:, :, :], ir[:, :, :], ALU.add).then_inc(s_Y, 1)
                if has(1):
                    sums(*later(j, p, 1))
                if has(-1):
                    pool.wait_ge(s_ve, t)
                    tt(rstd_sb[:, :], ve_sb[:, :], minus_half[:, :], ALU.pow).then_inc(s_rstd, 1)

            steps(pool, step, 4, 2, 0, B + 1)

            pool.wait_ge(s_prod, 4 * B)
            nc.gpsimd.memset(eh, 0.0).then_inc(e_zero, 1)

            pool.wait_ge(e_ve, 1)
            tt(erstd[:, :], eve[:, :], minus_half[:, :], ALU.pow).then_inc(e_rstd, 1)
            mask = const("headmask").rearrange("p (h s) -> p h s", h=H)
            pool.wait_ge(e_chain, 10)

            def keys(j, p):
                t = 2 * j + p
                wait(pool, c_sps, t - 1)
                tt(kb[:, p, :, :], ckT[:, bass.ds(t, 1), :].to_broadcast([P, H, S]), mask, ALU.mult).then_inc(c_kb, 1)

            keys(0, 0)
            pool.wait_ge(e_chain, 11)

            def combine(j, p, has):
                t = 2 * j + p
                if has(1):
                    keys(*later(j, p, 1))
                if has(-1):
                    jb, pb = later(j, p, -1)
                    wait(pool, c_vops, t - 2)
                    tt(vb[:, pb, :, :], cvT[:, bass.ds(2 * jb + pb, 1), :].to_broadcast([P, H, S]), mask,
                       ALU.mult).then_inc(c_vb, 1)
                    pool.wait_ge(c_rec, t)
                    wait(pool, c_tps, t - 2)
                    tt(cp[:, pb, :, :].rearrange("p h (g s) -> p (h g) s", s=S), ce[:, pb, :, :],
                       crec[:, pb, :].unsqueeze(2).to_broadcast([P, 2 * H, S]), ALU.mult).then_inc(c_p, 1)
                if has(-3):
                    _, pc = later(j, p, -3)
                    pool.wait_ge(c_ve, t - 2)
                    wait(pool, c_y, t - 4)
                    tt(crstd[:, pc, :], cve[:, pc, :], minus_half[:, :], ALU.pow).then_inc(c_rstd, 1)

            steps(pool, combine, 6, 2, 0, B + 3)

        @block.vector
        def _(dve):
            tt = nc.vector.tensor_tensor
            ts = nc.vector.tensor_scalar
            stt = nc.vector.scalar_tensor_tensor
            copy = nc.vector.tensor_copy

            chain = [0]

            def link(ins):
                chain[0] += 1
                ins.then_inc(s_pchain, 1)
                dve.wait_ge(s_pchain, chain[0])

            def split_rows():
                whole = pos("rows")
                link(copy(row_split[:, 0, :], whole))
                link(tt(row_res[:, 0, :], whole, row_split[:, 0, :], ALU.subtract))
                link(copy(row_split[:, 1, :], row_res[:, 0, :]))
                link(tt(row_res[:, 1, :], row_res[:, 0, :], row_split[:, 1, :], ALU.subtract))
                copy(row_split[:, 2, :], row_res[:, 1, :]).then_inc(s_rows, 1)

            def trailing(j, p):
                dve.wait_ge(s_xhi, 2 * j + p + 1)
                tt(x_lo[:, p, :], xT_sb[:, p, :], x_hi[:, p, :], ALU.subtract).then_inc(s_xlo, 1)

            def difference(j, p):
                t = 2 * j + p
                dve.wait_ge(s_v, 2 * t + 2)
                wait(dve, s_fwd, 2 * (t - 1))
                tt(vd_sb[:, p, :], v_sb[:, 0, :], v_sb[:, 1, :], ALU.subtract).then_inc(s_diff, 1)

            def trailing_difference(j, p):
                dve.wait_ge(s_dhi, 2 * j + p + 1)
                tt(vd_lo[:, :], vd_sb[:, p, :], vd_hi[:, :], ALU.subtract).then_inc(s_dlo, 1)

            nc.vector.memset(row_parts[:, :], 0.0).then_inc(s_zero, 1)
            dve.wait_ge(l_pos, 16)
            for c in range(2):
                first = stt(ph[:, c, :], pos("pos_w"), pos("index")[:, c:c + 1], pos("pos_b"), ALU.mult, ALU.add)
            link(first)
            for layer in range(4):
                wait(dve, s_ptr, 2 * layer)
                ts(pact[:, :, :], ph[:, :, :], 0.0, None, ALU.max).then_inc(s_pact, 1)
                link(tt(psq[:, :, :], ph[:, :, :], ph[:, :, :], ALU.mult))
                nc.vector.tensor_reduce(pss[:, :], psq[:, :, :], AX.X, ALU.add).then_inc(s_pms, 1)
                wait(dve, s_plin, 2 * layer)
                dve.wait_ge(s_ptr, 2 * layer + 2)
                copy(pactT[:, :, :].rearrange("p c n -> p (c n)"), bank[7][0:R, 0:2 * P]).then_inc(s_pactT, 1)
                dve.wait_ge(s_prms, layer + 1)
                link(ts(prms[:, :], pss2[:, :], R ** -0.5, RMS_EPS, ALU.mult, ALU.add))
                link(nc.vector.reciprocal(prec[:, :], prms[:, :]))
                if layer == 0:
                    split_rows()
                if layer == 1:
                    for c in range(2):
                        ts(pbd[:, c, :], pos("out_b"), pos("decay")[:, c:c + 1], None, ALU.mult)
                if layer == 3:
                    link(tt(prd[:, :], prec[:, :], pos("decay"), ALU.mult))
                for c in range(2):
                    dve.wait_ge(s_plin, 2 * layer + c + 1)
                    if layer < 3:
                        last = stt(ph[:, c, :], bank[5 + c][:, 0:R], prec[:, c:c + 1],
                                   pos("lin_b")[:, layer * R:(layer + 1) * R], ALU.mult, ALU.add)
                        if c == 1:
                            link(last)
                    else:
                        stt(coef[:, c, :], bank[5 + c][:, 0:CH], prd[:, c:c + 1], pbd[:, c, :], ALU.mult,
                            ALU.add).then_inc(s_coef, 1)
            dve.wait_ge(s_dq, 1)
            link(ts(dqT[:, :], bank[4][:, 0:S], slot("d_bq"), None, ALU.add))
            tt(dq_blocks[:, :, :], dqT[:, :].unsqueeze(1).to_broadcast([P, H, S]),
               const("headmask").rearrange("p (h s) -> p h s", h=H), ALU.mult).then_inc(s_dqb, 1)
            trailing(0, 0)
            trailing(0, 1)
            dve.wait_ge(s_dft_hi, 1)
            tt(dft_lo[:, :, :], dft_f_sb, dft_hi[:, :, :], ALU.subtract).then_inc(s_dft_lo, 1)
            difference(0, 0)
            trailing_difference(0, 0)
            for part in range(2):
                for q in range(NQ):
                    dve.wait_ge(s_Aps, 2 * part + q + 1)
                    copy((A_r, A_i)[part][:, q, :], bank[2 * part + q][:, 0:CH]).then_inc(s_A, 1)
                    if part == 0 and q == 0:
                        dve.wait_ge(s_dA, 1)
                        copy(dA[:, :], bank[4][:, 0:HS])
                        copy(dc[:, :], bank[4][:, HS:HS + 2]).then_inc(s_prep, 1)
                        dve.wait_ge(s_prep, 1)
                        ts(dcs[:, :], dc[:, :], SCALE, None, ALU.mult)
                        ts(slot_b[:, :], slot("slotT"), slot("d_bo"), None, ALU.add)
                        dve.wait_ge(d_zero, 1)
                        for k in range(EG):
                            heads = lambda w: w.rearrange("p (g k e) -> p g k e", g=H // EG, k=EG)[:, :, k, :]
                            last = copy(heads(values_w[:, k, :]), heads(slot("d_Wv")))
                        last.then_inc(s_values_w, 1)
            dve.wait_ge(s_A, 4)

            def moments(src, n, s_src, s_stats):
                dve.wait_ge(s_src, n + 1)
                for h in range(2):
                    last = nc.vector.bn_stats(st_sb[:, h, :], src[:, h, :])
                last.then_inc(s_stats, 1)

            def variance(mv, ve, n, s_stats, s_mean, s_eps):
                dve.wait_ge(s_stats, n + 1)
                dve.sem_inc(s_seen, 1)
                for h in range(2):
                    last = nc.vector.bn_aggr(mv[:, h, :], st_sb[:, h, :])
                last.then_inc(s_mean, 1)
                dve.wait_ge(s_mean, n + 1)
                ts(ve, mv[:, :, 1], LN_EPS, None, ALU.add).then_inc(s_eps, 1)

            def normalise(src, dst, n, s_inverse, s_dst):
                dve.wait_ge(s_inverse, n + 1)
                for h in range(2):
                    last = ts(dst[:, h, :], src[:, h, :], mv_sb[:, h, 0:1], rstd_sb[:, h:h + 1], ALU.subtract,
                              ALU.mult)
                last.then_inc(s_dst, 1)

            def unfold(t):
                dve.wait_ge(s_even, t)
                dve.wait_ge(s_inv, t)
                wait(dve, s_g, t - 1)
                odd = bank[3][:, 0:CH].rearrange("p (c n) -> p c n", c=NC)
                tt(y_sb[:, :, 0, :], even_sb[:, :, :], odd, ALU.add).then_inc(s_y, 1)
                tt(y_sb[:, :, 1, :], even_sb[:, :, :], odd, ALU.subtract).then_inc(s_y, 1)

            def bias(j, p):
                t = 2 * j + p
                dve.wait_ge(d_sps, t + 1)
                wait(dve, d_p, 2 * (t - 1))
                nc.vector.tensor_reduce(dmax[:, p, :], bank[4 + p][:, :].rearrange("p (c n) -> p c n", c=2), AX.X,
                                        ALU.max).then_inc(d_max, 1)
                dve.wait_ge(d_max, t + 1)
                tt(dmc[:, p, :], dmax[:, p, :], dc[:, :], ALU.add).then_inc(d_mc, 1)
                dve.wait_ge(d_mc, t + 1)
                stt(dnb[:, p, :], dmc[:, p, :], -SCALE, dcs[:, :], ALU.mult, ALU.add).then_inc(d_nb, 1)

            def dispatch(j, p, has):
                t = 2 * j + p
                if has(0):
                    dve.wait_ge(d_p, 2 * t + 2)
                    nc.vector.reciprocal(drec[:, :, bass.ds(t, 1)].rearrange("p c a -> p (c a)"),
                                         dsum[:, p, :]).then_inc(d_rec, 1)
                if has(2):
                    bias(*later(j, p, 2))
                if has(-1):
                    jb, pb = later(j, p, -1)
                    dve.wait_ge(d_zps, t)
                    copy(dZ[:, :, bass.ds(2 * jb + pb, 1), :].rearrange("p h a s -> p (h a) s"),
                         bank[2 + pb][:, 0:HS].rearrange("p (h s) -> p h s", s=S)).then_inc(d_z, 1)

            def step(j, p, has):
                t = 2 * j + p
                if has(-1):
                    unfold(t)
                if has(0):
                    wait(dve, s_Y, 2 * t)
                    if isinstance(t, int) and t == 0:
                        dve.wait_ge(s_wlo, 1)
                    for n, (o, b, a) in enumerate(((ii, 6, A_i), (rr, 4, A_r), (ri, 6, A_r), (ir, 4, A_i))):
                        dve.wait_ge(s_fwd, 2 * t + 1 + n % 2)
                        for q in range(NQ):
                            last = tt(o[:, q, :], bank[b + q][:, 0:CH], a[:, q, :], ALU.mult)
                        last.then_inc(s_prod, 1)
                if has(-2):
                    ja, pa = later(j, p, -2)
                    wait(dve, st_x1[pa], 16 * ja)
                    wait(dve, s_xtps, t - 3)
                    normalise(res_sb, x1_sb[:, pa, :, :], t - 2, s_rstd, s_x1)
                if has(1):
                    difference(*later(j, p, 1))
                elif isinstance(t, int) and t == B:
                    bias(0, 0)
                    bias(0, 1)
                if has(-1):
                    jb, pb = later(j, p, -1)
                    dve.wait_ge(l_x[pb], 16 * (jb + 1))
                    wait(dve, s_x1, t - 1)
                    dve.wait_ge(s_ops, t)
                    tt(res_sb[:, :, :].rearrange("p h d -> p (h d)"), bank[0][:, 0:2 * D],
                       x_sb[:, pb, :], ALU.add).then_inc(s_res, 1)
                    moments(res_sb, t - 1, s_res, s_bn)
                if has(1):
                    trailing_difference(*later(j, p, 1))
                if has(-1):
                    variance(mv_sb, ve_sb[:, :], t - 1, s_bn, s_mv, s_ve)
                if has(2):
                    trailing(*later(j, p, 2))

            def between(t):
                if t == B:
                    dispatch(0, 0, lambda k: k >= 0)
                    dispatch(0, 1, lambda k: k >= -1)

            steps(dve, step, 4, 2, 0, B + 2, between)
            def between(t):
                if t == B - 1:
                    dve.wait_ge(d_rec, B)
                    for c in range(2):
                        tt(rec_pick[:, c, :, :], drec[:, c, :].unsqueeze(2).to_broadcast([P, B, S]),
                           const("pick").unsqueeze(1).to_broadcast([P, B, S]), ALU.mult).then_inc(d_pick, 1)

            steps(dve, dispatch, 4, 2, 2, B + 1, between)
            dve.wait_ge(d_divps, 1)
            copy(drecT, bank[6][:, 0:B * S]).then_inc(d_div, 1)
            dve.wait_ge(d_div, 1)
            dve.wait_ge(d_ops, 1)
            flat_o = dOT[:, :, :].rearrange("p b s -> p (b s)")
            tt(flat_o, bank[4][:, 0:B * S], drecT, ALU.mult).then_inc(d_o, 1)
            dve.wait_ge(d_o, 1)
            ts(flat_o, flat_o, slot("d_bv"), None, ALU.add).then_inc(d_o, 1)

            def bcast(ap):
                return ap.unsqueeze(2).to_broadcast([P, ap.shape[1], B])

            en = [0]

            def elink(ins):
                en[0] += 1
                ins.then_inc(e_chain, 1)
                dve.wait_ge(e_chain, en[0])

            def grid(ap):
                return ap.rearrange("p (s b) -> p s b", b=B)

            dve.wait_ge(e_pe, 1)
            elink(tt(eo[:, :, :], grid(bank[0][:, 0:S * B]), bcast(slot_b[:, :]), ALU.add))
            tt(ey[:, :, :], eo[:, :, :], bcast(slot("b2T")), ALU.add)
            dve.wait_ge(e_pe, 2)
            elink(tt(ecen[:, :, :], eo[:, :, :], grid(bank[1][:, 0:S * B]), ALU.subtract))
            elink(tt(esq[:, :, :], ecen[:, :, :], ecen[:, :, :], ALU.mult))
            dve.wait_ge(e_pe, 3)
            ts(eve[:, :], bank[1][:, 0:2], LN_EPS, None, ALU.add).then_inc(e_ve, 1)
            elink(tt(eh2[:, :, :], ecen[:, :, :], bcast(slot("ln_gT")), ALU.mult))
            dve.wait_ge(e_rstd, 1)
            elink(tt(ediag[:, :, :], ident.unsqueeze(1).to_broadcast([P, 2, P]),
                     erstd[:, :].unsqueeze(2).to_broadcast([P, 2, P]), ALU.mult))
            dve.wait_ge(e_pe, 4)
            elink(tt(eh1[:, :, :], eh2[:, :, :], grid(bank[1][:, 0:S * B]), ALU.mult))
            dve.wait_ge(e_zero, 2)
            elink(tt(eh[:, :, 0:B], eh1[:, :, :], bcast(slot("ln_bT")), ALU.add))

            def biased(g):
                for k, buf, bias in ((2, eu_in, eb1), (4, eg_in, ebg)):
                    dve.wait_ge(e_up, 2 * g + k // 2)
                    wait(dve, e_ug, g - 1)
                    tt(buf[:, g % 2, :], bank[k + g % 2][:, :], bias[:, g, :], ALU.add).then_inc(e_in, 1)

            def products(g):
                dve.wait_ge(e_act, 2 * g + 2)
                wait(dve, e_tr, g - 1)
                tt(eug[:, g % 2, :], eu_in[:, g % 2, :], eg_in[:, g % 2, :], ALU.mult).then_inc(e_ug, 1)

            for k in range(2):
                dve.wait_ge(l_bias[k], 16 * GROUPS)
            for g in range(GROUPS + 1):
                if g < GROUPS:
                    biased(g)
                if g >= 1:
                    products(g - 1)
            dve.wait_ge(e_y, GROUPS)
            elink(copy(eyr.rearrange("p g d -> p (g d)"), bank[0][:, :]))
            dve.wait_ge(e_pe, 5)
            rows_of = bank[1][:, :].rearrange("p (s r) -> p s r", r=ROW)[:, :, 0:B]
            elink(tt(eo2[:, :, :], ey[:, :, :], rows_of, ALU.add))
            dve.wait_ge(e_pe, 6)
            elink(ts(ckT[:, :, :].rearrange("p b s -> p (b s)"), bank[0][:, 0:S * B], slot("c_bk"), None, ALU.add))
            elink(ts(cvT[:, :, :].rearrange("p b s -> p (b s)"), bank[0][:, S * B:2 * S * B], slot("c_bv"), None,
                     ALU.add))

            def combine(j, p, has):
                t = 2 * j + p
                scores = bank[2 + p][:, :].rearrange("p (h s) -> p h s", s=S)
                if has(0):
                    dve.wait_ge(c_sps, t + 1)
                    nc.vector.tensor_reduce(cmax[:, p, :], scores, AX.X, ALU.max).then_inc(c_max, 1)
                if has(-1):
                    _, pb = later(j, p, -1)
                    dve.wait_ge(c_exp, t)
                    wait(dve, c_p, t - 2)
                    nc.vector.tensor_reduce(csum[:, pb, :], ce[:, pb, :, :], AX.X, ALU.add).then_inc(c_sum, 1)
                if has(0):
                    dve.wait_ge(c_max, t + 1)
                    wait(dve, c_exp, t - 1)
                    tt(cs[:, p, :, :], scores, cmax[:, p, :].unsqueeze(2).to_broadcast([P, 2 * H, S]),
                       ALU.subtract).then_inc(c_sub, 1)
                if has(-3):
                    jc, pc = later(j, p, -3)
                    dve.wait_ge(c_ops, t - 2)
                    dve.wait_ge(l_x1[pc], 16 * (jc + 1))
                    wait(dve, c_y, t - 4)
                    tt(cres[:, pc, :, :].rearrange("p h d -> p (h d)"), bank[6 + pc][:, 0:2 * D],
                       x1_in[:, pc, :], ALU.add).then_inc(c_res, 1)
                if has(-4):
                    dve.wait_ge(c_rstd, t - 3)
                    stt(cnb[:, p, :], cmv[:, p, :, 0], -1.0, crstd[:, p, :], ALU.mult, ALU.mult).then_inc(c_nb, 1)
                if has(-3):
                    moments(cres[:, pc, :, :], t - 3, c_res, c_bn)
                if has(-1):
                    dve.wait_ge(c_sum, t)
                    nc.vector.reciprocal(crec[:, pb, :], csum[:, pb, :]).then_inc(c_rec, 1)
                if has(-3):
                    variance(cmv[:, pc, :, :], cve[:, pc, :], t - 3, c_bn, c_mv, c_ve)

            steps(dve, combine, 6, 2, 0, B + 4)

def constants():
    theta = np.pi * (2 * np.arange(NF) + 1) / (2 * NF)
    centre = np.arange(P) - (N - 1) / 2
    t = np.arange(N)
    dft_f = np.stack([np.cos(np.outer(centre, theta)), -np.sin(np.outer(centre, theta))], 1)
    dft_t = np.stack([np.cos(np.outer(t, theta)), -np.sin(np.outer(t, theta))], 1).reshape(2, P, 2, NF)
    dft_i = np.stack([np.cos(np.outer(theta, centre)), -np.sin(np.outer(theta, centre))], 1) / NF
    row = np.arange(P)
    of_head = (row[:, None] // DH == np.arange(H)[None, :])
    headmask = np.repeat(of_head[:, :, None], S, 2).reshape(P, HS)
    diag = np.stack([(c * (P // S) + row[:, None] // S) == (np.arange(D)[None, :] // DH) for c in range(2)], 1)
    pick = (row[:, None] % S) == np.arange(S)[None, :]
    const = np.concatenate([np.eye(P), np.full((P, P), 1.0 / D), headmask, diag.reshape(P, 2 * D), pick], 1)
    decay = np.float32(0.99) ** t.astype(np.float32)
    f = lambda a: np.ascontiguousarray(a, dtype=np.float32)
    return dict(dft_f=f(dft_f), dft_t=f(dft_t.transpose(1, 0, 2, 3)),
                dft_i=f(dft_i.reshape(NQ, P, 2, P).transpose(1, 0, 2, 3)), const=f(const),
                index=f(t.reshape(2, P).T), decay=f(decay.reshape(2, P).T))

def kernel(**inputs):
    import concourse.bacc as bacc
    from concourse.bass_utils import run_bass_kernel_spmd

    a = {k.removeprefix("L0_"): np.asarray(v) for k, v in inputs.items()}
    cat = lambda *parts: np.ascontiguousarray(np.concatenate(parts, 1))
    col = lambda v: v.reshape(-1, P).T
    c = constants()
    x = np.stack([a["attn_x"][:, :P], a["attn_x"][:, P:][:, ::-1]], 1)
    arrays = {
        "xT": x.transpose(0, 3, 1, 2).reshape(B, D, N),
        "x": x.transpose(0, 2, 1, 3).reshape(B, P, N),
        "w_vu": cat(a["attn_v_w"], a["attn_u_w"]),
        "w_main": cat(a["attn_o_w"].reshape(NC, P, D).transpose(1, 0, 2).reshape(P, NC * D),
                      col(a["attn_u_b"])),
        "w_slot": cat(a["ffn_d_Wq"], a["ffn_d_Wk"].T, a["ffn_d_Wv"], a["ffn_d_Wo"], a["ffn_c_Wq"], a["ffn_c_Wk"],
                      a["ffn_c_Wv"], a["ffn_c_Wo"], a["ffn_slot_query"][0].T, col(a["ffn_d_bq"]), col(a["ffn_d_bk"]),
                      col(a["ffn_d_bv"]), col(a["ffn_d_bo"]), col(a["ffn_c_bq"]), col(a["ffn_c_bk"]),
                      col(a["ffn_c_bv"]), a["ffn_e_ln_g"].T, a["ffn_e_ln_b"].T, a["ffn_e_b2"].T),
        "w_const": c["const"],
        "w_pos": cat(np.broadcast_to(a["attn_pos_w"], (P, R)), np.broadcast_to(a["attn_pos_b"][None], (P, R)),
                     c["index"], c["decay"],
                     *(np.broadcast_to(a["attn_" + k][None], (P, a["attn_" + k].size))
                       for k in ("lb0", "lb1", "lb2", "out_b")),
                     np.concatenate([a["attn_v_b"], a["attn_o_b"], a["ffn_c_bo"]]).reshape(P, ROWS // P)),
        "w_lin": cat(a["attn_lw0"], a["attn_lw1"], a["attn_lw2"], a["attn_out_w"]),
        "dft_t": c["dft_t"], "dft_f": c["dft_f"], "dft_i": c["dft_i"],
        "experts": np.concatenate([a["ffn_e_W1"], a["ffn_e_Wg"],
                                   a["ffn_e_W2"].reshape(H, NFC, P, D).transpose(0, 2, 1, 3).reshape(H, P, FF)], 2),
        "bias_1": np.broadcast_to(a["ffn_e_b1"].reshape(GROUPS, EG, 1, FF).transpose(1, 2, 0, 3),
                                  (EG, ROW, GROUPS, FF)).reshape(P, GROUPS, FF),
        "bias_g": np.broadcast_to(a["ffn_e_bg"].reshape(GROUPS, EG, 1, FF).transpose(1, 2, 0, 3),
                                  (EG, ROW, GROUPS, FF)).reshape(P, GROUPS, FF),
    }
    arrays = {k: np.ascontiguousarray(v) for k, v in arrays.items()}
    nc = bacc.Bacc("TRN2", target_bir_lowering=False, num_devices=1)
    args = [nc.dram_tensor(k, v.shape, F32, kind="ExternalInput").ap() for k, v in arrays.items()]
    args.append(nc.dram_tensor("out", (B, P, N), F32, kind="ExternalOutput").ap())
    build(nc, *args)
    r = run_bass_kernel_spmd(nc, [arrays], core_ids=[0]).results[0]["out"]
    y = r.reshape(B, P, 2, D).transpose(0, 2, 1, 3)
    return np.ascontiguousarray(np.concatenate([y[:, 0], y[:, 1, ::-1]], 1))
```
